# Optimizing a Trainium2 kernel written in Bass

```python
import numpy as np
import jax
import jax.numpy as jnp

def _softmax(x, axis=-1):
    return jax.nn.softmax(x, axis=axis)

def _gelu(x):
    return jax.nn.gelu(x, approximate=True)

def _silu(x):
    return jax.nn.silu(x)

def _sigmoid(x):
    return jax.nn.sigmoid(x)

def _layernorm(x, axis=-1, eps=1e-05):
    m = jnp.mean(x, axis=axis, keepdims=True)
    v = jnp.var(x, axis=axis, keepdims=True)
    return (x - m) / jnp.sqrt(v + eps)

def _scatter_add(tgt, idx, src, axis=0):
    return tgt.at[idx].add(src)

def _segment_sum(src, seg, n):
    return jax.ops.segment_sum(src, seg, n)
kernel_name = 'mk_decoder_preln_d2_seqx_r8_5b64c0'

def setup_inputs(seed: int=0):
    np.random.seed(seed)
    _w = jnp.asarray

    def _rec_inputs():
        import jax
        import jax.numpy as jnp
        _rk = jax.random.key(seed)
        x = -0.0002928 + 1 * jax.random.normal(jax.random.fold_in(_rk, 1), (16, 56, 128), jnp.float32)
        _lenS = 56 - jax.random.randint(jax.random.fold_in(_rk, 7), (16,), 0, max(1, 56 // 4) + 1, jnp.int32)
        _lenS2 = 1500 - jax.random.randint(jax.random.fold_in(_rk, 8), (16,), 0, max(1, 1500 // 4) + 1, jnp.int32)
        _ctx_1024P = jax.random.normal(jax.random.fold_in(_rk, 11), (16, 16, 128), jnp.float32)
        _ctx_1024c = jax.random.dirichlet(jax.random.fold_in(_rk, 511), 0.3 * jnp.ones((16,), jnp.float32), (16, 1500))
        _ctx_1024t = jnp.einsum('bsk,bkd->bsd', _ctx_1024c, _ctx_1024P)
        _ctx_1024t = _ctx_1024t * jax.lax.rsqrt(jnp.mean(jnp.square(_ctx_1024t)) + 1e-12) * 0.953939
        ctx_1024 = -1.39393e-06 + 0.999914 * (_ctx_1024t + 0.3 * jax.random.normal(jax.random.fold_in(_rk, 611), (16, 1500, 128), jnp.float32))
        _validS = jnp.arange(56)[None, :] < _lenS[:, None]
        _validS2 = jnp.arange(1500)[None, :] < _lenS2[:, None]
        _causal = jnp.tril(jnp.ones((56, 56), dtype=bool))
        mask_BxS2_bf0 = jnp.logical_not(jnp.ones((16, 1500), dtype=bool))
        return (x, ctx_1024, mask_BxS2_bf0)
    x, ctx_1024, mask_BxS2_bf0 = _rec_inputs()

    def _L0_attn_setup():
        import jax, jax.numpy as jnp
        import numpy as np
        DIM = 128
        HEADS = 16
        DIM_HEAD = 64
        INNER = HEADS * DIM_HEAD
        EPS = 1e-10

        def safe_softmax(s):
            m = jnp.max(s, axis=-1, keepdims=True)
            e = jnp.exp(s - m)
            return e / (jnp.sum(e, axis=-1, keepdims=True) + EPS)
        key = jax.random.key(seed)
        ks = jax.random.split(key, 6)
        B, N = (4, 256)
        x = jax.random.normal(ks[0], (B, N, DIM), dtype=jnp.float32)
        s_in = 1.0 / np.sqrt(DIM)
        s_inner = 1.0 / np.sqrt(INNER)
        Wq = jax.random.uniform(ks[1], (INNER, DIM), jnp.float32, -s_in, s_in)
        Wk = jax.random.uniform(ks[2], (INNER, DIM), jnp.float32, -s_in, s_in)
        Wv = jax.random.uniform(ks[3], (INNER, DIM), jnp.float32, -s_in, s_in)
        Wo = jax.random.uniform(ks[4], (DIM, INNER), jnp.float32, -s_inner, s_inner)
        bo = jax.random.uniform(ks[5], (DIM,), jnp.float32, -s_inner, s_inner)
        return {'x': x, 'Wq': Wq, 'Wk': Wk, 'Wv': Wv, 'Wo': Wo, 'bo': bo}
    _L0_attn_all = _L0_attn_setup()
    _L0_attn_in = {k: v for k, v in _L0_attn_all.items() if k in ('Wq', 'Wk', 'Wv', 'Wo', 'bo')}
    del _L0_attn_all

    def _L0_xattn_setup():
        import jax, jax.numpy as jnp
        import numpy as np
        D_MODEL = 128
        NUM_HEADS = 16
        D_K = D_MODEL // NUM_HEADS

        def _split_heads(x):
            B, S, _ = x.shape
            return x.reshape(B, S, NUM_HEADS, D_K).transpose(0, 2, 1, 3)
        key = jax.random.key(seed)
        ks = jax.random.split(key, 11)
        B, S = (2, 256)
        scale = 1.0 / np.sqrt(D_MODEL)
        inp = {'Q': jax.random.normal(ks[0], (B, S, D_MODEL), jnp.float32), 'K': jax.random.normal(ks[1], (B, S, D_MODEL), jnp.float32), 'V': jax.random.normal(ks[2], (B, S, D_MODEL), jnp.float32), 'W_q': jax.random.normal(ks[3], (D_MODEL, D_MODEL), jnp.float32) * scale, 'b_q': jnp.zeros((D_MODEL,), jnp.float32), 'W_k': jax.random.normal(ks[4], (D_MODEL, D_MODEL), jnp.float32) * scale, 'b_k': jnp.zeros((D_MODEL,), jnp.float32), 'W_v': jax.random.normal(ks[5], (D_MODEL, D_MODEL), jnp.float32) * scale, 'b_v': jnp.zeros((D_MODEL,), jnp.float32), 'W_o': jax.random.normal(ks[6], (D_MODEL, D_MODEL), jnp.float32) * scale, 'b_o': jnp.zeros((D_MODEL,), jnp.float32)}
        return inp
    _L0_xattn_all = _L0_xattn_setup()
    _L0_xattn_in = {k: v for k, v in _L0_xattn_all.items() if k in ('W_q', 'b_q', 'W_k', 'b_k', 'W_v', 'b_v', 'W_o', 'b_o')}
    del _L0_xattn_all

    def _L0_ffn_setup():
        import jax, jax.numpy as jnp
        import numpy as np
        B, S, D, H, E = (8, 512, 128, 256, 8)
        key = jax.random.key(seed)
        ks = jax.random.split(key, 7)
        scale = 0.02
        return {'x': jax.random.normal(ks[0], (B, S, D), dtype=jnp.float32), 'W1': jax.random.normal(ks[1], (E, D, H), dtype=jnp.float32) * scale, 'b1': jnp.zeros((E, H), dtype=jnp.float32), 'W2': jax.random.normal(ks[2], (E, H, D), dtype=jnp.float32) * scale, 'b2': jnp.zeros((E, D), dtype=jnp.float32), 'Wg': jax.random.normal(ks[3], (D, E), dtype=jnp.float32) * scale, 'bg': jnp.zeros((E,), dtype=jnp.float32)}
    _L0_ffn_all = _L0_ffn_setup()
    _L0_ffn_in = {k: v for k, v in _L0_ffn_all.items() if k in ('W1', 'b1', 'W2', 'b2', 'Wg', 'bg')}
    del _L0_ffn_all

    def _L1_attn_setup():
        import jax, jax.numpy as jnp
        import numpy as np
        import math
        EPS_LN = 1e-05
        SCALE = 16.0

        def layer_norm(x, g):
            mean = jnp.mean(x, axis=-1, keepdims=True)
            var = jnp.var(x, axis=-1, keepdims=True)
            return (x - mean) * jax.lax.rsqrt(var + EPS_LN) * g

        def l2norm(t):
            n = jnp.linalg.norm(t, axis=-1, keepdims=True)
            return t / jnp.maximum(n, 1e-12)
        key = jax.random.key(seed)
        ks = jax.random.split(key, 4)
        b, n, dim, h, dh = (4, 256, 128, 8, 64)
        inner = h * dh
        x = jax.random.normal(ks[0], (b, n, dim), dtype=jnp.float32)
        Wq = jax.random.normal(ks[1], (dim, inner), dtype=jnp.float32) * dim ** (-0.5)
        Wkv = jax.random.normal(ks[2], (dim, 2 * dh), dtype=jnp.float32) * dim ** (-0.5)
        Wout = jax.random.normal(ks[3], (inner, dim), dtype=jnp.float32) * inner ** (-0.5)
        norm_g = jnp.ones((dim,), dtype=jnp.float32)
        out_norm_g = jnp.ones((dim,), dtype=jnp.float32)
        return {'x': x, 'norm_g': norm_g, 'Wq': Wq, 'Wkv': Wkv, 'Wout': Wout, 'out_norm_g': out_norm_g}
    _L1_attn_all = _L1_attn_setup()
    _L1_attn_in = {k: v for k, v in _L1_attn_all.items() if k in ('norm_g', 'Wq', 'Wkv', 'Wout', 'out_norm_g')}
    del _L1_attn_all

    def _L1_xattn_setup():
        import jax, jax.numpy as jnp
        import numpy as np
        D_MODEL = 128
        N_HEADS = 16
        D_HEAD = 64
        EPS = 1e-05
        GROK_SCALE = 30.0
        ROPE_BASE = 10000.0

        def layer_norm(x, g, b):
            m = jnp.mean(x, axis=-1, keepdims=True)
            v = jnp.var(x, axis=-1, keepdims=True)
            return (x - m) * jax.lax.rsqrt(v + EPS) * g + b

        def rope(x):
            T, D = (x.shape[-2], x.shape[-1])
            inv_freq = 1.0 / ROPE_BASE ** (jnp.arange(0, D, 2, dtype=jnp.float32) / D)
            freqs = jnp.arange(T, dtype=jnp.float32)[:, None] * inv_freq[None, :]
            emb = jnp.repeat(freqs, 2, axis=-1)
            cos, sin = (jnp.cos(emb), jnp.sin(emb))
            xp = x.reshape(x.shape[:-1] + (D // 2, 2))
            rot = jnp.stack([-xp[..., 1], xp[..., 0]], axis=-1).reshape(x.shape)
            return x * cos + rot * sin
        key = jax.random.key(seed)
        ks = jax.random.split(key, 7)
        N, T = (2, 256)
        f = lambda k, sh: jax.random.normal(k, sh, dtype=jnp.float32)
        return {'query_sequences': f(ks[0], (N, T, D_MODEL)), 'key_sequences': f(ks[1], (N, T, D_MODEL)), 'value_sequences': f(ks[2], (N, T, D_MODEL)), 'attention_mask': jnp.zeros((N, T), dtype=bool), 'Wq': f(ks[3], (D_MODEL, N_HEADS * D_HEAD)) * 0.02, 'Wk': f(ks[4], (D_MODEL, N_HEADS * D_HEAD)) * 0.02, 'Wv': f(ks[5], (D_MODEL, N_HEADS * D_HEAD)) * 0.02, 'Wo': f(ks[6], (N_HEADS * D_HEAD, D_MODEL)) * 0.02, 'ln_g': jnp.ones((D_MODEL,), dtype=jnp.float32), 'ln_b': jnp.zeros((D_MODEL,), dtype=jnp.float32)}
    _L1_xattn_all = _L1_xattn_setup()
    _L1_xattn_in = {k: v for k, v in _L1_xattn_all.items() if k in ('Wq', 'Wk', 'Wv', 'Wo', 'ln_g', 'ln_b')}
    del _L1_xattn_all

    def _L1_ffn_setup():
        import math
        import jax, jax.numpy as jnp
        import numpy as np
        D_MODEL = 128
        D_HIDDEN = 512
        N_EXPERTS = 8
        TOP_K = 2
        CAPACITY_FACTOR = 1.25
        key = jax.random.key(seed)
        ks = jax.random.split(key, 8)
        s = 0.02
        x = jax.random.normal(ks[0], (4, 256, D_MODEL), dtype=jnp.float32)
        router_w = jax.random.normal(ks[1], (D_MODEL, N_EXPERTS), dtype=jnp.float32) * s
        router_b = jnp.zeros((N_EXPERTS,), dtype=jnp.float32)
        w1 = jax.random.normal(ks[2], (N_EXPERTS, D_MODEL, D_HIDDEN), dtype=jnp.float32) * s
        b1 = jnp.zeros((N_EXPERTS, D_HIDDEN), dtype=jnp.float32)
        w2 = jax.random.normal(ks[3], (N_EXPERTS, D_HIDDEN, D_MODEL), dtype=jnp.float32) * s
        b2 = jnp.zeros((N_EXPERTS, D_MODEL), dtype=jnp.float32)
        return {'x': x, 'router_w': router_w, 'router_b': router_b, 'w1': w1, 'b1': b1, 'w2': w2, 'b2': b2}
    _L1_ffn_all = _L1_ffn_setup()
    _L1_ffn_in = {k: v for k, v in _L1_ffn_all.items() if k in ('router_w', 'router_b', 'w1', 'b1', 'w2', 'b2')}
    del _L1_ffn_all
    return {'x': x, 'ctx_1024': ctx_1024, 'mask_BxS2_bf0': mask_BxS2_bf0, 'L0_attn_Wq': _L0_attn_in['Wq'], 'L0_attn_Wk': _L0_attn_in['Wk'], 'L0_attn_Wv': _L0_attn_in['Wv'], 'L0_attn_Wo': _L0_attn_in['Wo'], 'L0_attn_bo': _L0_attn_in['bo'], 'L0_xattn_W_q': _L0_xattn_in['W_q'], 'L0_xattn_b_q': _L0_xattn_in['b_q'], 'L0_xattn_W_k': _L0_xattn_in['W_k'], 'L0_xattn_b_k': _L0_xattn_in['b_k'], 'L0_xattn_W_v': _L0_xattn_in['W_v'], 'L0_xattn_b_v': _L0_xattn_in['b_v'], 'L0_xattn_W_o': _L0_xattn_in['W_o'], 'L0_xattn_b_o': _L0_xattn_in['b_o'], 'L0_ffn_W1': _L0_ffn_in['W1'], 'L0_ffn_b1': _L0_ffn_in['b1'], 'L0_ffn_W2': _L0_ffn_in['W2'], 'L0_ffn_b2': _L0_ffn_in['b2'], 'L0_ffn_Wg': _L0_ffn_in['Wg'], 'L0_ffn_bg': _L0_ffn_in['bg'], 'L1_attn_norm_g': _L1_attn_in['norm_g'], 'L1_attn_Wq': _L1_attn_in['Wq'], 'L1_attn_Wkv': _L1_attn_in['Wkv'], 'L1_attn_Wout': _L1_attn_in['Wout'], 'L1_attn_out_norm_g': _L1_attn_in['out_norm_g'], 'L1_xattn_Wq': _L1_xattn_in['Wq'], 'L1_xattn_Wk': _L1_xattn_in['Wk'], 'L1_xattn_Wv': _L1_xattn_in['Wv'], 'L1_xattn_Wo': _L1_xattn_in['Wo'], 'L1_xattn_ln_g': _L1_xattn_in['ln_g'], 'L1_xattn_ln_b': _L1_xattn_in['ln_b'], 'L1_ffn_router_w': _L1_ffn_in['router_w'], 'L1_ffn_router_b': _L1_ffn_in['router_b'], 'L1_ffn_w1': _L1_ffn_in['w1'], 'L1_ffn_b1': _L1_ffn_in['b1'], 'L1_ffn_w2': _L1_ffn_in['w2'], 'L1_ffn_b2': _L1_ffn_in['b2']}

def reference(x, ctx_1024, mask_BxS2_bf0, L0_attn_Wq, L0_attn_Wk, L0_attn_Wv, L0_attn_Wo, L0_attn_bo, L0_xattn_W_q, L0_xattn_b_q, L0_xattn_W_k, L0_xattn_b_k, L0_xattn_W_v, L0_xattn_b_v, L0_xattn_W_o, L0_xattn_b_o, L0_ffn_W1, L0_ffn_b1, L0_ffn_W2, L0_ffn_b2, L0_ffn_Wg, L0_ffn_bg, L1_attn_norm_g, L1_attn_Wq, L1_attn_Wkv, L1_attn_Wout, L1_attn_out_norm_g, L1_xattn_Wq, L1_xattn_Wk, L1_xattn_Wv, L1_xattn_Wo, L1_xattn_ln_g, L1_xattn_ln_b, L1_ffn_router_w, L1_ffn_router_b, L1_ffn_w1, L1_ffn_b1, L1_ffn_w2, L1_ffn_b2):
    import jax
    import jax.numpy as jnp

    def _L0_attn_ref(x, Wq, Wk, Wv, Wo, bo):
        import jax, jax.numpy as jnp
        import numpy as np
        DIM = 128
        HEADS = 16
        DIM_HEAD = 64
        INNER = HEADS * DIM_HEAD
        EPS = 1e-10

        def safe_softmax(s):
            m = jnp.max(s, axis=-1, keepdims=True)
            e = jnp.exp(s - m)
            return e / (jnp.sum(e, axis=-1, keepdims=True) + EPS)
        B, N, _ = x.shape
        scale = DIM_HEAD ** (-0.5)

        def split_heads(t):
            return t.reshape(B, N, HEADS, DIM_HEAD).transpose(0, 2, 1, 3)
        q = split_heads(x @ Wq.T)
        k = split_heads(x @ Wk.T)
        v = split_heads(x @ Wv.T)
        sim = jnp.einsum('bhid,bhjd->bhij', q, k) * scale
        attn = safe_softmax(sim)
        out = jnp.einsum('bhij,bhjd->bhid', attn, v)
        out = out.transpose(0, 2, 1, 3).reshape(B, N, INNER)
        return out @ Wo.T + bo

    def _L0_xattn_ref(Q, K, V, W_q, b_q, W_k, b_k, W_v, b_v, W_o, b_o):
        import jax, jax.numpy as jnp
        import numpy as np
        D_MODEL = 128
        NUM_HEADS = 16
        D_K = D_MODEL // NUM_HEADS

        def _split_heads(x):
            B, S, _ = x.shape
            return x.reshape(B, S, NUM_HEADS, D_K).transpose(0, 2, 1, 3)
        q = _split_heads(Q @ W_q.T + b_q)
        k = _split_heads(K @ W_k.T + b_k)
        v = _split_heads(V @ W_v.T + b_v)
        scores = jnp.einsum('bhqd,bhkd->bhqk', q, k) / jnp.sqrt(jnp.float32(D_K))
        probs = jax.nn.softmax(scores, axis=-1)
        ctx = jnp.einsum('bhqk,bhkd->bhqd', probs, v)
        B, H, S, d = ctx.shape
        ctx = ctx.transpose(0, 2, 1, 3).reshape(B, S, H * d)
        return ctx @ W_o.T + b_o

    def _L0_ffn_ref(x, W1, b1, W2, b2, Wg, bg):
        import jax, jax.numpy as jnp
        import numpy as np
        B, S, D, H, E = (8, 512, 128, 256, 8)
        logits = jnp.einsum('bsd,de->bse', x, Wg) + bg
        probs = jax.nn.softmax(logits, axis=-1)
        top1 = jnp.argmax(probs, axis=-1)
        out = jnp.zeros_like(x)
        for e in range(E):
            coef = jnp.where(top1 == e, probs[..., e], 0.0)[..., None]
            h = jax.nn.gelu(jnp.einsum('bsd,dh->bsh', x, W1[e]) + b1[e], approximate=False)
            y = jnp.einsum('bsh,hd->bsd', h, W2[e]) + b2[e]
            out = out + coef * y
        return out

    def _L1_attn_ref(x, norm_g, Wq, Wkv, Wout, out_norm_g):
        import jax, jax.numpy as jnp
        import numpy as np
        import math
        EPS_LN = 1e-05
        SCALE = 16.0

        def layer_norm(x, g):
            mean = jnp.mean(x, axis=-1, keepdims=True)
            var = jnp.var(x, axis=-1, keepdims=True)
            return (x - mean) * jax.lax.rsqrt(var + EPS_LN) * g

        def l2norm(t):
            n = jnp.linalg.norm(t, axis=-1, keepdims=True)
            return t / jnp.maximum(n, 1e-12)
        b, n, dim = x.shape
        h = 8
        dh = Wkv.shape[-1] // 2
        xn = layer_norm(x, norm_g)
        q = xn @ Wq
        kv = xn @ Wkv
        k, v = (kv[..., :dh], kv[..., dh:])
        q = q.reshape(b, n, h, dh).transpose(0, 2, 1, 3)
        q = q * SCALE
        q = l2norm(q)
        k = l2norm(k)
        rs = math.sqrt(SCALE)
        q = q * rs
        k = k * rs
        sim = jnp.einsum('bhid,bjd->bhij', q, k)
        attn = jax.nn.softmax(sim.astype(jnp.float32), axis=-1).astype(sim.dtype)
        out = jnp.einsum('bhij,bjd->bhid', attn, v)
        out = out.transpose(0, 2, 1, 3).reshape(b, n, h * dh)
        out = out @ Wout
        return layer_norm(out, out_norm_g)

    def _L1_xattn_ref(query_sequences, key_sequences, value_sequences, attention_mask, Wq, Wk, Wv, Wo, ln_g, ln_b):
        import jax, jax.numpy as jnp
        import numpy as np
        D_MODEL = 128
        N_HEADS = 16
        D_HEAD = 64
        EPS = 1e-05
        GROK_SCALE = 30.0
        ROPE_BASE = 10000.0

        def layer_norm(x, g, b):
            m = jnp.mean(x, axis=-1, keepdims=True)
            v = jnp.var(x, axis=-1, keepdims=True)
            return (x - m) * jax.lax.rsqrt(v + EPS) * g + b

        def rope(x):
            T, D = (x.shape[-2], x.shape[-1])
            inv_freq = 1.0 / ROPE_BASE ** (jnp.arange(0, D, 2, dtype=jnp.float32) / D)
            freqs = jnp.arange(T, dtype=jnp.float32)[:, None] * inv_freq[None, :]
            emb = jnp.repeat(freqs, 2, axis=-1)
            cos, sin = (jnp.cos(emb), jnp.sin(emb))
            xp = x.reshape(x.shape[:-1] + (D // 2, 2))
            rot = jnp.stack([-xp[..., 1], xp[..., 0]], axis=-1).reshape(x.shape)
            return x * cos + rot * sin
        q = layer_norm(query_sequences, ln_g, ln_b)
        k = layer_norm(key_sequences, ln_g, ln_b)
        v = layer_norm(value_sequences, ln_g, ln_b)
        N, t, _ = q.shape
        T = k.shape[1]
        qh = (q @ Wq).reshape(N, t, N_HEADS, D_HEAD).transpose(0, 2, 1, 3)
        kh = (k @ Wk).reshape(N, T, N_HEADS, D_HEAD).transpose(0, 2, 1, 3)
        vh = (v @ Wv).reshape(N, T, N_HEADS, D_HEAD).transpose(0, 2, 1, 3)
        qh = rope(qh)
        kh = rope(kh)
        aw = jnp.einsum('nhtd,nhTd->nhtT', qh, kh)
        aw = aw * (1.0 / jnp.sqrt(jnp.float32(D_HEAD)))
        aw = GROK_SCALE * jnp.tanh(aw / GROK_SCALE)
        pad = attention_mask[:, None, None, :]
        causal = ~jnp.tril(jnp.ones((t, T), dtype=bool))
        aw = jnp.where(pad | causal, -jnp.inf, aw)
        p = jax.nn.softmax(aw, axis=-1)
        out = jnp.einsum('nhtT,nhTd->nhtd', p, vh)
        out = out.transpose(0, 2, 1, 3).reshape(N, t, N_HEADS * D_HEAD)
        return out @ Wo

    def _L1_ffn_ref(x, router_w, router_b, w1, b1, w2, b2):
        import math
        import jax, jax.numpy as jnp
        import numpy as np
        D_MODEL = 128
        D_HIDDEN = 512
        N_EXPERTS = 8
        TOP_K = 2
        CAPACITY_FACTOR = 1.25
        B, T, D = x.shape
        N = B * T
        E = N_EXPERTS
        capacity = max(1, math.ceil(N / E * CAPACITY_FACTOR))
        x_flat = x.reshape(N, D)
        logits = x_flat.astype(jnp.float32) @ router_w + router_b
        gates = jax.nn.softmax(logits, axis=-1)
        _, topk_idx = jax.lax.top_k(gates, TOP_K)
        expert_mask = jax.nn.one_hot(topk_idx, E, dtype=jnp.int32).sum(1)
        pos = jnp.cumsum(expert_mask, axis=0) - 1
        expert_mask = expert_mask * (pos < capacity)
        valid = expert_mask > 0
        pos_c = jnp.where(valid, pos, capacity)
        e_idx = jnp.broadcast_to(jnp.arange(E), (N, E))
        dispatched = x_flat[:, None, :] * valid[:, :, None].astype(x.dtype)
        buf = jnp.zeros((E, capacity + 1, D), x.dtype).at[e_idx.ravel(), pos_c.ravel()].add(dispatched.reshape(N * E, D))
        buf = buf[:, :capacity]
        h = jax.nn.gelu(jnp.einsum('ecd,edh->ech', buf, w1) + b1[:, None, :], approximate=False)
        out = jnp.einsum('ech,ehd->ecd', h, w2) + b2[:, None, :]
        pos_g = jnp.minimum(pos_c, capacity - 1)
        gathered = out[e_idx, pos_g]
        weights = (gates * valid).astype(x.dtype)
        y = jnp.einsum('ned,ne->nd', gathered, weights)
        return y.reshape(B, T, D)
    x = x + _L0_attn_ref(_layernorm(x, axis=-1), L0_attn_Wq, L0_attn_Wk, L0_attn_Wv, L0_attn_Wo, L0_attn_bo)
    x = x + _L0_xattn_ref(_layernorm(x, axis=-1), ctx_1024, ctx_1024, L0_xattn_W_q, L0_xattn_b_q, L0_xattn_W_k, L0_xattn_b_k, L0_xattn_W_v, L0_xattn_b_v, L0_xattn_W_o, L0_xattn_b_o)
    x = x + _L0_ffn_ref(_layernorm(x, axis=-1), L0_ffn_W1, L0_ffn_b1, L0_ffn_W2, L0_ffn_b2, L0_ffn_Wg, L0_ffn_bg)
    x = x + _L1_attn_ref(_layernorm(x, axis=-1), L1_attn_norm_g, L1_attn_Wq, L1_attn_Wkv, L1_attn_Wout, L1_attn_out_norm_g)
    x = x + _L1_xattn_ref(_layernorm(x, axis=-1), ctx_1024, ctx_1024, mask_BxS2_bf0, L1_xattn_Wq, L1_xattn_Wk, L1_xattn_Wv, L1_xattn_Wo, L1_xattn_ln_g, L1_xattn_ln_b)
    x = x + _L1_ffn_ref(_layernorm(x, axis=-1), L1_ffn_router_w, L1_ffn_router_b, L1_ffn_w1, L1_ffn_b1, L1_ffn_w2, L1_ffn_b2)
    return x

_drawn_inputs = setup_inputs


def setup_inputs(seed=0):
    import zlib

    import numpy as np

    out = dict(_drawn_inputs(seed))
    spreads = {'L0_xattn_b_q': (0.0, 0.281),
     'L0_xattn_b_k': (0.0, 0.8),
     'L0_xattn_b_v': (0.0, 0.1),
     'L0_xattn_b_o': (0.0, 0.1),
     'L0_ffn_b1': (0.0, 0.8),
     'L0_ffn_b2': (0.0, 0.442),
     'L0_ffn_bg': (0.0, 0.675),
     'L1_attn_norm_g': (1.0, 0.2),
     'L1_attn_out_norm_g': (1.0, 0.2),
     'L1_xattn_ln_g': (1.0, 0.6),
     'L1_xattn_ln_b': (0.0, 0.8),
     'L1_ffn_router_b': (0.0, 0.776),
     'L1_ffn_b1': (0.0, 0.8),
     'L1_ffn_b2': (0.0, 0.689)}
    factors = {'L0_attn_Wq': 2.921,
     'L0_attn_Wk': 2.832,
     'L0_ffn_W1': 8.0,
     'L0_ffn_W2': 7.469,
     'L0_ffn_Wg': 3.293,
     'L1_xattn_Wq': 8.0,
     'L1_xattn_Wk': 8.0,
     'L1_ffn_router_w': 4.897,
     'L1_ffn_w1': 8.0,
     'L1_ffn_w2': 8.0}
    for name, (base, spread) in spreads.items():
        noise = np.random.default_rng([zlib.crc32(name.encode()), seed]).standard_normal(out[name].shape)
        drawn = base * np.exp(spread * noise) if base else spread * noise
        out[name] = jnp.asarray(drawn.astype(out[name].dtype))
    for name, factor in factors.items():
        out[name] = (out[name] * factor).astype(out[name].dtype)
    return out
```

```python
import math
from contextlib import ExitStack

import concourse.bass as bass
from concourse import mybir

B, S, D = 16, 56, 128
SK = 1500
PAIRS = B // 2
HALF = 64
TILE = 2 * HALF
HEADS, DH = 16, 64
INNER = HEADS * DH
XD = D // HEADS
XG = HEADS // 2
XQ = 2 * S
K_PART = (0, 0, 0, 1, 1, 2)
Q_PART = (0, 1, 2, 0, 1, 0)
STACK = len(K_PART) * 2 * XD
SHIFT = STACK
KT, KN = 12, 125
THIRDS, KC = 3, 500
VW = 2 * (XD + 1)
VROW = XG * VW + 32 - VW
H1 = 8
E, F0, F1 = 8, 256, 512
CAPACITY = max(1, math.ceil(B * S / E * 1.25))
LN_EPS, SAFE_EPS, NORM_EPS = 1e-5, 1e-10, 1e-12
GROK = 30.0

C_IDENT, C_COS, C_SIN, C_CAUSAL, C_TRI, C_ONES = 0, 128, 256, 384, 448, 576
C_TIE, C_BLK, C_MASK1, C_MASK2, C_MHALF, C_HALF, C_END = 704, 712, 714, 715, 716, 718, 736
R_BO, R_BV, R_BO2, R_BG, R_NG, R_ONG, R_LG, R_LB, R_RB, R_END = 0, 128, 256, 384, 392, 520, 648, 776, 904, 912
P_BK, P_BQ, P_B1, P_B1L, P_END = 0, 1, 9, 25, 57


class Steps:

    def __init__(self, engine, semaphore, before):
        self.engine, self.semaphore, self.before, self.n = engine, semaphore, before, 0

    def __call__(self, instruction):
        instruction.then_inc(self.semaphore, 1)
        self.n += 1
        self.engine.wait_ge(self.semaphore, self.before + self.n)


def decoder_kernel(nc, x, ctx_t, ctx_first, mask, consts, rows, cols, a_wq, a_wk, a_wv, a_wo,
                   x_wq, x_wk, x_wv, x_wo, g_w, f_w1, f_w2, f_b2, m_wq, m_wkv, m_wo,
                   r_wq, r_wqr, r_wk, r_wkr, r_wv, r_wo, l_w, l_w1, l_w2, l_b2, out):
    f32, bf16 = mybir.dt.float32, mybir.dt.bfloat16
    ALU, ACT, AX = mybir.AluOpType, mybir.ActivationFunctionType, mybir.AxisListType

    ctx = ExitStack()
    with ctx:
        def sb(name, shape, dt=f32):
            return ctx.enter_context(nc.sbuf_tensor(name, shape, dt))

        def signals(stage, names):
            return [ctx.enter_context(nc.semaphore(f"{stage}_{n}")) for n in names.split()]

        X = sb("X", [128, PAIRS, D])
        CT = sb("CT", [128, C_END])
        RW = sb("RW", [128, R_END])
        PC = sb("PC", [128, P_END])
        ident = CT[:, C_IDENT:C_IDENT + 128]
        identb = sb("identb", [128, 128], bf16)
        st = sb("st", [128, 2, 6])
        mv = sb("mv", [128, 2, 2])
        vr = sb("vr", [128, 2])
        rstd = sb("rstd", [128, 2])
        XN = sb("XN", [128, 2, D])
        XNT = sb("XNT", [128, 2, TILE])
        QS = sb("QS", [SHIFT + 1, B, XG, XQ], bf16)
        PO = sb("PO", [128, PAIRS, 2, 2, TILE])
        sm = sb("sm", [128, 2, 64])
        XWK, XWV, XWO = sb("XWK", [128, D]), sb("XWV", [128, D]), sb("XWO", [128, D])
        FW1 = sb("FW1", [128, E, F0])
        FW2 = sb("FW2", [128, E * F0 // 128, D])
        mask8 = sb("mask8", [128, PAIRS], mybir.dt.uint8)

        ARENA = 31400
        arena = sb("arena", [128, ARENA])
        place = [0]

        def take(*shape, dt=f32):
            n = math.prod(shape)
            words = n if dt == f32 else (n + 1) // 2
            part = arena[:, place[0]:place[0] + words]
            place[0] += words
            assert place[0] <= ARENA, place[0]
            if dt != f32:
                part = part.bitcast(dt)
            if len(shape) == 1:
                return part
            names = "abcd"[:len(shape)]
            return part.rearrange(f"p ({' '.join(names)}) -> p {' '.join(names)}",
                                  **{k: v for k, v in zip(names[1:], shape[1:])})

        WQ, WK, WV, WO = take(INNER), take(INNER), take(2, 8 * DH), take(8, D)
        WQS = take(XG, STACK)
        work = place[0]
        qT, kT, V = take(2, 8, TILE), take(2, 8, TILE), take(2, 2, 8 * DH)
        P, PT, OT = take(2, HEADS, HALF), take(2, 8, TILE), take(2, 8, TILE)
        qf = take(2, XG, TILE)
        q1, q2 = take(2, XG, TILE, dt=bf16), take(2, XG, TILE, dt=bf16)
        place[0] = work
        KS = [take(XG, SK, dt=bf16) for _ in range(2)]
        CX = [take(SK) for _ in range(2)]
        VX = [take(KT, VROW) for _ in range(2)]
        PX = [take(XG, XQ) for _ in range(2)]
        kf, kr, kp = take(THIRDS, KC), take(KC), take(THIRDS, 3, KC, dt=bf16)
        MX, CM, CB = take(XG, THIRDS), take(XG), take(XG, dt=bf16)
        place[0] = 0
        MWQ, MWKV, MWO = take(H1 * DH), take(2 * DH), take(4, D)
        GW, LW, FB2, LB2 = take(E), take(E), take(D), take(D)
        RWQ, RWQR = take(INNER), take(INNER)
        assert place[0] <= work
        place[0] = work
        RWK, RWKR, RWV, RWO = take(INNER), take(INNER), take(INNER), take(8, D)
        LW1, LW2 = take(E, F1), take(E * F1 // 128, D)
        coef, coefT = take(2, E), take(2, TILE)
        GATE, PICK, BEFORE, WGT = (take(PAIRS, E) for _ in range(4))
        XNTA = take(PAIRS, TILE)
        late = place[0]
        PF, CN, CNT = take(2, 4, TILE), take(2, D), take(2, TILE)
        HB = take(8, 2 * TILE)
        place[0] = late
        T1, T2, T3, T4 = (take(2, INNER) for _ in range(4))
        VM = take(2, HEADS, DH + 1)
        C56, KEEP, MK = take(PAIRS, D), take(PAIRS, HALF), take(PAIRS)
        KX, KXT = take(2, D), take(2, TILE)

        ps = ctx.enter_context(nc.psum_tensor("ps", [128, 8, 512], f32))
        k_scratch = nc.dram_tensor("k_parts", (2, 3, 128, SK), bf16, kind="Internal").ap()

        (load_passed, load_consts, load_tokens, load_attn_w, load_middle_w, load_late_w, load_context) = signals(
            "load", "passed consts tokens attn_w middle_w late_w context")
        (ln_stats, ln_moments, ln_variance, ln_rstd) = signals(
            "ln", "stats moments variance rstd")
        (attn_cleared, attn_normed, attn_xT, attn_xnT, attn_q_proj, attn_k_proj, attn_v_proj, attn_q, attn_k,
         attn_v, attn_scores, attn_top, attn_shifted, attn_expd, attn_steps, attn_probs, attn_probsT, attn_pT,
         attn_pv, attn_o, attn_proj, attn_sum, attn_x1, attn_normed2, attn_xT2, attn_xnT2, attn_stack, attn_qf,
         attn_q1, attn_r1, attn_q2, attn_r2, attn_qstack) = signals(
            "attn", "cleared normed xT xnT q_proj k_proj v_proj q k v scores top shifted expd steps probs probsT pT pv o "
            "proj sum x1 normed2 xT2 xnT2 stack qf q1 r1 q2 r2 qstack")
        (cross_cleared, cross_ctx0, cross_ctx1, cross_k_proj, cross_kf, cross_r1, cross_k2, cross_k3, cross_out0,
         cross_out1, cross_out2, cross_in0, cross_in1, cross_in2, cross_v_proj, cross_v, cross_smax, cross_top,
         cross_best, cross_negated, cross_shift, cross_shifted, cross_scores, cross_probs, cross_pv, cross_o) = signals(
            "cross", "cleared ctx0 ctx1 k_proj kf r1 k2 k3 out0 out1 out2 in0 in1 in2 v_proj v smax top best negated shift "
            "shifted scores probs pv o")
        (tail_copied, tail_turned, tail_steps, tail_ctx, tail_ctxT, tail_ctxS, tail_proj, tail_sum, tail_x2,
         tail_normed, tail_xT, tail_xnT, tail_logits, tail_shifted, tail_expd, tail_coef, tail_coefT, tail_coefS,
         tail_b2, tail_x2b, tail_h, tail_gelu, tail_y, tail_acc) = signals(
            "tail", "copied turned steps ctx ctxT ctxS proj sum x2 normed xT xnT logits shifted expd coef coefT coefS b2 "
            "x2b h gelu y acc")
        (mqa_cleared, mqa_normed1, mqa_normed, mqa_scaled, mqa_xT, mqa_xnT, mqa_qkv, mqa_sq, mqa_ss, mqa_root,
         mqa_steps, mqa_qn, mqa_v, mqa_turned, mqa_qT, mqa_kT, mqa_scores, mqa_probs, mqa_pv, mqa_o, mqa_oT, mqa_oS,
         mqa_proj, mqa_normed2, mqa_outn, mqa_sum) = signals(
            "mqa", "cleared normed1 normed scaled xT xnT qkv sq ss root steps qn v turned qT kT scores probs pv o oT oS "
            "proj normed2 outn sum")
        (rope_keep, rope_normed1, rope_normed, rope_knormed, rope_scaled, rope_xT, rope_xnT, rope_qproj, rope_kproj,
         rope_parts, rope_qT, rope_kT, rope_v_proj, rope_v, rope_scores, rope_tanh, rope_expd, rope_masked, rope_pv,
         rope_steps, rope_o, rope_oT, rope_oS, rope_out) = signals(
            "rope", "keep normed1 normed knormed scaled xT xnT qproj kproj parts qT kT v_proj v scores tanh expd masked "
            "pv steps o oT oS out")
        (moe_kept_xT, moe_steps, moe_weight, moe_count, moe_before, moe_wgt) = signals(
            "moe", "kept_xT steps weight count before wgt")
        (last_h, last_gelu, last_y, last_acc, last_out) = signals(
            "last", "h gelu y acc out")
        tail_ffn = (tail_h, tail_gelu, tail_y, tail_acc)
        last_ffn = (last_h, last_gelu, last_y, last_acc)

        block = ctx.enter_context(nc.Block())

        def mm(o, lhsT, rhs, start=True, stop=True, **kw):
            return nc.tensor.matmul(o, lhsT, rhs, start=start, stop=stop, **kw)

        def wide(ap, n):
            k = len(ap.shape)
            return ap.unsqueeze(k).broadcast_to([*ap.shape, n])

        def over(ap, n):
            return ap.unsqueeze(1).broadcast_to([ap.shape[0], n, *ap.shape[1:]])

        def bank(u, k, n=1):
            return ps[:, 4 * u + k:4 * u + k + n, :].rearrange("p a b -> p (a b)")

        def heads4(u, k, n):
            return ps[:, 4 * u + k:4 * u + k + n, 0:4 * (DH + 1)].rearrange("p a (h w) -> p a h w", w=DH + 1)

        def apart(engine):
            engine.sem_inc(load_passed, 1)

        def ln_vector(dve, nth, srcs, dsts, done):
            apart(dve)
            for u in (0, 1):
                ins = nc.vector.bn_stats(st[:, u, :], srcs[u])
            ins.then_inc(ln_stats, 1)
            dve.wait_ge(ln_stats, nth + 1)
            apart(dve)
            for u in (0, 1):
                ins = nc.vector.bn_aggr(mv[:, u, :], st[:, u, :])
            ins.then_inc(ln_moments, 1)
            dve.wait_ge(ln_moments, nth + 1)
            nc.vector.tensor_scalar(vr[:, :], mv[:, :, 1], LN_EPS, None, ALU.add).then_inc(ln_variance, 1)
            dve.wait_ge(ln_rstd, nth + 1)
            for u in (0, 1):
                ins = nc.vector.tensor_scalar(dsts[u], srcs[u], mv[:, u, 0:1], rstd[:, u:u + 1],
                                              ALU.subtract, ALU.mult)
            ins.then_inc(done, 1)

        def ln_pool(pool, nth):
            pool.wait_ge(ln_variance, nth + 1)
            nc.gpsimd.tensor_tensor(rstd[:, :], vr[:, :], CT[:, C_MHALF:C_MHALF + 2], ALU.pow)\
                .then_inc(ln_rstd, 1)

        N2 = PAIRS // 2
        LN_T = 2 * N2
        LN_M = LN_T + N2
        LN_R = LN_M + 3 * N2
        LN_F = LN_R + 3 * N2
        XS = [XN[:, u, :] for u in (0, 1)]

        @block.sync
        def _(sp):
            for dst, src in ((CT[:, :], consts), (RW[:, :], rows), (PC[:, :], cols)):
                sp.dma_start(dst, src).then_inc(load_consts, 16)
            sp.dma_start(X[:, :, :], x).then_inc(load_tokens, 16)
            sp.dma_start(mask8[:, :], mask).then_inc(load_tokens, 16)
            for dst, src in ((WQ, a_wq), (WK, a_wk), (WV.rearrange("p a b -> p (a b)"), a_wv),
                             (WO, a_wo.rearrange("(j p) d -> p j d", p=128)),
                             (WQS.rearrange("p a b -> p (a b)"), x_wq), (XWK[:, :], x_wk), (XWV[:, :], x_wv),
                             (XWO[:, :], x_wo), (FW1[:, :, :], f_w1.rearrange("e p h -> p e h")),
                             (FW2[:, :, :], f_w2.rearrange("e (j p) d -> p (e j) d", p=128))):
                sp.dma_start(dst, src).then_inc(load_attn_w, 16)

            sp.wait_ge(attn_qstack, PAIRS)
            for dst, src in ((MWQ, m_wq), (MWKV, m_wkv), (MWO, m_wo.rearrange("(j p) d -> p j d", p=128)),
                             (GW, g_w), (LW, l_w), (FB2[0:E, :], f_b2), (LB2[0:E, :], l_b2), (RWQ, r_wq), (RWQR, r_wqr)):
                sp.dma_start(dst, src).then_inc(load_middle_w, 16)
            outs, ins_ = (cross_out0, cross_out1, cross_out2), (cross_in0, cross_in1, cross_in2)

            def load_ctx(b, u, first=False):
                if not first:
                    sp.wait_ge(cross_v_proj, THIRDS * (b - 1))
                    sp.wait_ge(cross_k_proj, THIRDS * (b - 1))
                    apart(sp)
                sp.dma_start(CX[u], ctx_t[b, :, :]).then_inc((cross_ctx0, cross_ctx1)[u], 16)

            def stack_third(b, u, n, first=False):
                lo = n * KC
                sp.wait_ge(cross_k3, THIRDS * b + n + 1)
                apart(sp)
                sp.dma_start(k_scratch[u, :, :, lo:lo + KC].rearrange("c p n -> p c n"), kp[:, n])\
                    .then_inc(outs[n], 16)
                sp.wait_ge(outs[n], 16 * (b + 1))
                apart(sp)
                if not first:
                    sp.wait_ge(cross_scores, KT * (b - 2) + 4 * (n + 1))
                    apart(sp)
                for j, part in enumerate(K_PART):
                    sp.dma_start(KS[u][2 * XD * j:2 * XD * (j + 1), :, lo:lo + KC],
                                 k_scratch[u, part, :, lo:lo + KC].rearrange("(g r) n -> r g n", g=XG))\
                        .then_inc(ins_[n], 16)

            load_ctx(0, 0, True)
            load_ctx(1, 1, True)
            for b in (0, 1):
                for n in range(THIRDS):
                    stack_third(b, b, n, True)

            def cross(b, u):
                load_ctx(b + 2, u)
                for n in range(THIRDS):
                    stack_third(b + 2, u, n)

            with sp.Fori(0, PAIRS - 1) as p:
                cross(2 * p, 0)
                cross(2 * p + 1, 1)

            sp.wait_ge(cross_o, B + 1)
            for dst, src in ((RWK, r_wk), (RWKR, r_wkr), (RWV, r_wv), (RWO, r_wo.rearrange("(j p) d -> p j d", p=128)),
                             (LW1, l_w1.rearrange("e p h -> p e h")),
                             (LW2, l_w2.rearrange("e (j p) d -> p (e j) d", p=128))):
                sp.dma_start(dst, src).then_inc(load_late_w, 16)
            sp.wait_ge(tail_acc, 2 * E * N2 + 1)
            sp.dma_start(C56, ctx_first).then_inc(load_context, 16)

            with sp.Fori(0, N2) as i:
                sp.wait_ge(last_acc, 2 * E * i + 1 + 2 * E)
                apart(sp)
                for b in (0, 1):
                    sp.dma_start(out.rearrange("(t b) s d -> b s t d", b=2)[b, :, 2 * i:2 * i + 2, :] if isinstance(i, int)
                                 else out.rearrange("(t b) s d -> b s t d", b=2)[b, :, bass.ds(2 * i, 2), :],
                                 X[HALF * b:HALF * b + S, bass.ds(2 * i, 2), :]).then_inc(last_out, 16)
            sp.wait_ge(last_out, 16 * 2 * N2)

        @block.tensor
        def _(pe):
            pe.wait_ge(load_consts, 48)
            for y_made in (tail_y, last_y):
                pe.sem_inc(y_made, 1)

            def transposed(u, srcs, dst):
                for j, src in enumerate(srcs):
                    ins = nc.tensor.transpose(dst[:, j * TILE:(j + 1) * TILE], src, ident)
                return ins

            def self_attention(i):
                pe.wait_ge(attn_normed, i + 1)
                for u in (0, 1):
                    transposed(u, [XN[:, u, :]], bank(u, 0)).then_inc(attn_xT, 1)
                for u in (0, 1):
                    pe.wait_ge(attn_xnT, 2 * i + u + 1)
                    for j in range(8):
                        ins = mm(bank(u, 0, 2)[:, j * TILE:(j + 1) * TILE], WQ[:, j * 128:(j + 1) * 128], XNT[:, u, :])
                    ins.then_inc(attn_q_proj, 1)
                    for j in range(8):
                        ins = mm(bank(u, 2, 2)[:, j * TILE:(j + 1) * TILE], WK[:, j * 128:(j + 1) * 128], XNT[:, u, :])
                    ins.then_inc(attn_k_proj, 1)
                for u in (0, 1):
                    pe.wait_ge(attn_q, 2 * i + u + 1)
                    for b in (0, 1):
                        for o in (0, 1):
                            ins = mm(ps[HALF * o:HALF * (o + 1), 4 * u + b, :],
                                     XNT[:, u, HALF * b:HALF * (b + 1)], WV[:, o, :])
                    ins.then_inc(attn_v_proj, 1)
                for u in (0, 1):
                    pe.wait_ge(attn_k, 2 * i + u + 1)
                    apart(pe)
                    for h in range(HEADS):
                        lo = 64 * (h % 2)
                        for b in (0, 1):
                            ins = mm(bank(u, 2 + h % 2)[HALF * b:HALF * (b + 1), h // 2 * HALF:h // 2 * HALF + S],
                                     qT[lo:lo + DH, u, h // 2, HALF * b:HALF * (b + 1)],
                                     kT[lo:lo + DH, u, h // 2, HALF * b:HALF * b + S])
                    ins.then_inc(attn_scores, 1)
                for u in (0, 1):
                    pe.wait_ge(attn_v, 2 * i + u + 1)
                    pe.wait_ge(attn_probs, 2 * i + u + 1)
                    transposed(u, [P[:, u, 2 * j:2 * j + 2, :].rearrange("p a b -> p (a b)") for j in range(8)],
                               bank(u, 0, 2)).then_inc(attn_probsT, 1)
                for u in (0, 1):
                    pe.wait_ge(attn_pT, 2 * i + u + 1)
                    apart(pe)
                    for h in range(HEADS):
                        lo, j = 64 * (h % 2), h // 2
                        for b in (0, 1):
                            at = j * TILE + HALF * b
                            ins = mm(bank(u, 2, 2)[lo:lo + DH, at:at + HALF],
                                     V[lo:lo + S, u, b, j * DH:(j + 1) * DH],
                                     PT[lo:lo + S, u, j, HALF * b:HALF * (b + 1)])
                    ins.then_inc(attn_pv, 1)
                for u in (0, 1):
                    pe.wait_ge(attn_o, 2 * i + u + 1)
                    for j in range(8):
                        ins = mm(bank(u, 0)[:, 0:D], OT[:, u, j, :], WO[:, j, :], start=j == 0, stop=j == 7)
                    ins.then_inc(attn_proj, 1)
                pe.wait_ge(attn_normed2, i + 1)
                for u in (0, 1):
                    transposed(u, [XN[:, u, :]], bank(u, 1)).then_inc(attn_xT2, 1)
                for u in (0, 1):
                    pe.wait_ge(attn_xnT2, 2 * i + u + 1)
                    for n in range(XG):
                        ins = mm(bank(u, 2, 2)[0:STACK, n * TILE:(n + 1) * TILE], WQS[:, n, :], XNT[:, u, :])
                    ins.then_inc(attn_stack, 1)

            pe.wait_ge(load_attn_w, 160)
            with pe.Fori(0, N2) as i:
                self_attention(i)

            ins_ = (cross_in0, cross_in1, cross_in2)

            def project_k(turn, u, n):
                pe.wait_ge((cross_ctx0, cross_ctx1)[u], 16 * (turn + 1))
                mm(ps[:, 7, 0:KC], XWK[:, :], CX[u][:, n * KC:(n + 1) * KC]).then_inc(cross_k_proj, 1)

            def project_v(b, u, n):
                for j in range(4):
                    kt = 4 * n + j
                    ins = mm(ps[0:KN, 7, j * D:(j + 1) * D], CX[u][:, kt * KN:(kt + 1) * KN], XWV[:, :])
                ins.then_inc(cross_v_proj, 1)

            def first_scores(b, u, q):
                n, h = q // XG, q % XG
                if h == 0:
                    pe.wait_ge(ins_[n], 16 * len(K_PART) * (b + 1))
                if not (isinstance(b, int) and b == 0 and q < 2):
                    pe.wait_ge(cross_top, THIRDS * XG * b + q - 1)
                mm(ps[0:XQ, 5 + q % 2, 0:KC], QS[0:STACK, b, h, :], KS[u][0:STACK, h, n * KC:(n + 1) * KC])\
                    .then_inc(cross_smax, 1)

            def shift_row(b):
                pe.wait_ge(cross_negated, b + 1)
                for h in range(XG):
                    ins = mm(ps[SHIFT:SHIFT + 1, 5 + h // 4, (h % 4) * XQ:(h % 4 + 1) * XQ],
                             CB[0:XQ, h:h + 1], identb[0:XQ, 0:XQ])
                ins.then_inc(cross_shift, 1)

            def scores(b, u, kt):
                if kt == 0:
                    pe.wait_ge(cross_shifted, b + 1)
                for h in range(XG):
                    ins = mm(ps[0:KN, 2 * (kt % 2) + h // 4, (h % 4) * XQ:(h % 4 + 1) * XQ],
                             KS[u][0:SHIFT + 1, h, kt * KN:(kt + 1) * KN], QS[0:SHIFT + 1, b, h, :])
                ins.then_inc(cross_scores, 1)

            def outputs(b, u, kt):
                pe.wait_ge(cross_probs, KT * b + kt + 1)
                if kt == 0:
                    pe.wait_ge(cross_o, b + 1)
                for h in range(XG):
                    ins = mm(ps[32 * (h % 4):32 * (h % 4) + 32, 4, (h // 4) * XQ:(h // 4 + 1) * XQ],
                             VX[u][0:KN, kt, h * VW:h * VW + 32], PX[kt % 2][0:KN, h, :],
                             start=kt == 0 and h < 4, stop=kt == KT - 1, skip_group_check=True)
                ins.then_inc(cross_pv, 1)

            SLOTS = (3, 3, 2, 3, 3, 2, 3, 3, 2, 0, 0, 0)

            def cross(turn, u, next_too=True, second_too=True):
                b = 2 * turn + u
                q = 0
                for kt in range(KT):
                    scores(b, u, kt)
                    if next_too:
                        for _ in range(SLOTS[kt]):
                            first_scores(b + 1, 1 - u, q)
                            q += 1
                        if kt % 4 == 0:
                            pe.wait_ge(cross_kf, THIRDS * (b + 2) + (kt // 4 if second_too else 0))
                            project_v(b + 1, 1 - u, kt // 4)
                    if second_too and kt % 4 == 3:
                        pe.wait_ge(cross_v, THIRDS * (b + 1) + kt // 4 + 1)
                        project_k(turn + 1, u, kt // 4)
                    if kt > 0:
                        outputs(b, u, kt - 1)
                    if next_too and kt == 10:
                        shift_row(b + 1)
                outputs(b, u, KT - 1)

            for b in (0, 1):
                for n in range(THIRDS):
                    if b or n:
                        pe.wait_ge(cross_kf, THIRDS * b + n)
                    project_k(0, b, n)
            for n in range(THIRDS):
                pe.wait_ge(cross_kf, 2 * THIRDS)
                if n:
                    pe.wait_ge(cross_v, n)
                project_v(0, 0, n)
            pe.wait_ge(cross_v, THIRDS)
            for q in range(THIRDS * XG):
                first_scores(0, 0, q)
            shift_row(0)
            with pe.Fori(0, PAIRS - 1) as p:
                cross(p, 0)
                cross(p, 1)
            cross(PAIRS - 1, 0, second_too=False)
            cross(PAIRS - 1, 1, next_too=False, second_too=False)

            HBANK = (0, 1, 4, 5)

            def feed_forward(i, sig, tiles, w1, w2, tokens):
                h_made, gelu_done, y_made, y_added = sig
                first = i * E * tiles
                for e in range(E + 1):
                    if e < E:
                        for k in range(tiles):
                            q = e * tiles + k
                            if q % 2 == 0:
                                pe.wait_ge(gelu_done, first + 1 + max(q - 6, 0))
                            mm(ps[:, HBANK[q // 2 % 4], (q % 2) * 2 * TILE:(q % 2 + 1) * 2 * TILE],
                               w1[:, e, k * 128:(k + 1) * 128], tokens).then_inc(h_made, 1)
                    if e > 0:
                        y = e - 1
                        pe.wait_ge(gelu_done, first + 1 + e * tiles)
                        if y % 4 == 0:
                            pe.wait_ge(y_added, 2 * E * i + 1)
                        for u in (0, 1):
                            for k in range(tiles):
                                ins = mm(ps[:, 4 * u + 2 + y // 4, (y % 4) * D:(y % 4 + 1) * D],
                                         HB[:, y % 2 * tiles + k, u * TILE:(u + 1) * TILE],
                                         w2[:, y * tiles + k, :], start=k == 0, stop=k == tiles - 1)
                            ins.then_inc(y_made, 1)

            def tail(i):
                for u in (0, 1):
                    pe.wait_ge(tail_copied, 2 * i + u + 1)
                    transposed(u, [PF[:, u, j, :] for j in range(4)], bank(u, 0)).then_inc(tail_turned, 1)
                for u in (0, 1):
                    pe.wait_ge(tail_ctx, 2 * i + u + 1)
                    transposed(u, [CN[:, u, :]], bank(u, 1)).then_inc(tail_ctxT, 1)
                for u in (0, 1):
                    pe.wait_ge(tail_ctxS, 2 * i + u + 1)
                    mm(bank(u, 2)[:, 0:D], CNT[:, u, :], XWO[:, :]).then_inc(tail_proj, 1)
                pe.wait_ge(tail_normed, i + 1)
                for u in (0, 1):
                    transposed(u, [XN[:, u, :]], bank(u, 3)).then_inc(tail_xT, 1)
                for u in (0, 1):
                    pe.wait_ge(tail_xnT, 2 * i + u + 1)
                    mm(bank(u, 0)[:, 0:E], XNT[:, u, :], GW).then_inc(tail_logits, 1)
                expert_bias(i, FB2)
                feed_forward(i, tail_ffn, F0 // 128, FW1, FW2, XNT[:, :, :].rearrange("p a b -> p (a b)"))

            def expert_bias(i, bias):
                for u in (0, 1):
                    pe.wait_ge(tail_coef, i + 1)
                    nc.tensor.transpose(bank(u, 1)[0:E, 0:TILE], coef[:, u, :], ident).then_inc(tail_coefT, 1)
                for u in (0, 1):
                    pe.wait_ge(tail_coefS, 2 * i + u + 1)
                    mm(bank(u, 3)[:, 0:D], coefT[0:E, u, :], bias[0:E, :]).then_inc(tail_b2, 1)
                pe.wait_ge(tail_x2b, 2 * i + 2)

            pe.wait_ge(load_middle_w, 144)
            with pe.Fori(0, N2) as i:
                tail(i)

            def mqa(i):
                pe.wait_ge(mqa_scaled, i + 1)
                for u in (0, 1):
                    transposed(u, [XN[:, u, :]], bank(u, 0)).then_inc(mqa_xT, 1)
                for u in (0, 1):
                    pe.wait_ge(mqa_xnT, 2 * i + u + 1)
                    mm(bank(u, 0), XNT[:, u, :], MWQ)
                    mm(bank(u, 1)[:, 0:2 * DH], XNT[:, u, :], MWKV).then_inc(mqa_qkv, 1)
                for u in (0, 1):
                    pe.wait_ge(mqa_qn, 2 * i + u + 1)
                    transposed(u, [T1[:, u, j * 128:(j + 1) * 128] for j in range(4)], bank(u, 2))
                    transposed(u, [T1[:, u, 512:640]], bank(u, 3)).then_inc(mqa_turned, 1)
                for u in (0, 1):
                    pe.wait_ge(mqa_qT, 2 * i + u + 1)
                    pe.wait_ge(mqa_kT, 2 * i + u + 1)
                    apart(pe)
                    for b in (0, 1):
                        for o in (0, 1):
                            rhs = T2[64 * o:64 * o + DH, u, 0:512].rearrange("p (j n) -> p j n", n=TILE)
                            ins = mm(bank(u, o)[HALF * b:HALF * (b + 1), 0:4 * HALF],
                                     T2[64 * o:64 * o + DH, u, 512 + HALF * b:512 + HALF * (b + 1)],
                                     rhs[:, :, HALF * b:HALF * (b + 1)])
                    ins.then_inc(mqa_scores, 1)
                for u in (0, 1):
                    pe.wait_ge(mqa_probs, 2 * i + u + 1)
                    pe.wait_ge(mqa_v, 2 * i + u + 1)
                    apart(pe)
                    for b in (0, 1):
                        for h in range(H1):
                            at = 256 * (h % 2) + HALF * (h // 2)
                            ins = mm(heads4(u, 1, 2)[HALF * b:HALF * (b + 1), h // 4, h % 4, :],
                                     T3[HALF * b:HALF * b + S, u, at:at + HALF],
                                     VM[HALF * b:HALF * b + S, u, 0, :])
                    ins.then_inc(mqa_pv, 1)
                for u in (0, 1):
                    pe.wait_ge(mqa_o, 2 * i + u + 1)
                    transposed(u, [T1[:, u, j * 128:(j + 1) * 128] for j in range(4)], bank(u, 3)).then_inc(mqa_oT, 1)
                for u in (0, 1):
                    pe.wait_ge(mqa_oS, 2 * i + u + 1)
                    for j in range(4):
                        ins = mm(bank(u, 0)[:, 0:D], T2[:, u, j * 128:(j + 1) * 128], MWO[:, j, :],
                                 start=j == 0, stop=j == 3)
                    ins.then_inc(mqa_proj, 1)

            with pe.Fori(0, N2) as i:
                mqa(i)

            def rope(i):
                pe.wait_ge(rope_scaled, i + 1)
                for u in (0, 1):
                    transposed(u, [XN[:, u, :], KX[:, u, :]], bank(u, 0)).then_inc(rope_xT, 1)
                for u in (0, 1):
                    pe.wait_ge(rope_xnT, 2 * i + u + 1)
                    for w, k in ((RWQ, 0), (RWQR, 2)):
                        for j in range(8):
                            ins = mm(bank(u, k, 2)[:, j * TILE:(j + 1) * TILE], w[:, j * 128:(j + 1) * 128], XNT[:, u, :])
                    ins.then_inc(rope_qproj, 1)
                for u in (0, 1):
                    pe.wait_ge(rope_parts, 4 * i + u + 1)
                    for w, k in ((RWK, 0), (RWKR, 2)):
                        for j in range(8):
                            ins = mm(bank(u, k, 2)[:, j * TILE:(j + 1) * TILE], w[:, j * 128:(j + 1) * 128], KXT[:, u, :])
                    ins.then_inc(rope_kproj, 1)
                for u in (0, 1):
                    pe.wait_ge(rope_parts, 4 * i + 2 + u + 1)
                    for k in (0, 1):
                        ins = mm(bank(u, k), KXT[:, u, :], RWV[:, k * 512:(k + 1) * 512])
                    ins.then_inc(rope_v_proj, 1)
                for u in (0, 1):
                    pe.wait_ge(rope_qT, 2 * i + u + 1)
                    pe.wait_ge(rope_kT, 2 * i + u + 1)
                    apart(pe)
                    for h in range(HEADS):
                        lo, at = 64 * (h % 2), (h // 2) * TILE
                        for b in (0, 1):
                            ins = mm(bank(u, 2 + h % 2)[HALF * b:HALF * (b + 1), h // 2 * HALF:(h // 2 + 1) * HALF],
                                     T3[lo:lo + DH, u, at + HALF * b:at + HALF * (b + 1)],
                                     T1[lo:lo + DH, u, at + HALF * b:at + HALF * (b + 1)])
                    ins.then_inc(rope_scores, 1)
                for u in (0, 1):
                    pe.wait_ge(rope_masked, 2 * i + u + 1)
                    pe.wait_ge(rope_v, 2 * i + u + 1)
                    apart(pe)
                    for b in (0, 1):
                        for h in range(HEADS):
                            ins = mm(heads4(u, 0, 4)[HALF * b:HALF * (b + 1), h // 4, h % 4, :],
                                     T2[HALF * b:HALF * b + S, u, 512 * (h % 2) + HALF * (h // 2):
                                        512 * (h % 2) + HALF * (h // 2 + 1)],
                                     VM[HALF * b:HALF * b + S, u, h, :])
                    ins.then_inc(rope_pv, 1)
                for u in (0, 1):
                    pe.wait_ge(rope_o, 2 * i + u + 1)
                    transposed(u, [T1[:, u, j * 128:(j + 1) * 128] for j in range(8)], bank(u, 0, 2)).then_inc(rope_oT, 1)
                for u in (0, 1):
                    pe.wait_ge(rope_oS, 2 * i + u + 1)
                    for j in range(8):
                        ins = mm(bank(u, 2)[:, 0:D], T3[:, u, j * 128:(j + 1) * 128], RWO[:, j, :],
                                 start=j == 0, stop=j == 7)
                    ins.then_inc(rope_out, 1)

            pe.wait_ge(load_late_w, 96)
            with pe.Fori(0, N2) as i:
                rope(i)

            def router(i):
                pe.wait_ge(tail_normed, N2 + i + 1)
                for u in (0, 1):
                    transposed(u, [XN[:, u, :]], bank(u, 0)).then_inc(tail_xT, 1)
                for u in (0, 1):
                    pe.wait_ge(tail_xnT, 2 * (N2 + i) + u + 1)
                    mm(bank(u, 1)[:, 0:E], XNT[:, u, :], LW).then_inc(tail_logits, 1)

            with pe.Fori(0, N2) as i:
                router(i)
            pe.wait_ge(moe_before, 1)
            mm(ps[:, 0, 0:PAIRS * E], CT[:, C_TRI:C_TRI + 128], PICK.rearrange("p a b -> p (a b)"), stop=False)
            mm(ps[:, 0, 0:PAIRS * E], CT[:, C_ONES:C_ONES + 128], BEFORE.rearrange("p a b -> p (a b)"), start=False)\
                .then_inc(moe_count, 1)
            pe.wait_ge(moe_kept_xT, PAIRS)
            with pe.Fori(0, N2) as i:
                expert_bias(N2 + i, LB2)
                feed_forward(i, last_ffn, F1 // 128, LW1, LW2, XNTA[:, bass.ds(2 * i, 2), :])

        @block.scalar
        def _(act):
            def copy(dst, src, **kw):
                return nc.scalar.activation(dst, src, ACT.Copy, **kw)

            def self_attention(i):
                for u in (0, 1):
                    act.wait_ge(attn_xT, 2 * i + u + 1)
                    copy(XNT[:, u, :], bank(u, 0)[:, 0:TILE]).then_inc(attn_xnT, 1)
                for u in (0, 1):
                    act.wait_ge(attn_q_proj, 2 * i + u + 1)
                    copy(qT[:, u].rearrange("p a b -> p (a b)"), bank(u, 0, 2)).then_inc(attn_q, 1)
                for u in (0, 1):
                    act.wait_ge(attn_v_proj, 2 * i + u + 1)
                    copy(V[:, u].rearrange("p a b -> p (a b)"), bank(u, 0, 2)).then_inc(attn_v, 1)
                for u in (0, 1):
                    act.wait_ge(attn_shifted, 2 * i + u + 1)
                    nc.scalar.activation(P[:, u, :, 0:S], P[:, u, :, 0:S], ACT.Exp, scale=DH ** -0.5)\
                        .then_inc(attn_expd, 1)
                for u in (0, 1):
                    act.wait_ge(attn_probsT, 2 * i + u + 1)
                    copy(PT[:, u].rearrange("p a b -> p (a b)"), bank(u, 0, 2)).then_inc(attn_pT, 1)
                for u in (0, 1):
                    act.wait_ge(attn_pv, 2 * i + u + 1)
                    copy(OT[:, u].rearrange("p a b -> p (a b)"), bank(u, 2, 2)).then_inc(attn_o, 1)
                for u in (0, 1):
                    act.wait_ge(attn_xT2, 2 * i + u + 1)
                    copy(XNT[:, u, :], bank(u, 1)[:, 0:TILE]).then_inc(attn_xnT2, 1)
                for u in (0, 1):
                    act.wait_ge(attn_qf, 2 * i + u + 1)
                    copy(q1[0:STACK, u], qf[0:STACK, u], scale=CT[0:STACK, C_MASK1:C_MASK1 + 1]).then_inc(attn_q1, 1)
                for u in (0, 1):
                    act.wait_ge(attn_r1, 2 * i + u + 1)
                    copy(q2[0:STACK, u], qf[0:STACK, u], scale=CT[0:STACK, C_MASK2:C_MASK2 + 1]).then_inc(attn_q2, 1)
                for u in (0, 1):
                    act.wait_ge(attn_r2, 2 * i + u + 1)
                    for b in (0, 1):
                        for h in (0, 1):
                            ins = nc.scalar.activation(QS[0:STACK, 4 * i + 2 * u + b, :, h * S:(h + 1) * S],
                                                       qf[0:STACK, u, :, HALF * b:HALF * b + S], ACT.Copy,
                                                       scale=CT[0:STACK, C_BLK + h:C_BLK + h + 1])
                    ins.then_inc(attn_qstack, 1)

            act.wait_ge(load_consts, 48)
            for counted in (cross_o, tail_gelu, last_gelu):
                act.sem_inc(counted, 1)
            with act.Fori(0, N2) as i:
                self_attention(i)

            def take_k(b, u, n):
                act.wait_ge(cross_k_proj, THIRDS * b + n + 1)
                bias = PC[:, P_BK:P_BK + 1]
                if not (isinstance(b, int) and b == 0):
                    act.wait_ge((cross_out0, cross_out1, cross_out2)[n], 16 * b)
                nc.scalar.activation(kp[:, n, 0, :], ps[:, 7, 0:KC], ACT.Identity, bias=bias)
                nc.scalar.activation(kf[:, n, :], ps[:, 7, 0:KC], ACT.Identity, bias=bias).then_inc(cross_kf, 1)

            def take_shift(b):
                act.wait_ge(cross_shift, b + 1)
                copy(QS[SHIFT:SHIFT + 1, b, :, :].rearrange("p (a h) q -> p a (h q)", a=2),
                     ps[SHIFT:SHIFT + 1, 5:7, 0:4 * XQ]).then_inc(cross_shifted, 1)

            def cross(b, u, t_, next_too=True, second_too=True):
                for kt in range(KT):
                    act.wait_ge(cross_scores, KT * b + kt + 1)
                    nc.scalar.activation(PX[kt % 2][0:KN].rearrange("p (a h) q -> p a (h q)", a=2),
                                         ps[0:KN, 2 * (kt % 2):2 * (kt % 2) + 2, 0:4 * XQ],
                                         ACT.Exp, scale=XD ** -0.5).then_inc(cross_probs, 1)
                    if second_too and kt % 4 == 3:
                        take_k(b + 2, u, kt // 4)
                    if next_too and kt == KT - 1:
                        take_shift(b + 1)
                act.wait_ge(cross_pv, KT * b + KT)
                copy(PO[:, t_, :, :, HALF * u:HALF * u + S],
                     ps[:, 4, 0:2 * XQ].rearrange("p (j h q) -> p j h q", j=2, h=2)).then_inc(cross_o, 1)

            for b in (0, 1):
                for n in range(THIRDS):
                    take_k(b, b, n)
            take_shift(0)
            with act.Fori(0, PAIRS - 1) as p:
                cross(2 * p, 0, p)
                cross(2 * p + 1, 1, p)
            cross(B - 2, 0, PAIRS - 1, second_too=False)
            cross(B - 1, 1, PAIRS - 1, next_too=False, second_too=False)

            def feed_forward(i, sig, tiles, bias):
                h_made, gelu_done, y_made, y_added = sig
                first = i * E * tiles
                for e in range(E):
                    act.wait_ge(y_made, 2 * E * i + 1 + 2 * max(e - 1, 0))
                    for k in range(tiles):
                        q = e * tiles + k
                        if q % 2 == 0:
                            act.wait_ge(h_made, first + q + 2)
                        nc.scalar.activation(HB[:, e % 2 * tiles + k, :],
                                             ps[:, (0, 1, 4, 5)[q // 2 % 4], (q % 2) * 2 * TILE:(q % 2 + 1) * 2 * TILE],
                                             ACT.Gelu, bias=PC[:, bias + q:bias + q + 1]).then_inc(gelu_done, 1)

            def take_coef(i):
                for u in (0, 1):
                    act.wait_ge(tail_coefT, 2 * i + u + 1)
                    copy(coefT[0:E, u, :], bank(u, 1)[0:E, 0:TILE]).then_inc(tail_coefS, 1)

            def tail(i):
                for u in (0, 1):
                    act.wait_ge(tail_ctxT, 2 * i + u + 1)
                    copy(CNT[:, u, :], bank(u, 1)[:, 0:TILE]).then_inc(tail_ctxS, 1)
                for u in (0, 1):
                    act.wait_ge(tail_xT, 2 * i + u + 1)
                    copy(XNT[:, u, :], bank(u, 3)[:, 0:TILE]).then_inc(tail_xnT, 1)
                act.wait_ge(tail_shifted, i + 1)
                nc.scalar.activation(sm[:, :, 8:16], sm[:, :, 0:8], ACT.Exp).then_inc(tail_expd, 1)
                take_coef(i)
                feed_forward(i, tail_ffn, F0 // 128, P_B1)

            with act.Fori(0, N2) as i:
                tail(i)

            def mqa(i):
                for u in (0, 1):
                    act.wait_ge(mqa_xT, 2 * i + u + 1)
                    copy(XNT[:, u, :], bank(u, 0)[:, 0:TILE]).then_inc(mqa_xnT, 1)
                for u in (0, 1):
                    act.wait_ge(mqa_qkv, 2 * i + u + 1)
                    nc.scalar.activation(T3[:, u, 0:512], bank(u, 0), ACT.Square, scale=16.0)
                    nc.scalar.activation(T3[:, u, 512:576], bank(u, 1)[:, 0:DH], ACT.Square).then_inc(mqa_sq, 1)
                    copy(VM[:, u, 0, 0:DH], bank(u, 1)[:, DH:2 * DH]).then_inc(mqa_v, 1)
                for u in (0, 1):
                    act.wait_ge(mqa_turned, 2 * i + u + 1)
                    copy(T2[:, u, 0:512], bank(u, 2)).then_inc(mqa_qT, 1)
                for u in (0, 1):
                    act.wait_ge(mqa_scores, 2 * i + u + 1)
                    nc.scalar.activation(T3[:, u, 0:512].rearrange("p (o n) -> p o n", o=2),
                                         bank(u, 0, 2).rearrange("p (o n) -> p o n", o=2)[:, :, 0:4 * HALF], ACT.Exp)\
                        .then_inc(mqa_probs, 1)
                for u in (0, 1):
                    act.wait_ge(mqa_oT, 2 * i + u + 1)
                    copy(T2[:, u, 0:512], bank(u, 3)).then_inc(mqa_oS, 1)

            with act.Fori(0, N2) as i:
                mqa(i)

            def rope(i):
                for u in (0, 1):
                    act.wait_ge(rope_xT, 2 * i + u + 1)
                    copy(XNT[:, u, :], bank(u, 0)[:, 0:TILE])
                    copy(KXT[:, u, :], bank(u, 0)[:, TILE:2 * TILE]).then_inc(rope_xnT, 1)
                for u in (0, 1):
                    act.wait_ge(rope_v_proj, 2 * i + u + 1)
                    copy(VM[:, u, :, 0:DH], bank(u, 0, 2).rearrange("p (h w) -> p h w", w=DH)).then_inc(rope_v, 1)
                for u in (0, 1):
                    act.wait_ge(rope_scores, 2 * i + u + 1)
                    nc.scalar.activation(T2[:, u, :], bank(u, 2, 2), ACT.Tanh, scale=DH ** -0.5 / GROK).then_inc(rope_tanh, 1)
                for u in (0, 1):
                    act.wait_ge(rope_tanh, 2 * i + u + 1)
                    nc.scalar.activation(T2[:, u, :], T2[:, u, :], ACT.Exp, scale=GROK).then_inc(rope_expd, 1)
                for u in (0, 1):
                    act.wait_ge(rope_oT, 2 * i + u + 1)
                    copy(T3[:, u, :], bank(u, 0, 2)).then_inc(rope_oS, 1)

            with act.Fori(0, N2) as i:
                rope(i)

            def router(i):
                for u in (0, 1):
                    act.wait_ge(tail_xT, 2 * (N2 + i) + u + 1)
                    copy(XNT[:, u, :], bank(u, 0)[:, 0:TILE]).then_inc(tail_xnT, 1)
                act.wait_ge(tail_shifted, N2 + i + 1)
                nc.scalar.activation(sm[:, :, 8:16], sm[:, :, 0:8], ACT.Exp).then_inc(tail_expd, 1)

            with act.Fori(0, N2) as i:
                router(i)
            with act.Fori(0, N2) as i:
                take_coef(N2 + i)
                feed_forward(i, last_ffn, F1 // 128, P_B1L)

        @block.gpsimd
        def _(pool):
            pool.wait_ge(load_consts, 48)

            def self_attention(i):
                ln_pool(pool, 2 * i)
                ln_pool(pool, 2 * i + 1)
                for part, made, left in ((q1, attn_q1, attn_r1), (q2, attn_q2, attn_r2)):
                    for u in (0, 1):
                        pool.wait_ge(made, 2 * i + u + 1)
                        nc.gpsimd.tensor_tensor(qf[0:STACK, u], qf[0:STACK, u], part[0:STACK, u], ALU.add)\
                            .then_inc(left, 1)

            with pool.Fori(0, N2) as i:
                self_attention(i)

            def split_k(b, n):
                at = THIRDS * b + n + 1
                pool.wait_ge(cross_kf, at)
                pool.wait_ge(cross_k3, at - 1)
                nc.gpsimd.tensor_tensor(kr, kf[:, n, :], kp[:, n, 0, :], ALU.subtract).then_inc(cross_r1, 1)
                nc.gpsimd.tensor_tensor(kp[:, n, 1, :], kf[:, n, :], kp[:, n, 0, :], ALU.subtract).then_inc(cross_k2, 1)
                pool.wait_ge(cross_r1, at)
                pool.wait_ge(cross_k2, at)
                nc.gpsimd.tensor_tensor(kp[:, n, 2, :], kr, kp[:, n, 1, :], ALU.subtract).then_inc(cross_k3, 1)

            for b in (0, 1):
                for n in range(THIRDS):
                    split_k(b, n)
            with pool.Fori(2, B) as b:
                for n in range(THIRDS):
                    split_k(b, n)

            def tail(i):
                for u in (0, 1):
                    if u == 0:
                        pool.wait_ge(ln_variance, LN_T + i)
                    nc.gpsimd.tensor_copy(PF[:, u].rearrange("p a b -> p (a b)"),
                                          PO[:, 2 * i + u].rearrange("p a b c -> p (a b c)")).then_inc(tail_copied, 1)
                ln_pool(pool, LN_T + i)

            pool.wait_ge(cross_o, B + 1)
            with pool.Fori(0, N2) as i:
                tail(i)

            def mqa(i):
                ln_pool(pool, LN_M + 3 * i)
                ln_pool(pool, LN_M + 3 * i + 1)
                pool.wait_ge(mqa_ss, i + 1)
                nc.gpsimd.tensor_tensor(sm[:, :, 16:25], sm[:, :, 0:9],
                                        CT[:, C_HALF:C_HALF + 18].rearrange("p (a b) -> p a b", a=2), ALU.pow)\
                    .then_inc(mqa_root, 1)
                ln_pool(pool, LN_M + 3 * i + 2)

            with pool.Fori(0, N2) as i:
                mqa(i)

            def rope(i):
                for k in range(3):
                    ln_pool(pool, LN_R + 3 * i + k)
                for into, other, k, done in ((T1, T2, 0, rope_qT), (T3, T4, 2, rope_kT)):
                    for u in (0, 1):
                        pool.wait_ge(rope_parts, 4 * i + k + u + 1)
                        nc.gpsimd.tensor_tensor(into[:, u, :], into[:, u, :], other[:, u, :], ALU.add).then_inc(done, 1)
                for u in (0, 1):
                    pool.wait_ge(rope_expd, 2 * i + u + 1)
                    nc.gpsimd.tensor_tensor(T2[:, u, :].rearrange("p (h n) -> p h n", n=HALF),
                                            T2[:, u, :].rearrange("p (h n) -> p h n", n=HALF),
                                            over(KEEP[:, 2 * i + u, :], HEADS), ALU.mult).then_inc(rope_masked, 1)

            with pool.Fori(0, N2) as i:
                rope(i)

            def router(i):
                ln_pool(pool, LN_F + i)
                for u in (0, 1):
                    pool.wait_ge(tail_xnT, 2 * (N2 + i) + u + 1)
                    nc.gpsimd.tensor_copy(XNTA[:, 2 * i + u, :], XNT[:, u, :]).then_inc(moe_kept_xT, 1)

            with pool.Fori(0, N2) as i:
                router(i)

        @block.vector
        def _(dve):
            dve.wait_ge(load_consts, 48)
            dve.wait_ge(load_tokens, 32)
            for y_added in (tail_acc, last_acc):
                dve.sem_inc(y_added, 1)
            nc.vector.tensor_copy(identb[:, :], ident).then_inc(attn_cleared, 1)
            nc.vector.memset(P[:, :, :, S:HALF], 0.0).then_inc(attn_cleared, 1)

            def tiles(ap, i):
                return [ap[:, 2 * i + u, :] for u in (0, 1)]

            def add_to_x(i, sig_in, sig_sum, sig_out, k, row):
                for u, xt in enumerate(tiles(X, i)):
                    dve.wait_ge(sig_in, 2 * i + u + 1)
                    nc.vector.tensor_tensor(xt, bank(u, k)[:, 0:D], xt, ALU.add).then_inc(sig_sum, 1)
                for u, xt in enumerate(tiles(X, i)):
                    dve.wait_ge(sig_sum, 2 * i + u + 1)
                    nc.vector.tensor_tensor(xt, xt, RW[:, row:row + D], ALU.add).then_inc(sig_out, 1)

            def self_attention(i):
                ln_vector(dve, 2 * i, tiles(X, i), XS, attn_normed)
                for u in (0, 1):
                    dve.wait_ge(attn_k_proj, 2 * i + u + 1)
                    nc.vector.tensor_copy(kT[:, u].rearrange("p a b -> p (a b)"), bank(u, 2, 2)).then_inc(attn_k, 1)
                for u in (0, 1):
                    dve.wait_ge(attn_scores, 2 * i + u + 1)
                    sc = bank(u, 2, 2).rearrange("p (o j n) -> p o j n", o=2, n=HALF)[:, :, :, 0:S]
                    best = sm[:, u, 0:HEADS].rearrange("p (o j) -> p o j", o=2)
                    nc.vector.tensor_reduce(best, sc, AX.X, ALU.max).then_inc(attn_top, 1)
                    dve.wait_ge(attn_top, 2 * i + u + 1)
                    nc.vector.tensor_tensor(P[:, u].rearrange("p (j o) n -> p o j n", o=2)[:, :, :, 0:S],
                                            sc, wide(best, S), ALU.subtract).then_inc(attn_shifted, 1)
                for u in (0, 1):
                    step = Steps(dve, attn_steps, 6 * i + 3 * u)
                    dve.wait_ge(attn_expd, 2 * i + u + 1)
                    step(nc.vector.tensor_reduce(sm[:, u, 16:32], P[:, u, :, 0:S], AX.X, ALU.add))
                    step(nc.vector.tensor_scalar(sm[:, u, 32:48], sm[:, u, 16:32], SAFE_EPS, None, ALU.add))
                    step(nc.vector.reciprocal(sm[:, u, 48:64], sm[:, u, 32:48]))
                    nc.vector.tensor_tensor(P[:, u, :, 0:S], P[:, u, :, 0:S], wide(sm[:, u, 48:64], S), ALU.mult)\
                        .then_inc(attn_probs, 1)
                add_to_x(i, attn_proj, attn_sum, attn_x1, 0, R_BO)
                dve.wait_ge(attn_x1, 2 * i + 2)
                ln_vector(dve, 2 * i + 1, tiles(X, i), XS, attn_normed2)
                for u in (0, 1):
                    dve.wait_ge(attn_stack, 2 * i + u + 1)
                    nc.vector.tensor_tensor(qf[0:STACK, u],
                                            bank(u, 2, 2)[0:STACK, :].rearrange("p (g n) -> p g n", n=TILE),
                                            wide(PC[0:STACK, P_BQ:P_BQ + XG], TILE), ALU.add).then_inc(attn_qf, 1)

            with dve.Fori(0, N2) as i:
                self_attention(i)

            dve.wait_ge(attn_qstack, PAIRS)
            for u in (0, 1):
                nc.vector.memset(KS[u][SHIFT:SHIFT + 1], 1.0)
                nc.vector.memset(VX[u], 1.0).then_inc(cross_cleared, 1)
            nc.vector.memset(PO[:, :, :, :, :], 1.0).then_inc(cross_cleared, 1)
            dve.wait_ge(cross_cleared, 3)

            def take_v(b, u, n):
                dve.wait_ge(cross_v_proj, THIRDS * b + n + 1)
                at = VX[u][0:KN, 4 * n:4 * n + 4, 0:XG * VW].rearrange("p k (h w) -> p k h w", w=XD + 1)
                for j in range(4):
                    ins = nc.vector.tensor_tensor(at[:, j, :, 0:XD],
                                                  ps[0:KN, 7, j * D:(j + 1) * D].rearrange("p (h w) -> p h w", w=XD),
                                                  RW[0:KN, R_BV:R_BV + D].rearrange("p (h w) -> p h w", w=XD), ALU.add)
                ins.then_inc(cross_v, 1)

            def maximum(b, q):
                dve.wait_ge(cross_smax, THIRDS * XG * b + q + 1)
                nc.vector.tensor_reduce(MX[0:XQ, q % XG, q // XG:q // XG + 1], ps[0:XQ, 5 + q % 2, 0:KC], AX.X, ALU.max)\
                    .then_inc(cross_top, 1)

            def shift(b):
                dve.wait_ge(cross_top, THIRDS * XG * (b + 1))
                nc.vector.tensor_reduce(CM[0:XQ, :], MX[0:XQ], AX.X, ALU.max).then_inc(cross_best, 1)
                dve.wait_ge(cross_best, b + 1)
                nc.vector.tensor_scalar(CB[0:XQ, :], CM[0:XQ, :], -1.0, None, ALU.mult).then_inc(cross_negated, 1)

            def cross(b, u, next_too=True):
                q = 0
                for kt in range(KT):
                    if not next_too:
                        continue
                    for _ in range((3, 3, 2, 3, 3, 2, 3, 3, 2, 0, 0, 0)[kt]):
                        maximum(b + 1, q)
                        q += 1
                    if kt % 4 == 0:
                        take_v(b + 1, 1 - u, kt // 4)
                if next_too:
                    shift(b + 1)

            for n in range(THIRDS):
                take_v(0, 0, n)
            for q in range(THIRDS * XG):
                maximum(0, q)
            shift(0)
            with dve.Fori(0, PAIRS - 1) as p:
                cross(2 * p, 0)
                cross(2 * p + 1, 1)
            cross(B - 2, 0)

            def add_experts(i, sig, xs):
                h_made, gelu_done, y_made, y_added = sig
                for e in range(E):
                    for u, xt in enumerate(xs):
                        if e % 4 == 0 and u == 0:
                            dve.wait_ge(y_made, 2 * E * i + 1 + 2 * (e + 4))
                        if e > 0:
                            dve.wait_ge(y_added, 2 * E * i + 1 + 2 * (e - 1) + u + 1)
                        nc.vector.scalar_tensor_tensor(xt, bank(u, 2 + e // 4)[:, (e % 4) * D:(e % 4 + 1) * D],
                                                       coef[:, u, e:e + 1], xt, ALU.mult, ALU.add).then_inc(y_added, 1)

            def add_bias(i, xs):
                for u, xt in enumerate(xs):
                    dve.wait_ge(tail_b2, 2 * i + u + 1)
                    nc.vector.tensor_tensor(xt, bank(u, 3)[:, 0:D], xt, ALU.add).then_inc(tail_x2b, 1)
                dve.wait_ge(tail_x2b, 2 * i + 2)

            tie = over(CT[:, C_TIE:C_TIE + E], 2)

            def pick(step, g_, top, won, hot):
                step(nc.vector.tensor_reduce(top, g_, AX.X, ALU.max))
                step(nc.vector.tensor_tensor(hot, g_, wide(top, E), ALU.is_equal))
                step(nc.vector.tensor_tensor(hot, hot, tie, ALU.mult))
                step(nc.vector.tensor_reduce(won, hot, AX.X, ALU.max))
                step(nc.vector.tensor_tensor(hot, hot, wide(won, E), ALU.is_equal))

            def gates(i, step, k, row, into):
                for u in (0, 1):
                    dve.wait_ge(tail_logits, 2 * i + u + 1)
                    step(nc.vector.tensor_tensor(sm[:, u, 0:8], bank(u, k)[:, 0:E], RW[:, row:row + E], ALU.add))
                step(nc.vector.tensor_reduce(sm[:, :, 16], sm[:, :, 0:8], AX.X, ALU.max))
                nc.vector.tensor_tensor(sm[:, :, 0:8], sm[:, :, 0:8], wide(sm[:, :, 16], E), ALU.subtract)\
                    .then_inc(tail_shifted, 1)
                dve.wait_ge(tail_expd, i + 1)
                step(nc.vector.tensor_reduce(sm[:, :, 17], sm[:, :, 8:16], AX.X, ALU.add))
                step(nc.vector.reciprocal(sm[:, :, 18], sm[:, :, 17]))
                step(nc.vector.tensor_tensor(into, sm[:, :, 8:16], wide(sm[:, :, 18], E), ALU.mult))

            def tail(i):
                for u in (0, 1):
                    dve.wait_ge(tail_turned, 2 * i + u + 1)
                    step = Steps(dve, tail_steps, 19 * i + 4 * u)
                    for j in (0, 1):
                        for h in (0, 1):
                            got = bank(u, 0).rearrange("p (j h g w) -> p j h g w", j=2, h=2, w=32)[:, j, h]
                            at = sm[:, u, 4 * (2 * j + h):4 * (2 * j + h) + 4]
                            step(nc.vector.reciprocal(at, got[:, :, h * (XD + 1) + XD]))
                    for j in (0, 1):
                        for h in (0, 1):
                            got = bank(u, 0).rearrange("p (j h g w) -> p j h g w", j=2, h=2, w=32)[:, j, h]
                            at = sm[:, u, 4 * (2 * j + h):4 * (2 * j + h) + 4]
                            ins = nc.vector.tensor_tensor(
                                CN[:, u].rearrange("p (j g h w) -> p j g h w", j=2, h=2, w=XD)[:, j, :, h, :],
                                got[:, :, h * (XD + 1):h * (XD + 1) + XD], wide(at, XD), ALU.mult)
                    ins.then_inc(tail_ctx, 1)
                add_to_x(i, tail_proj, tail_sum, tail_x2, 2, R_BO2)
                dve.wait_ge(tail_x2, 2 * i + 2)
                ln_vector(dve, LN_T + i, tiles(X, i), XS, tail_normed)
                step = Steps(dve, tail_steps, 19 * i + 8)
                gates(i, step, 0, R_BG, sm[:, :, 24:32])
                pick(step, sm[:, :, 24:32], sm[:, :, 19], sm[:, :, 20], sm[:, :, 32:40])
                nc.vector.tensor_tensor(coef[:, :, :], sm[:, :, 24:32], sm[:, :, 32:40], ALU.mult).then_inc(tail_coef, 1)
                assert step.n == 11
                add_bias(i, tiles(X, i))
                add_experts(i, tail_ffn, tiles(X, i))

            with dve.Fori(0, N2) as i:
                tail(i)

            dve.wait_ge(tail_acc, 2 * E * N2 + 1)
            nc.vector.memset(VM, 1.0).then_inc(mqa_cleared, 1)
            dve.wait_ge(mqa_cleared, 1)

            def mqa(i):
                ln_vector(dve, LN_M + 3 * i, tiles(X, i), XS, mqa_normed1)
                dve.wait_ge(mqa_normed1, i + 1)
                ln_vector(dve, LN_M + 3 * i + 1, XS, XS, mqa_normed)
                dve.wait_ge(mqa_normed, i + 1)
                nc.vector.tensor_tensor(XN[:, :, :], XN[:, :, :], over(RW[:, R_NG:R_NG + D], 2), ALU.mult).then_inc(mqa_scaled, 1)
                for u in (0, 1):
                    dve.wait_ge(mqa_sq, 2 * i + u + 1)
                    ins = nc.vector.tensor_reduce(sm[:, u, 0:9], T3[:, u, 0:576].rearrange("p (h w) -> p h w", w=DH),
                                                  AX.X, ALU.add)
                ins.then_inc(mqa_ss, 1)
                step = Steps(dve, mqa_steps, 4 * i)
                dve.wait_ge(mqa_root, i + 1)
                step(nc.vector.tensor_scalar(sm[:, :, 32:41], sm[:, :, 16:25], NORM_EPS, None, ALU.max))
                step(nc.vector.reciprocal(sm[:, :, 48:57], sm[:, :, 32:41]))
                for u in (0, 1):
                    dve.wait_ge(mqa_v, 2 * i + u + 1)
                    nc.vector.scalar_tensor_tensor(T1[:, u, 0:512].rearrange("p (h w) -> p h w", w=DH),
                                                   bank(u, 0).rearrange("p (h w) -> p h w", w=DH), 64.0,
                                                   wide(sm[:, u, 48:56], DH), ALU.mult, ALU.mult)
                    nc.vector.scalar_tensor_tensor(T1[:, u, 512:640].rearrange("p (h w) -> p h w", w=DH),
                                                   over(bank(u, 1)[:, 0:DH], 2), 4.0,
                                                   wide(sm[:, u, 56:57].broadcast_to([128, 2]), DH), ALU.mult, ALU.mult)\
                        .then_inc(mqa_qn, 1)
                for u in (0, 1):
                    dve.wait_ge(mqa_turned, 2 * i + u + 1)
                    nc.vector.tensor_copy(T2[:, u, 512:640], bank(u, 3)[:, 0:128]).then_inc(mqa_kT, 1)
                for u in (0, 1):
                    dve.wait_ge(mqa_pv, 2 * i + u + 1)
                    got = heads4(u, 1, 2)
                    den = sm[:, u, 0:8].rearrange("p (a h) -> p a h", a=2)
                    step2 = Steps(dve, mqa_steps, 4 * i + 2 + u)
                    step2(nc.vector.reciprocal(den, got[:, :, :, DH]))
                    nc.vector.tensor_tensor(T1[:, u, 0:512].rearrange("p (a h w) -> p a h w", a=2, w=DH),
                                            got[:, :, :, 0:DH], wide(den, DH), ALU.mult).then_inc(mqa_o, 1)
                dve.wait_ge(mqa_proj, 2 * i + 2)
                ln_vector(dve, LN_M + 3 * i + 2, [bank(u, 0)[:, 0:D] for u in (0, 1)], XS, mqa_normed2)
                dve.wait_ge(mqa_normed2, i + 1)
                nc.vector.tensor_tensor(XN[:, :, :], XN[:, :, :], over(RW[:, R_ONG:R_ONG + D], 2), ALU.mult).then_inc(mqa_outn, 1)
                dve.wait_ge(mqa_outn, i + 1)
                for u, xt in enumerate(tiles(X, i)):
                    ins = nc.vector.tensor_tensor(xt, xt, XN[:, u, :], ALU.add)
                ins.then_inc(mqa_sum, 1)

            with dve.Fori(0, N2) as i:
                mqa(i)

            dve.wait_ge(mqa_sum, N2)
            keep = Steps(dve, rope_keep, 0)
            keep(nc.vector.tensor_copy(MK, mask8[:, :]))
            keep(nc.vector.tensor_scalar(MK, MK, -1.0, 1.0, ALU.mult, ALU.add))
            for k in range(PAIRS):
                ins = nc.vector.tensor_scalar(KEEP[:, k, :], CT[:, C_CAUSAL:C_CAUSAL + HALF], MK[:, k:k + 1], None, ALU.mult)
            keep(ins)
            dve.wait_ge(load_context, 16)

            def rope(i):
                ln_vector(dve, LN_R + 3 * i, tiles(X, i), XS, rope_normed1)
                dve.wait_ge(rope_normed1, i + 1)
                ln_vector(dve, LN_R + 3 * i + 1, XS, XS, rope_normed)
                ln_vector(dve, LN_R + 3 * i + 2, tiles(C56, i), [KX[:, u, :] for u in (0, 1)], rope_knormed)
                step = Steps(dve, rope_steps, 5 * i)
                dve.wait_ge(rope_normed, i + 1)
                dve.wait_ge(rope_knormed, i + 1)
                for y in (XN[:, :, :], KX):
                    ins = nc.vector.tensor_tensor(y, y, over(RW[:, R_LG:R_LG + D], 2), ALU.mult)
                step(ins)
                nc.vector.tensor_tensor(XN[:, :, :], XN[:, :, :], over(RW[:, R_LB:R_LB + D], 2), ALU.add)
                nc.vector.tensor_tensor(KX, KX, over(RW[:, R_LB:R_LB + D], 2), ALU.add).then_inc(rope_scaled, 1)
                for made, into, other in ((rope_qproj, T1, T2), (rope_kproj, T3, T4)):
                    for u in (0, 1):
                        dve.wait_ge(made, 2 * i + u + 1)
                        for k, dst, table in ((0, into, C_COS), (2, other, C_SIN)):
                            ins = nc.vector.tensor_tensor(dst[:, u, :].rearrange("p (j n) -> p j n", n=TILE),
                                                          bank(u, k, 2).rearrange("p (j n) -> p j n", n=TILE),
                                                          over(CT[:, table:table + TILE], 8), ALU.mult)
                        ins.then_inc(rope_parts, 1)
                for u in (0, 1):
                    dve.wait_ge(rope_pv, 2 * i + u + 1)
                    got = heads4(u, 0, 4)
                    den = sm[:, u, 0:16].rearrange("p (a h) -> p a h", a=4)
                    step(nc.vector.reciprocal(den, got[:, :, :, DH]))
                    nc.vector.tensor_tensor(T1[:, u, :].rearrange("p (a h w) -> p a h w", a=4, w=DH),
                                            got[:, :, :, 0:DH], wide(den, DH), ALU.mult).then_inc(rope_o, 1)
                for u, xt in enumerate(tiles(X, i)):
                    dve.wait_ge(rope_out, 2 * i + u + 1)
                    step(nc.vector.tensor_tensor(xt, bank(u, 2)[:, 0:D], xt, ALU.add))
                assert step.n == 5

            with dve.Fori(0, N2) as i:
                rope(i)

            def router(i):
                ln_vector(dve, LN_F + i, tiles(X, i), XS, tail_normed)
                step = Steps(dve, moe_steps, 18 * i)
                gate, picked = GATE[:, bass.ds(2 * i, 2), :], PICK[:, bass.ds(2 * i, 2), :]
                ga, left, hot = sm[:, :, 24:32], sm[:, :, 32:40], sm[:, :, 40:48]
                gates(N2 + i, step, 1, R_RB, ga)
                pick(step, ga, sm[:, :, 19], sm[:, :, 20], hot)
                step(nc.vector.scalar_tensor_tensor(left, hot, -4.0, ga, ALU.mult, ALU.add))
                nc.vector.tensor_copy(picked, hot)
                pick(step, left, sm[:, :, 19], sm[:, :, 20], sm[:, :, 48:56])
                nc.vector.tensor_tensor(picked, sm[:, :, 48:56], hot, ALU.add)
                step(nc.vector.tensor_copy(gate, ga))
                assert step.n == 18, step.n

            with dve.Fori(0, N2) as i:
                router(i)

            step = Steps(dve, moe_before, 0)
            nc.vector.memset(BEFORE[:, 0, :], 0.0)
            nc.vector.tensor_copy(BEFORE[:, 1, :], PICK[:, 0, :]).then_inc(moe_wgt, 1)
            for k in range(2, PAIRS):
                dve.wait_ge(moe_wgt, k - 1)
                nc.vector.tensor_tensor(BEFORE[:, k, :], BEFORE[:, k - 1, :], PICK[:, k - 1, :], ALU.add).then_inc(moe_wgt, 1)
            dve.wait_ge(moe_wgt, PAIRS - 1)
            nc.vector.tensor_copy(sm[:, 0, 0:1], sm[:, 0, 1:2]).then_inc(moe_before, 1)
            dve.wait_ge(moe_count, 1)
            flat = lambda ap: ap.rearrange("p a b -> p (a b)")
            nc.vector.tensor_scalar(flat(WGT), ps[:, 0, 0:PAIRS * E], float(CAPACITY), None, ALU.is_le).then_inc(moe_weight, 1)
            dve.wait_ge(moe_weight, 1)
            nc.vector.tensor_tensor(flat(WGT), flat(WGT), flat(PICK), ALU.mult).then_inc(moe_weight, 1)
            dve.wait_ge(moe_weight, 2)
            nc.vector.tensor_tensor(flat(WGT), flat(WGT), flat(GATE), ALU.mult).then_inc(moe_weight, 1)
            dve.wait_ge(moe_weight, 3)

            with dve.Fori(0, N2) as i:
                dve.wait_ge(last_acc, 2 * E * i + 1)
                nc.vector.tensor_copy(coef, WGT[:, bass.ds(2 * i, 2), :]).then_inc(tail_coef, 1)
                dve.wait_ge(tail_coef, N2 + i + 1)
                add_bias(N2 + i, tiles(X, i))
                add_experts(i, last_ffn, tiles(X, i))


def tables():
    import numpy as np

    t = np.zeros((128, C_END), np.float32)
    t[:, C_IDENT:C_IDENT + 128] = np.eye(128)
    p = np.arange(128)
    inv = (np.float32(1.0) / np.float32(10000.0) ** (np.arange(0, DH, 2, dtype=np.float32) / np.float32(DH)))
    angle = (np.arange(HALF, dtype=np.float32)[None, :] * np.repeat(inv, 2)[:, None]).astype(np.float32)
    sign = np.where(np.arange(DH) % 2, 1.0, -1.0)[:, None]
    t[:, C_COS:C_COS + 128] = np.tile(np.cos(angle), (2, 2))
    t[:, C_SIN:C_SIN + 128] = np.tile(np.sin(angle) * sign, (2, 2))
    token, batch = p % HALF, p // HALF
    t[:, C_CAUSAL:C_CAUSAL + HALF] = (token[:, None] <= np.arange(HALF)[None, :]) & (token[:, None] < S)
    order = batch * HALF + token
    t[:, C_TRI:C_TRI + 128] = (order[:, None] <= order[None, :]) & (token[:, None] < S)
    t[:, C_ONES:C_ONES + 128] = (token[:, None] < S)
    t[:, C_TIE:C_TIE + E] = E - np.arange(E)
    row = np.arange(STACK)
    for h in (0, 1):
        t[:STACK, C_BLK + h] = (row // XD % 2) == h
    part = np.array(Q_PART)[row // (2 * XD)]
    t[:STACK, C_MASK1] = -(part >= 1).astype(np.float32)
    t[:STACK, C_MASK2] = -(part >= 2).astype(np.float32)
    t[:, C_MHALF:C_MHALF + 2] = -0.5
    t[:, C_HALF:C_HALF + 18] = 0.5
    return t


def kernel(**inputs):
    import numpy as np
    import concourse.bacc as bacc
    from concourse import mybir as mb
    from concourse.bass_utils import run_bass_kernel_spmd as run

    v = {k: np.asarray(a) for k, a in inputs.items()}

    def halves(z):
        w = np.zeros((B, HALF) + z.shape[2:], z.dtype)
        w[:, :S] = z
        w = w.reshape((PAIRS, TILE) + z.shape[2:])
        return np.ascontiguousarray(np.moveaxis(w, 0, 1))

    def by_row(z):
        return np.broadcast_to(z, (128,) + z.shape)

    def by_parity(w):
        return w.reshape(D, 8, 2, DH).transpose(0, 2, 1, 3).reshape(D, INNER)

    def stacked(w):
        w = w.reshape(w.shape[:-1] + (XG, 1, 2 * XD))
        w = np.repeat(w, len(K_PART), axis=-2)
        return w.reshape(w.shape[:-2] + (STACK,))

    def swapped(w):
        return w.reshape(D, INNER // 2, 2)[:, :, ::-1].reshape(D, INNER)

    rows = np.concatenate([by_row(v[n]) for n in (
        "L0_attn_bo", "L0_xattn_b_v", "L0_xattn_b_o", "L0_ffn_bg", "L1_attn_norm_g", "L1_attn_out_norm_g",
        "L1_xattn_ln_g", "L1_xattn_ln_b", "L1_ffn_router_b")], axis=1)
    bq = np.zeros((128, XG), np.float32)
    bq[:STACK] = stacked(v["L0_xattn_b_q"]).T
    cols = np.concatenate([v["L0_xattn_b_k"][:, None], bq,
                           v["L0_ffn_b1"].reshape(-1, 128).T, v["L1_ffn_b1"].reshape(-1, 128).T], axis=1)
    data = {
        "x": halves(v["x"]),
        "ctx_t": v["ctx_1024"].transpose(0, 2, 1),
        "ctx_first": halves(v["ctx_1024"][:, :S]),
        "mask": halves(v["mask_BxS2_bf0"][:, :S]),
        "consts": tables(), "rows": rows, "cols": cols,
        "a_wq": v["L0_attn_Wq"].T, "a_wk": v["L0_attn_Wk"].T, "a_wv": by_parity(v["L0_attn_Wv"].T),
        "a_wo": v["L0_attn_Wo"].T,
        "x_wq": stacked(v["L0_xattn_W_q"].T).reshape(D, XG * STACK),
        "x_wk": v["L0_xattn_W_k"].T, "x_wv": v["L0_xattn_W_v"].T, "x_wo": v["L0_xattn_W_o"].T,
        "g_w": v["L0_ffn_Wg"], "f_w1": v["L0_ffn_W1"], "f_w2": v["L0_ffn_W2"], "f_b2": v["L0_ffn_b2"],
        "m_wq": v["L1_attn_Wq"], "m_wkv": v["L1_attn_Wkv"], "m_wo": v["L1_attn_Wout"],
        "r_wq": v["L1_xattn_Wq"], "r_wqr": swapped(v["L1_xattn_Wq"]),
        "r_wk": v["L1_xattn_Wk"], "r_wkr": swapped(v["L1_xattn_Wk"]),
        "r_wv": v["L1_xattn_Wv"], "r_wo": v["L1_xattn_Wo"],
        "l_w": v["L1_ffn_router_w"], "l_w1": v["L1_ffn_w1"], "l_w2": v["L1_ffn_w2"], "l_b2": v["L1_ffn_b2"],
    }
    nc = bacc.Bacc("TRN2", target_bir_lowering=False, num_devices=1)
    arrays, args = {}, []
    for name, z in data.items():
        z = np.ascontiguousarray(z)
        arrays[f"in_{name}"] = z
        args.append(nc.dram_tensor(f"in_{name}", z.shape, mb.dt.from_np(z.dtype), kind="ExternalInput").ap())
    args.append(nc.dram_tensor("out", (B, S, D), mb.dt.float32, kind="ExternalOutput").ap())
    decoder_kernel(nc, *args)
    return run(nc, [arrays], core_ids=[0]).results[0]["out"]
```

```python
import math
from contextlib import ExitStack

import concourse.bass as bass
from concourse import mybir

B, S, D = 16, 56, 128
SK = 1500
PAIRS = B // 2
HALF = 64
TILE = 2 * HALF
HEADS, DH = 16, 64
INNER = HEADS * DH
XD = D // HEADS
XG = HEADS // 2
XQ = 2 * S
K_PART = (0, 1, 2, 0, 1, 0)
Q_PART = (0, 0, 0, 1, 1, 2)
K_RUNS = (3, 2, 1)
STACK = len(K_PART) * 2 * XD
SHIFT = STACK
KT, KN = 12, 125
THIRDS, KC = 3, 500
VW = 2 * (XD + 1)
VROW = XG * VW + 32 - VW
H1 = 8
E, F0, F1 = 8, 256, 512
CAPACITY = max(1, math.ceil(B * S / E * 1.25))
SLOTS = -(-CAPACITY // 32) * 32
CHUNKS = E * SLOTS // 128
K1 = F1 // 128
LN_EPS, SAFE_EPS, NORM_EPS = 1e-5, 1e-10, 1e-12
GROK = 30.0

FIRST = (2, 3, 3, 2, 2, 3, 3, 2, 2, 2, 0, 0)
assert sum(FIRST) == THIRDS * XG

C_IDENT, C_COS, C_SIN, C_CAUSAL, C_TRI, C_ONES = 0, 128, 256, 384, 448, 576
C_TIE, C_BLK, C_MASK1, C_MASK2, C_MHALF, C_HALF, C_PLACE = 704, 712, 714, 715, 716, 724, 742
C_END = C_PLACE + SLOTS
R_BO, R_BV, R_BO2, R_BG, R_NG, R_ONG, R_LG, R_LB, R_RB, R_END = 0, 128, 256, 384, 392, 520, 648, 776, 904, 912
P_BK, P_BQ, P_B1, P_B1L, P_END = 0, 1, 9, 25, 57


class Steps:

    def __init__(self, engine, semaphore, before):
        self.engine, self.semaphore, self.before, self.n = engine, semaphore, before, 0

    def __call__(self, instruction):
        instruction.then_inc(self.semaphore, 1)
        self.n += 1
        self.engine.wait_ge(self.semaphore, self.before + self.n)


def decoder_kernel(nc, x, ctx_t, ctx_first, mask, consts, rows, cols, a_wq, a_wk, a_wv, a_wo,
                   x_wq, x_wk, x_wv, x_wo, g_w, f_w1, f_w2, f_b2, m_wq, m_wkv, m_wo,
                   r_wq, r_wqr, r_wk, r_wkr, r_wv, r_wo, l_w, l_w1, l_w2, l_b2, out):
    f32, bf16 = mybir.dt.float32, mybir.dt.bfloat16
    ALU, ACT, AX = mybir.AluOpType, mybir.ActivationFunctionType, mybir.AxisListType

    ctx = ExitStack()
    with ctx:
        def sb(name, shape, dt=f32):
            return ctx.enter_context(nc.sbuf_tensor(name, shape, dt))

        def signals(stage, names):
            return [ctx.enter_context(nc.semaphore(f"{stage}_{n}")) for n in names.split()]

        X = sb("X", [128, PAIRS, D])
        CT = sb("CT", [128, C_END])
        RW = sb("RW", [128, R_END])
        PC = sb("PC", [128, P_END])
        ident = CT[:, C_IDENT:C_IDENT + 128]
        identb = sb("identb", [128, 128], bf16)
        st = sb("st", [128, 2, 6])
        mv = sb("mv", [128, 2, 2])
        vr = sb("vr", [128, 2])
        rstd = sb("rstd", [128, 2])
        XN = sb("XN", [128, 2, D])
        XNT = sb("XNT", [128, 2, TILE])
        QS = sb("QS", [SHIFT + 1, B, XG, XQ], bf16)
        PO = sb("PO", [128, PAIRS, 2, 2, TILE])
        sm = sb("sm", [128, 2, 64])
        XWK, XWV, XWO = sb("XWK", [128, D]), sb("XWV", [128, D]), sb("XWO", [128, D])
        FW1 = sb("FW1", [128, E, F0])
        FW2 = sb("FW2", [128, E * F0 // 128, D])
        ones = sb("ones", [125, XG * SK // 125], bf16)
        mask8 = sb("mask8", [128, PAIRS], mybir.dt.uint8)

        ARENA = 31400
        arena = sb("arena", [128, ARENA])
        place = [0]

        def take(*shape, dt=f32):
            n = math.prod(shape)
            words = n if dt == f32 else (n + 1) // 2
            part = arena[:, place[0]:place[0] + words]
            place[0] += words
            assert place[0] <= ARENA, place[0]
            if dt != f32:
                part = part.bitcast(dt)
            if len(shape) == 1:
                return part
            names = "abcd"[:len(shape)]
            return part.rearrange(f"p ({' '.join(names)}) -> p {' '.join(names)}",
                                  **{k: v for k, v in zip(names[1:], shape[1:])})

        WQ, WK, WV, WO = take(INNER), take(INNER), take(2, 8 * DH), take(8, D)
        WQS = take(XG, STACK)
        work = place[0]
        qT, kT, V = take(2, 8, TILE), take(2, 8, TILE), take(2, 2, 8 * DH)
        P, PT, OT = take(2, HEADS, HALF), take(2, 8, TILE), take(2, 8, TILE)
        q_work = place[0]
        XF = take(2, D)
        qf = take(2, XG, TILE)
        q1, q2 = take(2, XG, TILE, dt=bf16), take(2, XG, TILE, dt=bf16)
        attn_end = place[0]
        place[0] = work
        kf, kr, kp = take(THIRDS, KC), take(KC), take(THIRDS, 3, KC, dt=bf16)
        KS = [take(XG, SK, dt=bf16)]
        PX = [take(XG, XQ) for _ in range(2)]
        MX, CM, CB = take(XG, THIRDS), take(XG), take(XG, dt=bf16)
        assert place[0] <= q_work, (place[0], q_work)
        place[0] = q_work
        KS.append(take(XG, SK, dt=bf16))
        CX = [take(SK) for _ in range(2)]
        assert place[0] - 2 * SK >= attn_end
        VX = [take(KT, VROW) for _ in range(2)]
        place[0] = 0
        MWQ, MWKV, MWO = take(H1 * DH), take(2 * DH), take(4, D)
        GW, LW, FB2 = take(E), take(E), take(D)
        rope_w = place[0]
        RWQ, RWQR = take(INNER), take(INNER)
        assert place[0] <= work
        place[0] = work
        RWK, RWKR, RWV, RWO = take(INNER), take(INNER), take(INNER), take(8, D)
        rope_w_end = place[0]
        LW1, LW2 = take(E, F1), take(E * F1 // 128, D)
        coef, coefT = take(2, E), take(2, TILE)
        GATE, PICK, WGT = (take(PAIRS, E) for _ in range(3))
        XNTA = take(PAIRS, TILE)
        late = place[0]
        PF, CN, CNT = take(2, 4, TILE), take(2, D), take(2, TILE)
        HB = take(8, 2 * TILE)
        XA = take(PAIRS, D)
        LG, EX, HOT, LEFT, HOT2 = (take(PAIRS, E) for _ in range(5))
        SLOT, OUTS, PT2 = take(PAIRS, E), take(CHUNKS, D), take(2, CHUNKS, TILE)
        st8, mv8, var8, rstd8, TOP = take(PAIRS, 6), take(PAIRS, 2), take(PAIRS), take(PAIRS), take(3, PAIRS)
        place[0] = rope_w
        ONEHOT, XTS = take(2, E * SLOTS), take(E * SLOTS)
        HG, LB2 = take(2, K1, SLOTS), take(E, D)
        assert place[0] <= rope_w_end
        place[0] = late
        T1, T2, T3, T4 = (take(2, INNER) for _ in range(4))
        VM = take(2, HEADS, DH + 1)
        C56, KEEP, MK = take(PAIRS, D), take(PAIRS, HALF), take(PAIRS)
        KX, KXT = take(2, D), take(2, TILE)

        ps = ctx.enter_context(nc.psum_tensor("ps", [128, 8, 512], f32))
        k_scratch = nc.dram_tensor("k_parts", (2, 3, 128, SK), bf16, kind="Internal").ap()
        ones_scratch = nc.dram_tensor("k_ones", (1, XG, SK), bf16, kind="Internal").ap()

        (load_passed, load_consts, load_tokens, load_attn_w, load_rest_w, load_ones, load_middle_w, load_late_w, load_context) = signals(
            "load", "passed consts tokens attn_w rest_w ones middle_w late_w context")
        (ln_stats, ln_moments, ln_variance, ln_rstd) = signals(
            "ln", "stats moments variance rstd")
        (attn_cleared, attn_normed, attn_xT, attn_xnT, attn_q_proj, attn_k_proj, attn_v_proj, attn_q, attn_k,
         attn_v, attn_scores, attn_top, attn_shifted, attn_expd, attn_steps, attn_probs, attn_probsT, attn_pT,
         attn_pv, attn_o, attn_proj, attn_sum, attn_x1, attn_normed2, attn_xT2, attn_xnT2, attn_stack, attn_qf,
         attn_q1, attn_r1, attn_q2, attn_r2, attn_qstack) = signals(
            "attn", "cleared normed xT xnT q_proj k_proj v_proj q k v scores top shifted expd steps probs probsT pT pv o "
            "proj sum x1 normed2 xT2 xnT2 stack qf q1 r1 q2 r2 qstack")
        (cross_cleared, cross_ctx0, cross_ctx1, cross_k_proj, cross_kf, cross_r1, cross_k2, cross_k3, cross_out0,
         cross_out1, cross_out2, cross_in0, cross_in1, cross_in2, cross_v_proj, cross_v, cross_smax, cross_top,
         cross_best, cross_negated, cross_shift, cross_shifted, cross_scores, cross_probs, cross_pv, cross_o) = signals(
            "cross", "cleared ctx0 ctx1 k_proj kf r1 k2 k3 out0 out1 out2 in0 in1 in2 v_proj v smax top best negated shift "
            "shifted scores probs pv o")
        (tail_copied, tail_turned, tail_steps, tail_ctx, tail_ctxT, tail_ctxS, tail_proj, tail_sum, tail_x2,
         tail_normed, tail_xT, tail_xnT, tail_logits, tail_shifted, tail_expd, tail_coef, tail_coefT, tail_coefS,
         tail_b2, tail_x2b, tail_h, tail_gelu, tail_y, tail_acc) = signals(
            "tail", "copied turned steps ctx ctxT ctxS proj sum x2 normed xT xnT logits shifted expd coef coefT coefS b2 "
            "x2b h gelu y acc")
        (mqa_normed, mqa_scaled, mqa_xT, mqa_xnT, mqa_qkv, mqa_sq, mqa_ss, mqa_root,
         mqa_steps, mqa_qn, mqa_v, mqa_turned, mqa_qT, mqa_kT, mqa_scores, mqa_probs, mqa_pv, mqa_o, mqa_oT, mqa_oS,
         mqa_proj, mqa_normed2, mqa_outn, mqa_sum) = signals(
            "mqa", "normed scaled xT xnT qkv sq ss root steps qn v turned qT kT scores probs pv o oT oS "
            "proj normed2 outn sum")
        (rope_keep, rope_normed, rope_scaled, rope_xT, rope_xnT, rope_qproj, rope_kproj,
         rope_parts, rope_qT, rope_kT, rope_v_proj, rope_v, rope_scores, rope_tanh, rope_expd, rope_masked, rope_pv,
         rope_steps, rope_o, rope_oT, rope_oS, rope_out) = signals(
            "rope", "keep normed scaled xT xnT qproj kproj parts qT kT v_proj v scores tanh expd masked "
            "pv steps o oT oS out")
        (moe_steps, moe_normed, moe_xT, moe_xnT, moe_logits, moe_picked, moe_count) = signals(
            "moe", "steps normed xT xnT logits picked count")
        (last_onehot, last_read, last_copied, last_h, last_gelu, last_y, last_acc, last_out) = signals(
            "last", "onehot read copied h gelu y acc out")
        tail_ffn = (tail_h, tail_gelu, tail_y, tail_acc)

        block = ctx.enter_context(nc.Block())

        def mm(o, lhsT, rhs, start=True, stop=True, **kw):
            return nc.tensor.matmul(o, lhsT, rhs, start=start, stop=stop, **kw)

        def pieces(e):
            at, end = e * SLOTS, (e + 1) * SLOTS
            while at < end:
                row = at % 128
                n = min(end - at, (128 if row == 0 else 64 if row == 64 else 32))
                n = 1 << (n.bit_length() - 1)
                yield at // 128, row, n, at - e * SLOTS
                at += n

        def wide(ap, n):
            k = len(ap.shape)
            return ap.unsqueeze(k).broadcast_to([*ap.shape, n])

        def over(ap, n):
            return ap.unsqueeze(1).broadcast_to([ap.shape[0], n, *ap.shape[1:]])

        def bank(u, k, n=1):
            return ps[:, 4 * u + k:4 * u + k + n, :].rearrange("p a b -> p (a b)")

        def heads4(u, k, n):
            return ps[:, 4 * u + k:4 * u + k + n, 0:4 * (DH + 1)].rearrange("p a (h w) -> p a h w", w=DH + 1)

        def apart(engine):
            engine.sem_inc(load_passed, 1)

        def ln_vector(dve, nth, srcs, dsts, done):
            apart(dve)
            for u in (0, 1):
                ins = nc.vector.bn_stats(st[:, u, :], srcs[u])
            ins.then_inc(ln_stats, 1)
            dve.wait_ge(ln_stats, nth + 1)
            apart(dve)
            for u in (0, 1):
                ins = nc.vector.bn_aggr(mv[:, u, :], st[:, u, :])
            ins.then_inc(ln_moments, 1)
            dve.wait_ge(ln_moments, nth + 1)
            nc.vector.tensor_scalar(vr[:, :], mv[:, :, 1], LN_EPS, None, ALU.add).then_inc(ln_variance, 1)
            dve.wait_ge(ln_rstd, nth + 1)
            for u in (0, 1):
                ins = nc.vector.tensor_scalar(dsts[u], srcs[u], mv[:, u, 0:1], rstd[:, u:u + 1],
                                              ALU.subtract, ALU.mult)
            ins.then_inc(done, 1)

        def ln_pool(pool, nth):
            pool.wait_ge(ln_variance, nth + 1)
            nc.gpsimd.tensor_tensor(rstd[:, :], vr[:, :], CT[:, C_MHALF:C_MHALF + 2], ALU.pow)\
                .then_inc(ln_rstd, 1)

        N2 = PAIRS // 2
        LN_T = 2 * N2
        LN_M = LN_T + N2
        LN_R = LN_M + 3 * N2
        LN_F = LN_R + 3 * N2
        XS = [XN[:, u, :] for u in (0, 1)]

        @block.sync
        def _(sp):
            sp.dma_start(CT[:, :], consts).then_inc(load_consts, 16)
            sp.dma_start(X[:, :, :], x).then_inc(load_tokens, 16)
            for dst, src in ((WQ, a_wq), (WK, a_wk), (WV.rearrange("p a b -> p (a b)"), a_wv)):
                sp.dma_start(dst, src).then_inc(load_attn_w, 16)
            sp.wait_ge(attn_xT, 1)
            for dst, src in ((RW[:, :], rows), (PC[:, :], cols), (mask8[:, :], mask),
                             (WO, a_wo.rearrange("(j p) d -> p j d", p=128)),
                             (WQS.rearrange("p a b -> p (a b)"), x_wq), (XWK[:, :], x_wk), (XWV[:, :], x_wv),
                             (XWO[:, :], x_wo), (FW1[:, :, :], f_w1.rearrange("e p h -> p e h")),
                             (FW2[:, :, :], f_w2.rearrange("e (j p) d -> p (e j) d", p=128))):
                sp.dma_start(dst, src).then_inc(load_rest_w, 16)

            sp.wait_ge(cross_cleared, 1)
            sp.dma_start(ones_scratch.rearrange("o g n -> o (g n)").rearrange("o (p n) -> (o p) n", p=125), ones[:, :])\
                .then_inc(load_ones, 16)
            for u in (0, 1):
                sp.dma_start(CX[u], ctx_t[u, :, :]).then_inc((cross_ctx0, cross_ctx1)[u], 16)
            sp.wait_ge(attn_stack, PAIRS)
            sp.wait_ge(load_ones, 16)
            sp.dma_start(KS[0][SHIFT:SHIFT + 1], ones_scratch).then_inc(load_ones, 16)
            for dst, src in ((MWQ, m_wq), (MWKV, m_wkv), (MWO, m_wo.rearrange("(j p) d -> p j d", p=128)),
                             (GW, g_w), (LW, l_w), (FB2[0:E, :], f_b2), (RWQ, r_wq), (RWQR, r_wqr)):
                sp.dma_start(dst, src).then_inc(load_middle_w, 16)
            outs, ins_ = (cross_out0, cross_out1, cross_out2), (cross_in0, cross_in1, cross_in2)

            def load_ctx(b, u):
                sp.wait_ge(cross_v_proj, THIRDS * (b - 1))
                sp.wait_ge(cross_k_proj, THIRDS * (b - 1))
                apart(sp)
                sp.dma_start(CX[u], ctx_t[b, :, :]).then_inc((cross_ctx0, cross_ctx1)[u], 16)

            def stack_third(b, u, n, first=False):
                lo = n * KC
                sp.wait_ge(cross_k3, THIRDS * b + n + 1)
                apart(sp)
                sp.dma_start(k_scratch[u, :, :, lo:lo + KC].rearrange("c p n -> p c n"), kp[:, n])\
                    .then_inc(outs[n], 16)
                sp.wait_ge(outs[n], 16 * (b + 1))
                apart(sp)
                if not first:
                    sp.wait_ge(cross_scores, KT * (b - 2) + 4 * (n + 1))
                    apart(sp)
                at = 0
                for run in K_RUNS:
                    rows_ = 2 * XD * run
                    sp.dma_start(KS[u][at:at + rows_, :, lo:lo + KC],
                                 k_scratch[u, 0:run, :, lo:lo + KC].rearrange("c (r g) n -> (c r) g n", g=XG))\
                        .then_inc(ins_[n], 16)
                    at += rows_

            for n in range(THIRDS):
                stack_third(0, 0, n, True)
            sp.wait_ge(attn_qstack, PAIRS)
            sp.wait_ge(load_ones, 32)
            sp.dma_start(KS[1][SHIFT:SHIFT + 1], ones_scratch).then_inc(load_ones, 16)
            for n in range(THIRDS):
                stack_third(1, 1, n, True)

            def cross(b, u, more=True):
                for n in range(THIRDS):
                    if n == THIRDS - 1 and more:
                        load_ctx(b + 3, 1 - u)
                    stack_third(b + 2, u, n)

            load_ctx(2, 0)
            with sp.Fori(0, PAIRS - 2) as p:
                cross(2 * p, 0)
                cross(2 * p + 1, 1)
            cross(B - 4, 0)
            cross(B - 3, 1, more=False)

            sp.wait_ge(cross_o, B + 1)
            for dst, src in ((RWK, r_wk), (RWKR, r_wkr), (RWV, r_wv), (RWO, r_wo.rearrange("(j p) d -> p j d", p=128)),
                             (LW1, l_w1.rearrange("e p h -> p e h")),
                             (LW2, l_w2.rearrange("e (j p) d -> p (e j) d", p=128))):
                sp.dma_start(dst, src).then_inc(load_late_w, 16)
            sp.wait_ge(tail_acc, 2 * E * N2 + 1)
            sp.dma_start(C56, ctx_first).then_inc(load_context, 16)
            sp.wait_ge(moe_normed, 1)
            sp.dma_start(LB2.rearrange("p a b -> p (a b)"), l_b2).then_inc(load_late_w, 16)

            with sp.Fori(0, N2) as i:
                sp.wait_ge(last_acc, E + 2 * i + 2)
                apart(sp)
                for b in (0, 1):
                    sp.dma_start(out.rearrange("(t b) s d -> b s t d", b=2)[b, :, 2 * i:2 * i + 2, :] if isinstance(i, int)
                                 else out.rearrange("(t b) s d -> b s t d", b=2)[b, :, bass.ds(2 * i, 2), :],
                                 X[HALF * b:HALF * b + S, bass.ds(2 * i, 2), :]).then_inc(last_out, 16)
            sp.wait_ge(last_out, 16 * 2 * N2)

        @block.tensor
        def _(pe):
            pe.wait_ge(load_consts, 16)
            pe.sem_inc(tail_y, 1)

            def transposed(u, srcs, dst):
                for j, src in enumerate(srcs):
                    ins = nc.tensor.transpose(dst[:, j * TILE:(j + 1) * TILE], src, ident)
                return ins

            def self_attention(i):
                pe.wait_ge(attn_normed, i + 1)
                for u in (0, 1):
                    transposed(u, [XF[:, u, :]], bank(u, 0)).then_inc(attn_xT, 1)
                pe.wait_ge(load_attn_w, 48)
                for u in (0, 1):
                    pe.wait_ge(attn_xnT, 2 * i + u + 1)
                    for j in range(8):
                        ins = mm(bank(u, 0, 2)[:, j * TILE:(j + 1) * TILE], WQ[:, j * 128:(j + 1) * 128], XNT[:, u, :])
                    ins.then_inc(attn_q_proj, 1)
                    pe.wait_ge(attn_qf, 2 * i + u + 1)
                    apart(pe)
                    for j in range(8):
                        ins = mm(bank(u, 2, 2)[:, j * TILE:(j + 1) * TILE], WK[:, j * 128:(j + 1) * 128], XNT[:, u, :])
                    ins.then_inc(attn_k_proj, 1)
                for u in (0, 1):
                    pe.wait_ge(attn_q, 2 * i + u + 1)
                    for b in (0, 1):
                        for o in (0, 1):
                            ins = mm(ps[HALF * o:HALF * (o + 1), 4 * u + b, :],
                                     XNT[:, u, HALF * b:HALF * (b + 1)], WV[:, o, :])
                    ins.then_inc(attn_v_proj, 1)
                for u in (0, 1):
                    pe.wait_ge(attn_k, 2 * i + u + 1)
                    apart(pe)
                    for h in range(HEADS):
                        lo = 64 * (h % 2)
                        for b in (0, 1):
                            ins = mm(bank(u, 2 + h % 2)[HALF * b:HALF * (b + 1), h // 2 * HALF:h // 2 * HALF + S],
                                     qT[lo:lo + DH, u, h // 2, HALF * b:HALF * (b + 1)],
                                     kT[lo:lo + DH, u, h // 2, HALF * b:HALF * b + S])
                    ins.then_inc(attn_scores, 1)
                for u in (0, 1):
                    pe.wait_ge(attn_v, 2 * i + u + 1)
                    pe.wait_ge(attn_probs, 2 * i + u + 1)
                    transposed(u, [P[:, u, 2 * j:2 * j + 2, :].rearrange("p a b -> p (a b)") for j in range(8)],
                               bank(u, 0, 2)).then_inc(attn_probsT, 1)
                for u in (0, 1):
                    pe.wait_ge(attn_pT, 2 * i + u + 1)
                    apart(pe)
                    for h in range(HEADS):
                        lo, j = 64 * (h % 2), h // 2
                        for b in (0, 1):
                            at = j * TILE + HALF * b
                            ins = mm(bank(u, 2, 2)[lo:lo + DH, at:at + HALF],
                                     V[lo:lo + S, u, b, j * DH:(j + 1) * DH],
                                     PT[lo:lo + S, u, j, HALF * b:HALF * (b + 1)])
                    ins.then_inc(attn_pv, 1)
                pe.wait_ge(load_rest_w, 160)
                for u in (0, 1):
                    pe.wait_ge(attn_o, 2 * i + u + 1)
                    for j in range(8):
                        ins = mm(bank(u, 0)[:, 0:D], OT[:, u, j, :], WO[:, j, :], start=j == 0, stop=j == 7)
                    ins.then_inc(attn_proj, 1)
                pe.wait_ge(attn_normed2, i + 1)
                for u in (0, 1):
                    transposed(u, [XN[:, u, :]], bank(u, 1)).then_inc(attn_xT2, 1)
                for u in (0, 1):
                    pe.wait_ge(attn_xnT2, 2 * i + u + 1)
                    for n in range(XG):
                        ins = mm(bank(u, 2, 2)[0:STACK, n * TILE:(n + 1) * TILE], WQS[:, n, :], XNT[:, u, :])
                    ins.then_inc(attn_stack, 1)

            with pe.Fori(0, N2) as i:
                self_attention(i)

            ins_ = (cross_in0, cross_in1, cross_in2)

            def project_k(turn, u, n):
                pe.wait_ge((cross_ctx0, cross_ctx1)[u], 16 * (turn + 1))
                mm(ps[:, 7, 0:KC], XWK[:, :], CX[u][:, n * KC:(n + 1) * KC]).then_inc(cross_k_proj, 1)

            def project_v(b, u, n):
                for j in range(4):
                    kt = 4 * n + j
                    ins = mm(ps[0:KN, 7, j * D:(j + 1) * D], CX[u][:, kt * KN:(kt + 1) * KN], XWV[:, :])
                ins.then_inc(cross_v_proj, 1)

            def first_scores(b, u, q):
                n, h = q // XG, q % XG
                if h == 0:
                    pe.wait_ge(ins_[n], 16 * len(K_RUNS) * (b + 1))
                if not (isinstance(b, int) and b == 0 and q < 2):
                    pe.wait_ge(cross_top, THIRDS * XG * b + q - 1)
                mm(ps[0:XQ, 5 + q % 2, 0:KC], QS[0:STACK, b, h, :], KS[u][0:STACK, h, n * KC:(n + 1) * KC])\
                    .then_inc(cross_smax, 1)

            def shift_row(b):
                pe.wait_ge(cross_negated, b + 1)
                for h in range(XG):
                    ins = mm(ps[SHIFT:SHIFT + 1, 5 + h // 4, (h % 4) * XQ:(h % 4 + 1) * XQ],
                             CB[0:XQ, h:h + 1], identb[0:XQ, 0:XQ])
                ins.then_inc(cross_shift, 1)

            def scores(b, u, kt):
                if kt == 0:
                    pe.wait_ge(cross_shifted, b + 1)
                for h in range(XG):
                    ins = mm(ps[0:KN, 2 * (kt % 2) + h // 4, (h % 4) * XQ:(h % 4 + 1) * XQ],
                             KS[u][0:SHIFT + 1, h, kt * KN:(kt + 1) * KN], QS[0:SHIFT + 1, b, h, :])
                ins.then_inc(cross_scores, 1)

            def outputs(b, u, kt):
                pe.wait_ge(cross_probs, KT * b + kt + 1)
                if kt in (0, 4):
                    pe.wait_ge(cross_v, THIRDS * b + (2 if kt == 0 else 3))
                if kt == 0:
                    pe.wait_ge(cross_o, b + 1)
                for h in range(XG):
                    ins = mm(ps[32 * (h % 4):32 * (h % 4) + 32, 4, (h // 4) * XQ:(h // 4 + 1) * XQ],
                             VX[u][0:KN, kt, h * VW:h * VW + 32], PX[kt % 2][0:KN, h, :],
                             start=kt == 0 and h < 4, stop=kt == KT - 1, skip_group_check=True)
                ins.then_inc(cross_pv, 1)

            def cross(turn, u, next_too=True, second_too=True):
                b = 2 * turn + u
                q = 0
                for kt in range(KT):
                    if kt > 0:
                        scores(b, u, kt)
                    for k in range(FIRST[kt]) if next_too else ():
                        first_scores(b + 1, 1 - u, q)
                        q += 1
                        if k == FIRST[kt] - 2:
                            break
                    if next_too and kt % 4 == 1:
                        pe.wait_ge(cross_kf, THIRDS * (b + 2) + (kt // 4 if second_too else 0))
                        project_v(b + 1, 1 - u, kt // 4)
                    if second_too and kt % 4 == 3:
                        pe.wait_ge(cross_v, THIRDS * (b + 1) + kt // 4 + 1)
                        project_k(turn + 1, u, kt // 4)
                    if kt > 0:
                        outputs(b, u, kt - 1)
                    if next_too and FIRST[kt]:
                        first_scores(b + 1, 1 - u, q)
                        q += 1
                    if next_too and kt == KT - 2:
                        shift_row(b + 1)
                if next_too:
                    pe.wait_ge(load_ones, 48)
                    scores(b + 1, 1 - u, 0)
                outputs(b, u, KT - 1)

            pe.wait_ge(attn_qf, PAIRS + 2)
            for n in range(THIRDS):
                if n:
                    pe.wait_ge(cross_kf, n)
                project_k(0, 0, n)
            for n in range(THIRDS):
                pe.wait_ge(cross_kf, THIRDS + n)
                if n:
                    pe.wait_ge(cross_v, n)
                project_v(0, 0, n)
                pe.wait_ge(cross_v, n + 1)
                project_k(0, 1, n)
            pe.wait_ge(attn_qstack, PAIRS)
            for q in range(THIRDS * XG):
                first_scores(0, 0, q)
            shift_row(0)
            pe.wait_ge(load_ones, 32)
            scores(0, 0, 0)
            with pe.Fori(0, PAIRS - 1) as p:
                cross(p, 0)
                cross(p, 1)
            cross(PAIRS - 1, 0, second_too=False)
            cross(PAIRS - 1, 1, next_too=False, second_too=False)

            HBANK = (0, 1, 4, 5)

            def feed_forward(i, sig, tiles, w1, w2, tokens):
                h_made, gelu_done, y_made, y_added = sig
                first = i * E * tiles
                for e in range(E + 1):
                    if e < E:
                        for k in range(tiles):
                            q = e * tiles + k
                            if q % 2 == 0:
                                pe.wait_ge(gelu_done, first + 1 + max(q - 6, 0))
                            mm(ps[:, HBANK[q // 2 % 4], (q % 2) * 2 * TILE:(q % 2 + 1) * 2 * TILE],
                               w1[:, e, k * 128:(k + 1) * 128], tokens).then_inc(h_made, 1)
                    if e > 0:
                        y = e - 1
                        pe.wait_ge(gelu_done, first + 1 + e * tiles)
                        if y % 4 == 0:
                            pe.wait_ge(y_added, 2 * E * i + 1)
                        for u in (0, 1):
                            for k in range(tiles):
                                ins = mm(ps[:, 4 * u + 2 + y // 4, (y % 4) * D:(y % 4 + 1) * D],
                                         HB[:, y % 2 * tiles + k, u * TILE:(u + 1) * TILE],
                                         w2[:, y * tiles + k, :], start=k == 0, stop=k == tiles - 1)
                            ins.then_inc(y_made, 1)

            def tail(i):
                for u in (0, 1):
                    pe.wait_ge(tail_copied, 2 * i + u + 1)
                    transposed(u, [PF[:, u, j, :] for j in range(4)], bank(u, 0)).then_inc(tail_turned, 1)
                for u in (0, 1):
                    pe.wait_ge(tail_ctx, 2 * i + u + 1)
                    transposed(u, [CN[:, u, :]], bank(u, 1)).then_inc(tail_ctxT, 1)
                for u in (0, 1):
                    pe.wait_ge(tail_ctxS, 2 * i + u + 1)
                    mm(bank(u, 2)[:, 0:D], CNT[:, u, :], XWO[:, :]).then_inc(tail_proj, 1)
                pe.wait_ge(tail_normed, i + 1)
                for u in (0, 1):
                    transposed(u, [XN[:, u, :]], bank(u, 3)).then_inc(tail_xT, 1)
                for u in (0, 1):
                    pe.wait_ge(tail_xnT, 2 * i + u + 1)
                    mm(bank(u, 0)[:, 0:E], XNT[:, u, :], GW).then_inc(tail_logits, 1)
                expert_bias(i, FB2)
                feed_forward(i, tail_ffn, F0 // 128, FW1, FW2, XNT[:, :, :].rearrange("p a b -> p (a b)"))

            def expert_bias(i, bias):
                for u in (0, 1):
                    pe.wait_ge(tail_coef, i + 1)
                    nc.tensor.transpose(bank(u, 1)[0:E, 0:TILE], coef[:, u, :], ident).then_inc(tail_coefT, 1)
                for u in (0, 1):
                    pe.wait_ge(tail_coefS, 2 * i + u + 1)
                    mm(bank(u, 3)[:, 0:D], coefT[0:E, u, :], bias[0:E, :]).then_inc(tail_b2, 1)
                pe.wait_ge(tail_x2b, 2 * i + 2)

            pe.wait_ge(load_middle_w, 128)
            with pe.Fori(0, N2) as i:
                tail(i)

            def mqa(i):
                pe.wait_ge(mqa_scaled, i + 1)
                for u in (0, 1):
                    transposed(u, [KX[:, u, :]], bank(u, 3)).then_inc(mqa_xT, 1)
                pe.wait_ge(mqa_normed2, i + 1)
                apart(pe)
                for u in (0, 1):
                    pe.wait_ge(mqa_xnT, 2 * i + u + 1)
                    mm(bank(u, 0), XNT[:, u, :], MWQ)
                    mm(bank(u, 1)[:, 0:2 * DH], XNT[:, u, :], MWKV).then_inc(mqa_qkv, 1)
                for u in (0, 1):
                    pe.wait_ge(mqa_qn, 2 * i + u + 1)
                    transposed(u, [T1[:, u, j * 128:(j + 1) * 128] for j in range(4)], bank(u, 2))
                    transposed(u, [T1[:, u, 512:640]], bank(u, 3)).then_inc(mqa_turned, 1)
                for u in (0, 1):
                    pe.wait_ge(mqa_qT, 2 * i + u + 1)
                    pe.wait_ge(mqa_kT, 2 * i + u + 1)
                    apart(pe)
                    for b in (0, 1):
                        for o in (0, 1):
                            rhs = T2[64 * o:64 * o + DH, u, 0:512].rearrange("p (j n) -> p j n", n=TILE)
                            ins = mm(bank(u, o)[HALF * b:HALF * (b + 1), 0:4 * HALF],
                                     T2[64 * o:64 * o + DH, u, 512 + HALF * b:512 + HALF * (b + 1)],
                                     rhs[:, :, HALF * b:HALF * (b + 1)])
                    ins.then_inc(mqa_scores, 1)
                for u in (0, 1):
                    pe.wait_ge(mqa_probs, 2 * i + u + 1)
                    pe.wait_ge(mqa_v, 2 * i + u + 1)
                    apart(pe)
                    for b in (0, 1):
                        for h in range(H1):
                            at = 256 * (h % 2) + HALF * (h // 2)
                            ins = mm(heads4(u, 1, 2)[HALF * b:HALF * (b + 1), h // 4, h % 4, :],
                                     T3[HALF * b:HALF * b + S, u, at:at + HALF],
                                     VM[HALF * b:HALF * b + S, u, 0, :])
                    ins.then_inc(mqa_pv, 1)
                for u in (0, 1):
                    pe.wait_ge(mqa_o, 2 * i + u + 1)
                    transposed(u, [T1[:, u, j * 128:(j + 1) * 128] for j in range(4)], bank(u, 3)).then_inc(mqa_oT, 1)
                for u in (0, 1):
                    pe.wait_ge(mqa_oS, 2 * i + u + 1)
                    for j in range(4):
                        ins = mm(bank(u, 0)[:, 0:D], T2[:, u, j * 128:(j + 1) * 128], MWO[:, j, :],
                                 start=j == 0, stop=j == 3)
                    ins.then_inc(mqa_proj, 1)

            pe.wait_ge(tail_acc, 2 * E * N2 + 1)
            with pe.Fori(0, N2) as i:
                mqa(i)

            def rope(i):
                pe.wait_ge(rope_scaled, i + 1)
                for u in (0, 1):
                    transposed(u, [XN[:, u, :], KX[:, u, :]], bank(u, 0)).then_inc(rope_xT, 1)
                pe.wait_ge(rope_steps, 5 * i + 1)
                apart(pe)
                for u in (0, 1):
                    pe.wait_ge(rope_xnT, 2 * i + u + 1)
                    for w, k in ((RWQ, 0), (RWQR, 2)):
                        for j in range(8):
                            ins = mm(bank(u, k, 2)[:, j * TILE:(j + 1) * TILE], w[:, j * 128:(j + 1) * 128], XNT[:, u, :])
                    ins.then_inc(rope_qproj, 1)
                for u in (0, 1):
                    pe.wait_ge(rope_parts, 4 * i + u + 1)
                    for w, k in ((RWK, 0), (RWKR, 2)):
                        for j in range(8):
                            ins = mm(bank(u, k, 2)[:, j * TILE:(j + 1) * TILE], w[:, j * 128:(j + 1) * 128], KXT[:, u, :])
                    ins.then_inc(rope_kproj, 1)
                for u in (0, 1):
                    pe.wait_ge(rope_parts, 4 * i + 2 + u + 1)
                    for k in (0, 1):
                        ins = mm(bank(u, k), KXT[:, u, :], RWV[:, k * 512:(k + 1) * 512])
                    ins.then_inc(rope_v_proj, 1)
                for u in (0, 1):
                    pe.wait_ge(rope_qT, 2 * i + u + 1)
                    pe.wait_ge(rope_kT, 2 * i + u + 1)
                    apart(pe)
                    for h in range(HEADS):
                        lo, at = 64 * (h % 2), (h // 2) * TILE
                        for b in (0, 1):
                            ins = mm(bank(u, 2 + h % 2)[HALF * b:HALF * (b + 1), h // 2 * HALF:(h // 2 + 1) * HALF],
                                     T3[lo:lo + DH, u, at + HALF * b:at + HALF * (b + 1)],
                                     T1[lo:lo + DH, u, at + HALF * b:at + HALF * (b + 1)])
                    ins.then_inc(rope_scores, 1)
                for u in (0, 1):
                    pe.wait_ge(rope_masked, 2 * i + u + 1)
                    pe.wait_ge(rope_v, 2 * i + u + 1)
                    apart(pe)
                    for b in (0, 1):
                        for h in range(HEADS):
                            ins = mm(heads4(u, 0, 4)[HALF * b:HALF * (b + 1), h // 4, h % 4, :],
                                     T2[HALF * b:HALF * b + S, u, 512 * (h % 2) + HALF * (h // 2):
                                        512 * (h % 2) + HALF * (h // 2 + 1)],
                                     VM[HALF * b:HALF * b + S, u, h, :])
                    ins.then_inc(rope_pv, 1)
                for u in (0, 1):
                    pe.wait_ge(rope_o, 2 * i + u + 1)
                    transposed(u, [T1[:, u, j * 128:(j + 1) * 128] for j in range(8)], bank(u, 0, 2)).then_inc(rope_oT, 1)
                for u in (0, 1):
                    pe.wait_ge(rope_oS, 2 * i + u + 1)
                    for j in range(8):
                        ins = mm(bank(u, 2)[:, 0:D], T3[:, u, j * 128:(j + 1) * 128], RWO[:, j, :],
                                 start=j == 0, stop=j == 7)
                    ins.then_inc(rope_out, 1)

            pe.wait_ge(mqa_normed2, N2 + 1)
            pe.wait_ge(load_late_w, 96)
            with pe.Fori(0, N2) as i:
                rope(i)

            for k in (0, 1):
                pe.wait_ge(moe_normed, k + 1)
                transposed(k, [XA[:, 4 * k + j, :] for j in range(4)], bank(k, 0)).then_inc(moe_xT, 1)
            for k in (0, 1):
                pe.wait_ge(moe_xnT, k + 1)
                for t in range(4 * k, 4 * k + 4):
                    ins = mm(ps[:, 1, t * E:(t + 1) * E], XNTA[:, t, :], LW)
            ins.then_inc(moe_logits, 1)
            pe.wait_ge(moe_picked, 1)
            mm(ps[:, 2, 0:PAIRS * E], CT[:, C_TRI:C_TRI + 128], PICK.rearrange("p a b -> p (a b)"), stop=False)
            for t in range(PAIRS - 1):
                ins = mm(ps[:, 2, (t + 1) * E:PAIRS * E], CT[:, C_ONES:C_ONES + 128],
                         over(PICK[:, t, :], PAIRS - 1 - t), start=False, stop=t == PAIRS - 2)
            ins.then_inc(moe_count, 1)

            for t in range(PAIRS):
                pe.wait_ge(last_onehot, t + 1)
                for at in range(0, E * SLOTS, 512):
                    n = min(512, E * SLOTS - at)
                    ins = mm(ps[:, at // 512, 0:n], XA[:, t, :], ONEHOT[:, t % 2, at:at + n], start=t == 0, stop=t == PAIRS - 1)
                ins.then_inc(last_read, 1)
            pe.wait_ge(last_copied, 3)
            for e in range(E + 1):
                if e < E:
                    if e >= 2:
                        pe.wait_ge(last_gelu, K1 * (e - 1))
                    for k in range(K1):
                        mm(ps[:, 4 + 2 * (e % 2) + k // 2, k % 2 * SLOTS:(k % 2 + 1) * SLOTS],
                           LW1[:, e, k * 128:(k + 1) * 128], XTS[:, e * SLOTS:(e + 1) * SLOTS]).then_inc(last_h, 1)
                if e > 0:
                    y = e - 1
                    pe.wait_ge(last_gelu, K1 * e)
                    if y >= 3:
                        pe.wait_ge(last_acc, y - 2)
                    for j, (chunk, row, n, first) in enumerate(pieces(y)):
                        for k in range(K1):
                            ins = mm(ps[row:row + n, y % 3, j * D:(j + 1) * D], HG[:, y % 2, k, first:first + n],
                                     LW2[:, y * K1 + k, :], start=k == 0, stop=k == K1 - 1)
                    ins.then_inc(last_y, 1)
            pe.wait_ge(last_acc, E)

            def bring_back(i):
                for u in (0, 1):
                    pe.wait_ge(last_onehot, PAIRS + 4 * i + 2 * u + 2)
                    pe.wait_ge(last_copied, 3 + 2 * i + u - 1)
                    transposed(u, [ONEHOT[:, u, c * 128:(c + 1) * 128] for c in range(CHUNKS)], bank(u, 0, 3))\
                        .then_inc(last_read, 1)
                for u in (0, 1):
                    pe.wait_ge(last_copied, 3 + 2 * i + u + 1)
                    pe.wait_ge(last_acc, E + 2 * i + u - 1)
                    for c in range(CHUNKS):
                        ins = mm(bank(u, 3)[:, 0:D], PT2[:, u, c, :], OUTS[:, c, :], start=c == 0, stop=c == CHUNKS - 1)
                    ins.then_inc(last_y, 1)

            with pe.Fori(0, N2) as i:
                bring_back(i)

        @block.scalar
        def _(act):
            def copy(dst, src, **kw):
                return nc.scalar.activation(dst, src, ACT.Copy, **kw)

            def first_parts(i):
                for u in (0, 1):
                    act.wait_ge(attn_qf, 2 * i + u + 3)
                    copy(q1[0:STACK, u], qf[0:STACK, u], scale=CT[0:STACK, C_MASK1:C_MASK1 + 1]).then_inc(attn_q1, 1)

            def second_parts(i):
                for u in (0, 1):
                    act.wait_ge(attn_r1, 2 * i + u + 1)
                    copy(q2[0:STACK, u], qf[0:STACK, u], scale=CT[0:STACK, C_MASK2:C_MASK2 + 1]).then_inc(attn_q2, 1)

            def stacks(i):
                for u in (0, 1):
                    act.wait_ge(attn_r2, 2 * i + u + 1)
                    for b in (0, 1):
                        for h in (0, 1):
                            ins = nc.scalar.activation(QS[0:STACK, 4 * i + 2 * u + b, :, h * S:(h + 1) * S],
                                                       qf[0:STACK, u, :, HALF * b:HALF * b + S], ACT.Copy,
                                                       scale=CT[0:STACK, C_BLK + h:C_BLK + h + 1])
                    ins.then_inc(attn_qstack, 1)

            def self_attention(i, first=False):
                for u in (0, 1):
                    act.wait_ge(attn_xT, 2 * i + u + 1)
                    copy(XNT[:, u, :], bank(u, 0)[:, 0:TILE]).then_inc(attn_xnT, 1)
                if not first:
                    first_parts(i - 1)
                for u in (0, 1):
                    act.wait_ge(attn_q_proj, 2 * i + u + 1)
                    copy(qT[:, u].rearrange("p a b -> p (a b)"), bank(u, 0, 2)).then_inc(attn_q, 1)
                if not first:
                    second_parts(i - 1)
                for u in (0, 1):
                    act.wait_ge(attn_v_proj, 2 * i + u + 1)
                    copy(V[:, u].rearrange("p a b -> p (a b)"), bank(u, 0, 2)).then_inc(attn_v, 1)
                if not first:
                    stacks(i - 1)
                for u in (0, 1):
                    act.wait_ge(attn_shifted, 2 * i + u + 1)
                    nc.scalar.activation(P[:, u, :, 0:S], P[:, u, :, 0:S], ACT.Exp, scale=DH ** -0.5)\
                        .then_inc(attn_expd, 1)
                for u in (0, 1):
                    act.wait_ge(attn_probsT, 2 * i + u + 1)
                    copy(PT[:, u].rearrange("p a b -> p (a b)"), bank(u, 0, 2)).then_inc(attn_pT, 1)
                for u in (0, 1):
                    act.wait_ge(attn_pv, 2 * i + u + 1)
                    copy(OT[:, u].rearrange("p a b -> p (a b)"), bank(u, 2, 2)).then_inc(attn_o, 1)
                for u in (0, 1):
                    act.wait_ge(attn_xT2, 2 * i + u + 1)
                    copy(XNT[:, u, :], bank(u, 1)[:, 0:TILE]).then_inc(attn_xnT2, 1)
            act.wait_ge(load_consts, 16)
            for counted in (cross_o, tail_gelu):
                act.sem_inc(counted, 1)
            self_attention(0, True)
            with act.Fori(1, N2) as i:
                self_attention(i)

            def take_k(b, u, n):
                act.wait_ge(cross_k_proj, THIRDS * b + n + 1)
                bias = PC[:, P_BK:P_BK + 1]
                if not (isinstance(b, int) and b == 0):
                    act.wait_ge((cross_out0, cross_out1, cross_out2)[n], 16 * b)
                nc.scalar.activation(kp[:, n, 0, :], ps[:, 7, 0:KC], ACT.Identity, bias=bias)
                nc.scalar.activation(kf[:, n, :], ps[:, 7, 0:KC], ACT.Identity, bias=bias).then_inc(cross_kf, 1)

            def take_shift(b):
                act.wait_ge(cross_shift, b + 1)
                copy(QS[SHIFT:SHIFT + 1, b, :, :].rearrange("p (a h) q -> p a (h q)", a=2),
                     ps[SHIFT:SHIFT + 1, 5:7, 0:4 * XQ]).then_inc(cross_shifted, 1)

            def exponentials(b, kt):
                act.wait_ge(cross_scores, KT * b + kt + 1)
                nc.scalar.activation(PX[kt % 2][0:KN].rearrange("p (a h) q -> p a (h q)", a=2),
                                     ps[0:KN, 2 * (kt % 2):2 * (kt % 2) + 2, 0:4 * XQ],
                                     ACT.Exp, scale=XD ** -0.5).then_inc(cross_probs, 1)

            def cross(b, u, t_, next_too=True, second_too=True):
                for kt in range(KT):
                    if kt > 0:
                        exponentials(b, kt)
                    if second_too and kt % 4 == 3:
                        take_k(b + 2, u, kt // 4)
                    if next_too and kt == KT - 2:
                        take_shift(b + 1)
                if next_too:
                    exponentials(b + 1, 0)
                act.wait_ge(cross_pv, KT * b + KT)
                copy(PO[:, t_, :, :, HALF * u:HALF * u + S],
                     ps[:, 4, 0:2 * XQ].rearrange("p (j h q) -> p j h q", j=2, h=2)).then_inc(cross_o, 1)

            take_k(0, 0, 0)
            first_parts(N2 - 1)
            take_k(0, 0, 1)
            second_parts(N2 - 1)
            take_k(0, 0, 2)
            stacks(N2 - 1)
            for n in range(THIRDS):
                take_k(1, 1, n)
            act.wait_ge(cross_cleared, 4)
            take_shift(0)
            exponentials(0, 0)
            with act.Fori(0, PAIRS - 1) as p:
                cross(2 * p, 0, p)
                cross(2 * p + 1, 1, p)
            cross(B - 2, 0, PAIRS - 1, second_too=False)
            cross(B - 1, 1, PAIRS - 1, next_too=False, second_too=False)

            def feed_forward(i, sig, tiles, bias):
                h_made, gelu_done, y_made, y_added = sig
                first = i * E * tiles
                for e in range(E):
                    act.wait_ge(y_made, 2 * E * i + 1 + 2 * max(e - 1, 0))
                    for k in range(tiles):
                        q = e * tiles + k
                        if q % 2 == 0:
                            act.wait_ge(h_made, first + q + 2)
                        nc.scalar.activation(HB[:, e % 2 * tiles + k, :],
                                             ps[:, (0, 1, 4, 5)[q // 2 % 4], (q % 2) * 2 * TILE:(q % 2 + 1) * 2 * TILE],
                                             ACT.Gelu, bias=PC[:, bias + q:bias + q + 1]).then_inc(gelu_done, 1)

            def take_coef(i):
                for u in (0, 1):
                    act.wait_ge(tail_coefT, 2 * i + u + 1)
                    copy(coefT[0:E, u, :], bank(u, 1)[0:E, 0:TILE]).then_inc(tail_coefS, 1)

            def tail(i):
                for u in (0, 1):
                    act.wait_ge(tail_ctxT, 2 * i + u + 1)
                    copy(CNT[:, u, :], bank(u, 1)[:, 0:TILE]).then_inc(tail_ctxS, 1)
                for u in (0, 1):
                    act.wait_ge(tail_xT, 2 * i + u + 1)
                    copy(XNT[:, u, :], bank(u, 3)[:, 0:TILE]).then_inc(tail_xnT, 1)
                act.wait_ge(tail_shifted, i + 1)
                nc.scalar.activation(sm[:, :, 8:16], sm[:, :, 0:8], ACT.Exp).then_inc(tail_expd, 1)
                take_coef(i)
                feed_forward(i, tail_ffn, F0 // 128, P_B1)

            with act.Fori(0, N2) as i:
                tail(i)

            def mqa(i):
                for u in (0, 1):
                    act.wait_ge(mqa_xT, 2 * i + u + 1)
                    copy(XNT[:, u, :], bank(u, 3)[:, 0:TILE]).then_inc(mqa_xnT, 1)
                for u in (0, 1):
                    act.wait_ge(mqa_qkv, 2 * i + u + 1)
                    nc.scalar.activation(T3[:, u, 0:512], bank(u, 0), ACT.Square, scale=16.0)
                    nc.scalar.activation(T3[:, u, 512:576], bank(u, 1)[:, 0:DH], ACT.Square).then_inc(mqa_sq, 1)
                    copy(VM[:, u, 0, 0:DH], bank(u, 1)[:, DH:2 * DH]).then_inc(mqa_v, 1)
                for u in (0, 1):
                    act.wait_ge(mqa_turned, 2 * i + u + 1)
                    copy(T2[:, u, 0:512], bank(u, 2)).then_inc(mqa_qT, 1)
                for u in (0, 1):
                    act.wait_ge(mqa_scores, 2 * i + u + 1)
                    nc.scalar.activation(T3[:, u, 0:512].rearrange("p (o n) -> p o n", o=2),
                                         bank(u, 0, 2).rearrange("p (o n) -> p o n", o=2)[:, :, 0:4 * HALF], ACT.Exp)\
                        .then_inc(mqa_probs, 1)
                for u in (0, 1):
                    act.wait_ge(mqa_oT, 2 * i + u + 1)
                    copy(T2[:, u, 0:512], bank(u, 3)).then_inc(mqa_oS, 1)

            with act.Fori(0, N2) as i:
                mqa(i)

            def rope(i):
                for u in (0, 1):
                    act.wait_ge(rope_xT, 2 * i + u + 1)
                    copy(XNT[:, u, :], bank(u, 0)[:, 0:TILE])
                    copy(KXT[:, u, :], bank(u, 0)[:, TILE:2 * TILE]).then_inc(rope_xnT, 1)
                for u in (0, 1):
                    act.wait_ge(rope_v_proj, 2 * i + u + 1)
                    copy(VM[:, u, :, 0:DH], bank(u, 0, 2).rearrange("p (h w) -> p h w", w=DH)).then_inc(rope_v, 1)
                for u in (0, 1):
                    act.wait_ge(rope_scores, 2 * i + u + 1)
                    nc.scalar.activation(T2[:, u, :], bank(u, 2, 2), ACT.Tanh, scale=DH ** -0.5 / GROK).then_inc(rope_tanh, 1)
                for u in (0, 1):
                    act.wait_ge(rope_tanh, 2 * i + u + 1)
                    nc.scalar.activation(T2[:, u, :], T2[:, u, :], ACT.Exp, scale=GROK).then_inc(rope_expd, 1)
                for u in (0, 1):
                    act.wait_ge(rope_oT, 2 * i + u + 1)
                    copy(T3[:, u, :], bank(u, 0, 2)).then_inc(rope_oS, 1)

            with act.Fori(0, N2) as i:
                rope(i)

            for k in (0, 1):
                act.wait_ge(moe_xT, k + 1)
                copy(XNTA[:, 4 * k:4 * k + 4, :].rearrange("p a b -> p (a b)"), bank(k, 0)).then_inc(moe_xnT, 1)
            act.wait_ge(tail_shifted, N2 + 1)
            nc.scalar.activation(EX, LG, ACT.Exp).then_inc(tail_expd, 1)

            act.wait_ge(last_read, PAIRS)
            for at in range(0, E * SLOTS, 512):
                n = min(512, E * SLOTS - at)
                copy(XTS[:, at:at + n], ps[:, at // 512, 0:n]).then_inc(last_copied, 1)
            for e in range(E):
                if e >= 2:
                    act.wait_ge(last_y, e - 1)
                for k in range(K1):
                    if k % 2 == 0:
                        act.wait_ge(last_h, K1 * e + k + 2)
                    nc.scalar.activation(HG[:, e % 2, k, :], ps[:, 4 + 2 * (e % 2) + k // 2, k % 2 * SLOTS:(k % 2 + 1) * SLOTS],
                                         ACT.Gelu, bias=PC[:, P_B1L + K1 * e + k:P_B1L + K1 * e + k + 1]).then_inc(last_gelu, 1)
            with act.Fori(0, N2) as i:
                for u in (0, 1):
                    act.wait_ge(last_read, PAIRS + 2 * i + u + 1)
                    copy(PT2[:, u].rearrange("p c n -> p (c n)"), bank(u, 0, 3)[:, 0:E * SLOTS]).then_inc(last_copied, 1)

        @block.gpsimd
        def _(pool):
            nc.gpsimd.memset(ones[:, :], 1.0).then_inc(cross_cleared, 1)
            for u in (0, 1):
                nc.gpsimd.memset(VX[u], 1.0).then_inc(cross_cleared, 1)
            nc.gpsimd.memset(PO[:, :, :, :, :], 1.0).then_inc(cross_cleared, 1)
            pool.wait_ge(load_consts, 16)

            def self_attention(i, last=False):
                if not last:
                    ln_pool(pool, 2 * i + 1)
                ln_pool(pool, 2 * i + (1 if last else 2))
                for part, made, left in ((q1, attn_q1, attn_r1), (q2, attn_q2, attn_r2)):
                    for u in (0, 1):
                        pool.wait_ge(made, 2 * i + u + 1)
                        nc.gpsimd.tensor_tensor(qf[0:STACK, u], qf[0:STACK, u], part[0:STACK, u], ALU.add)\
                            .then_inc(left, 1)

            ln_pool(pool, 0)
            with pool.Fori(0, N2 - 1) as i:
                self_attention(i)
            self_attention(N2 - 1, True)

            def split_k(b, n):
                at = THIRDS * b + n + 1
                pool.wait_ge(cross_kf, at)
                pool.wait_ge(cross_k3, at - 1)
                nc.gpsimd.tensor_tensor(kr, kf[:, n, :], kp[:, n, 0, :], ALU.subtract).then_inc(cross_r1, 1)
                nc.gpsimd.tensor_tensor(kp[:, n, 1, :], kf[:, n, :], kp[:, n, 0, :], ALU.subtract).then_inc(cross_k2, 1)
                pool.wait_ge(cross_r1, at)
                pool.wait_ge(cross_k2, at)
                nc.gpsimd.tensor_tensor(kp[:, n, 2, :], kr, kp[:, n, 1, :], ALU.subtract).then_inc(cross_k3, 1)

            for b in (0, 1):
                for n in range(THIRDS):
                    split_k(b, n)
            with pool.Fori(2, B) as b:
                for n in range(THIRDS):
                    split_k(b, n)

            def tail(i):
                for u in (0, 1):
                    if u == 0:
                        pool.wait_ge(ln_variance, LN_T + i)
                    nc.gpsimd.tensor_copy(PF[:, u].rearrange("p a b -> p (a b)"),
                                          PO[:, 2 * i + u].rearrange("p a b c -> p (a b c)")).then_inc(tail_copied, 1)
                ln_pool(pool, LN_T + i)

            pool.wait_ge(cross_o, B + 1)
            with pool.Fori(0, N2) as i:
                tail(i)

            def mqa(i, last=False):
                pool.wait_ge(mqa_ss, i + 1)
                nc.gpsimd.tensor_tensor(sm[:, :, 16:25], sm[:, :, 0:9],
                                        CT[:, C_HALF:C_HALF + 18].rearrange("p (a b) -> p a b", a=2), ALU.pow)\
                    .then_inc(mqa_root, 1)
                for k in range(4 if last else 3):
                    ln_pool(pool, LN_M + 3 * i + 2 + k)

            for k in (0, 1):
                ln_pool(pool, LN_M + k)
            with pool.Fori(0, N2 - 1) as i:
                mqa(i)
            mqa(N2 - 1, True)

            def rope(i, last=False):
                for into, other, k, done in ((T1, T2, 0, rope_qT), (T3, T4, 2, rope_kT)):
                    for u in (0, 1):
                        pool.wait_ge(rope_parts, 4 * i + k + u + 1)
                        nc.gpsimd.tensor_tensor(into[:, u, :], into[:, u, :], other[:, u, :], ALU.add).then_inc(done, 1)
                if not last:
                    for k in range(3):
                        ln_pool(pool, LN_R + 3 * i + 3 + k)
                for u in (0, 1):
                    pool.wait_ge(rope_expd, 2 * i + u + 1)
                    nc.gpsimd.tensor_tensor(T2[:, u, :].rearrange("p (h n) -> p h n", n=HALF),
                                            T2[:, u, :].rearrange("p (h n) -> p h n", n=HALF),
                                            over(KEEP[:, 2 * i + u, :], HEADS), ALU.mult).then_inc(rope_masked, 1)

            with pool.Fori(0, N2 - 1) as i:
                rope(i)
            rope(N2 - 1, True)

            pool.wait_ge(ln_variance, LN_F + 1)
            nc.gpsimd.tensor_tensor(rstd8, var8, CT[:, C_MHALF:C_MHALF + PAIRS], ALU.pow).then_inc(ln_rstd, 1)

        @block.vector
        def _(dve):
            dve.wait_ge(load_tokens, 16)
            dve.wait_ge(load_consts, 16)
            dve.sem_inc(tail_acc, 1)
            nc.vector.tensor_copy(identb[:, :], ident).then_inc(attn_cleared, 1)
            nc.vector.memset(P[:, :, :, S:HALF], 0.0).then_inc(attn_cleared, 1)

            def tiles(ap, i):
                return [ap[:, 2 * i + u, :] for u in (0, 1)]

            def add_to_x(i, sig_in, sig_sum, sig_out, k, row):
                for u, xt in enumerate(tiles(X, i)):
                    dve.wait_ge(sig_in, 2 * i + u + 1)
                    nc.vector.tensor_tensor(xt, bank(u, k)[:, 0:D], xt, ALU.add).then_inc(sig_sum, 1)
                for u, xt in enumerate(tiles(X, i)):
                    dve.wait_ge(sig_sum, 2 * i + u + 1)
                    nc.vector.tensor_tensor(xt, xt, RW[:, row:row + D], ALU.add).then_inc(sig_out, 1)

            def self_attention(i, last=False):
                for u in (0, 1):
                    dve.wait_ge(attn_k_proj, 2 * i + u + 1)
                    nc.vector.tensor_copy(kT[:, u].rearrange("p a b -> p (a b)"), bank(u, 2, 2)).then_inc(attn_k, 1)
                for u in (0, 1):
                    dve.wait_ge(attn_scores, 2 * i + u + 1)
                    sc = bank(u, 2, 2).rearrange("p (o j n) -> p o j n", o=2, n=HALF)[:, :, :, 0:S]
                    best = sm[:, u, 0:HEADS].rearrange("p (o j) -> p o j", o=2)
                    nc.vector.tensor_reduce(best, sc, AX.X, ALU.max).then_inc(attn_top, 1)
                    dve.wait_ge(attn_top, 2 * i + u + 1)
                    nc.vector.tensor_tensor(P[:, u].rearrange("p (j o) n -> p o j n", o=2)[:, :, :, 0:S],
                                            sc, wide(best, S), ALU.subtract).then_inc(attn_shifted, 1)
                if not last:
                    ln_vector(dve, 2 * i + 1, tiles(X, i + 1), XFS, attn_normed)
                for u in (0, 1):
                    step = Steps(dve, attn_steps, 6 * i + 3 * u)
                    dve.wait_ge(attn_expd, 2 * i + u + 1)
                    step(nc.vector.tensor_reduce(sm[:, u, 16:32], P[:, u, :, 0:S], AX.X, ALU.add))
                    step(nc.vector.tensor_scalar(sm[:, u, 32:48], sm[:, u, 16:32], SAFE_EPS, None, ALU.add))
                    step(nc.vector.reciprocal(sm[:, u, 48:64], sm[:, u, 32:48]))
                    nc.vector.tensor_tensor(P[:, u, :, 0:S], P[:, u, :, 0:S], wide(sm[:, u, 48:64], S), ALU.mult)\
                        .then_inc(attn_probs, 1)
                add_to_x(i, attn_proj, attn_sum, attn_x1, 0, R_BO)
                dve.wait_ge(attn_x1, 2 * i + 2)
                ln_vector(dve, 2 * i + (1 if last else 2), tiles(X, i), XS, attn_normed2)
                for u in (0, 1):
                    dve.wait_ge(attn_stack, 2 * i + u + 1)
                    nc.vector.tensor_tensor(qf[0:STACK, u],
                                            bank(u, 2, 2)[0:STACK, :].rearrange("p (g n) -> p g n", n=TILE),
                                            wide(PC[0:STACK, P_BQ:P_BQ + XG], TILE), ALU.add).then_inc(attn_qf, 1)

            XFS = [XF[:, u, :] for u in (0, 1)]
            dve.sem_inc(attn_qf, 2)
            dve.sem_inc(mqa_normed2, 1)
            ln_vector(dve, 0, tiles(X, 0), XFS, attn_normed)
            with dve.Fori(0, N2 - 1) as i:
                self_attention(i)
            self_attention(N2 - 1, True)

            dve.wait_ge(cross_cleared, 3)

            def take_v(b, u, n):
                dve.wait_ge(cross_v_proj, THIRDS * b + n + 1)
                at = VX[u][0:KN, 4 * n:4 * n + 4, 0:XG * VW].rearrange("p k (h w) -> p k h w", w=XD + 1)
                for j in range(4):
                    ins = nc.vector.tensor_tensor(at[:, j, :, 0:XD],
                                                  ps[0:KN, 7, j * D:(j + 1) * D].rearrange("p (h w) -> p h w", w=XD),
                                                  RW[0:KN, R_BV:R_BV + D].rearrange("p (h w) -> p h w", w=XD), ALU.add)
                ins.then_inc(cross_v, 1)

            def maximum(b, q):
                dve.wait_ge(cross_smax, THIRDS * XG * b + q + 1)
                nc.vector.tensor_reduce(MX[0:XQ, q % XG, q // XG:q // XG + 1], ps[0:XQ, 5 + q % 2, 0:KC], AX.X, ALU.max)\
                    .then_inc(cross_top, 1)

            def shift(b):
                dve.wait_ge(cross_top, THIRDS * XG * (b + 1))
                nc.vector.tensor_reduce(CM[0:XQ, :], MX[0:XQ], AX.X, ALU.max).then_inc(cross_best, 1)
                dve.wait_ge(cross_best, b + 1)
                nc.vector.tensor_scalar(CB[0:XQ, :], CM[0:XQ, :], -1.0, None, ALU.mult).then_inc(cross_negated, 1)

            def cross(b, u):
                q = 0
                for kt in range(KT):
                    if kt % 4 == 1:
                        for _ in range(max(FIRST[kt] - 1, 0)):
                            maximum(b + 1, q)
                            q += 1
                        take_v(b + 1, 1 - u, kt // 4)
                    for _ in range(min(FIRST[kt], 1) if kt % 4 == 1 else FIRST[kt]):
                        maximum(b + 1, q)
                        q += 1
                    if kt == KT - 3:
                        shift(b + 1)

            for n in range(THIRDS):
                take_v(0, 0, n)
            for q in range(THIRDS * XG):
                maximum(0, q)
            shift(0)
            with dve.Fori(0, PAIRS - 1) as p:
                cross(2 * p, 0)
                cross(2 * p + 1, 1)
            cross(B - 2, 0)

            def add_experts(i, sig, xs):
                h_made, gelu_done, y_made, y_added = sig
                for e in range(E):
                    for u, xt in enumerate(xs):
                        if e % 4 == 0 and u == 0:
                            dve.wait_ge(y_made, 2 * E * i + 1 + 2 * (e + 4))
                        if e > 0:
                            dve.wait_ge(y_added, 2 * E * i + 1 + 2 * (e - 1) + u + 1)
                        nc.vector.scalar_tensor_tensor(xt, bank(u, 2 + e // 4)[:, (e % 4) * D:(e % 4 + 1) * D],
                                                       coef[:, u, e:e + 1], xt, ALU.mult, ALU.add).then_inc(y_added, 1)

            def add_bias(i, xs):
                for u, xt in enumerate(xs):
                    dve.wait_ge(tail_b2, 2 * i + u + 1)
                    nc.vector.tensor_tensor(xt, bank(u, 3)[:, 0:D], xt, ALU.add).then_inc(tail_x2b, 1)
                dve.wait_ge(tail_x2b, 2 * i + 2)

            tie = over(CT[:, C_TIE:C_TIE + E], 2)

            def pick(step, g_, top, won, hot, tie):
                step(nc.vector.tensor_reduce(top, g_, AX.X, ALU.max))
                step(nc.vector.tensor_tensor(hot, g_, wide(top, E), ALU.is_equal))
                step(nc.vector.tensor_tensor(hot, hot, tie, ALU.mult))
                step(nc.vector.tensor_reduce(won, hot, AX.X, ALU.max))
                step(nc.vector.tensor_tensor(hot, hot, wide(won, E), ALU.is_equal))

            def gates(i, step, k, row, into):
                for u in (0, 1):
                    dve.wait_ge(tail_logits, 2 * i + u + 1)
                    step(nc.vector.tensor_tensor(sm[:, u, 0:8], bank(u, k)[:, 0:E], RW[:, row:row + E], ALU.add))
                step(nc.vector.tensor_reduce(sm[:, :, 16], sm[:, :, 0:8], AX.X, ALU.max))
                nc.vector.tensor_tensor(sm[:, :, 0:8], sm[:, :, 0:8], wide(sm[:, :, 16], E), ALU.subtract)\
                    .then_inc(tail_shifted, 1)
                dve.wait_ge(tail_expd, i + 1)
                step(nc.vector.tensor_reduce(sm[:, :, 17], sm[:, :, 8:16], AX.X, ALU.add))
                step(nc.vector.reciprocal(sm[:, :, 18], sm[:, :, 17]))
                step(nc.vector.tensor_tensor(into, sm[:, :, 8:16], wide(sm[:, :, 18], E), ALU.mult))

            KXS = [KX[:, u, :] for u in (0, 1)]

            def mqa_norms(i, nth):
                ln_vector(dve, nth, tiles(X, i), KXS, mqa_normed)
                dve.wait_ge(mqa_normed, 2 * i + 1)
                ln_vector(dve, nth + 1, KXS, KXS, mqa_normed)
                dve.wait_ge(mqa_normed, 2 * i + 2)
                nc.vector.tensor_tensor(KX, KX, over(RW[:, R_NG:R_NG + D], 2), ALU.mult).then_inc(mqa_scaled, 1)

            def tail(i, last=False):
                for u in (0, 1):
                    dve.wait_ge(tail_turned, 2 * i + u + 1)
                    step = Steps(dve, tail_steps, 19 * i + 4 * u)
                    for j in (0, 1):
                        for h in (0, 1):
                            got = bank(u, 0).rearrange("p (j h g w) -> p j h g w", j=2, h=2, w=32)[:, j, h]
                            at = sm[:, u, 4 * (2 * j + h):4 * (2 * j + h) + 4]
                            step(nc.vector.reciprocal(at, got[:, :, h * (XD + 1) + XD]))
                    for j in (0, 1):
                        for h in (0, 1):
                            got = bank(u, 0).rearrange("p (j h g w) -> p j h g w", j=2, h=2, w=32)[:, j, h]
                            at = sm[:, u, 4 * (2 * j + h):4 * (2 * j + h) + 4]
                            ins = nc.vector.tensor_tensor(
                                CN[:, u].rearrange("p (j g h w) -> p j g h w", j=2, h=2, w=XD)[:, j, :, h, :],
                                got[:, :, h * (XD + 1):h * (XD + 1) + XD], wide(at, XD), ALU.mult)
                    ins.then_inc(tail_ctx, 1)
                add_to_x(i, tail_proj, tail_sum, tail_x2, 2, R_BO2)
                dve.wait_ge(tail_x2, 2 * i + 2)
                ln_vector(dve, LN_T + i, tiles(X, i), XS, tail_normed)
                step = Steps(dve, tail_steps, 19 * i + 8)
                gates(i, step, 0, R_BG, sm[:, :, 24:32])
                pick(step, sm[:, :, 24:32], sm[:, :, 19], sm[:, :, 20], sm[:, :, 32:40], tie)
                nc.vector.tensor_tensor(coef[:, :, :], sm[:, :, 24:32], sm[:, :, 32:40], ALU.mult).then_inc(tail_coef, 1)
                assert step.n == 11
                add_bias(i, tiles(X, i))
                if last:
                    nc.vector.memset(VM, 1.0).then_inc(rope_keep, 1)
                    mqa_norms(0, LN_M)
                add_experts(i, tail_ffn, tiles(X, i))

            with dve.Fori(0, N2 - 1) as i:
                tail(i)
            tail(N2 - 1, True)

            def rope_norms(i, step):
                nth = LN_R + 3 * i if not isinstance(i, int) or i else LN_R - 1
                ln_vector(dve, nth, tiles(X, i), XS, rope_normed)
                dve.wait_ge(rope_normed, 3 * i + 1)
                ln_vector(dve, nth + 1, XS, XS, rope_normed)
                ln_vector(dve, nth + 2, tiles(C56, i), [KX[:, u, :] for u in (0, 1)], rope_normed)
                dve.wait_ge(rope_normed, 3 * i + 3)
                for y in (XN[:, :, :], KX):
                    ins = nc.vector.tensor_tensor(y, y, over(RW[:, R_LG:R_LG + D], 2), ALU.mult)
                step(ins)
                nc.vector.tensor_tensor(XN[:, :, :], XN[:, :, :], over(RW[:, R_LB:R_LB + D], 2), ALU.add)
                nc.vector.tensor_tensor(KX, KX, over(RW[:, R_LB:R_LB + D], 2), ALU.add).then_inc(rope_scaled, 1)

            def mqa(i, last=False):
                for u in (0, 1):
                    dve.wait_ge(mqa_sq, 2 * i + u + 1)
                    ins = nc.vector.tensor_reduce(sm[:, u, 0:9], T3[:, u, 0:576].rearrange("p (h w) -> p h w", w=DH),
                                                  AX.X, ALU.add)
                ins.then_inc(mqa_ss, 1)
                step = Steps(dve, mqa_steps, 4 * i)
                dve.wait_ge(mqa_root, i + 1)
                step(nc.vector.tensor_scalar(sm[:, :, 32:41], sm[:, :, 16:25], NORM_EPS, None, ALU.max))
                step(nc.vector.reciprocal(sm[:, :, 48:57], sm[:, :, 32:41]))
                for u in (0, 1):
                    dve.wait_ge(mqa_v, 2 * i + u + 1)
                    nc.vector.scalar_tensor_tensor(T1[:, u, 0:512].rearrange("p (h w) -> p h w", w=DH),
                                                   bank(u, 0).rearrange("p (h w) -> p h w", w=DH), 64.0,
                                                   wide(sm[:, u, 48:56], DH), ALU.mult, ALU.mult)
                    nc.vector.scalar_tensor_tensor(T1[:, u, 512:640].rearrange("p (h w) -> p h w", w=DH),
                                                   over(bank(u, 1)[:, 0:DH], 2), 4.0,
                                                   wide(sm[:, u, 56:57].broadcast_to([128, 2]), DH), ALU.mult, ALU.mult)\
                        .then_inc(mqa_qn, 1)
                for u in (0, 1):
                    dve.wait_ge(mqa_turned, 2 * i + u + 1)
                    nc.vector.tensor_copy(T2[:, u, 512:640], bank(u, 3)[:, 0:128]).then_inc(mqa_kT, 1)
                if not last:
                    mqa_norms(i + 1, LN_M + 3 * i + 2)
                else:
                    keep = Steps(dve, rope_keep, 1)
                    keep(nc.vector.tensor_copy(MK, mask8[:, :]))
                    keep(nc.vector.tensor_scalar(MK, MK, -1.0, 1.0, ALU.mult, ALU.add))
                    for k in range(PAIRS):
                        ins = nc.vector.tensor_scalar(KEEP[:, k, :], CT[:, C_CAUSAL:C_CAUSAL + HALF], MK[:, k:k + 1], None, ALU.mult)
                    keep(ins)
                    dve.wait_ge(load_context, 16)
                    rope_norms(0, Steps(dve, rope_steps, 0))
                for u in (0, 1):
                    dve.wait_ge(mqa_pv, 2 * i + u + 1)
                    got = heads4(u, 1, 2)
                    den = sm[:, u, 0:8].rearrange("p (a h) -> p a h", a=2)
                    step2 = Steps(dve, mqa_steps, 4 * i + 2 + u)
                    step2(nc.vector.reciprocal(den, got[:, :, :, DH]))
                    nc.vector.tensor_tensor(T1[:, u, 0:512].rearrange("p (a h w) -> p a h w", a=2, w=DH),
                                            got[:, :, :, 0:DH], wide(den, DH), ALU.mult).then_inc(mqa_o, 1)
                dve.wait_ge(mqa_proj, 2 * i + 2)
                ln_vector(dve, LN_M + 3 * i + (5 if last else 4), [bank(u, 0)[:, 0:D] for u in (0, 1)],
                          [T4[:, u, 0:D] for u in (0, 1)], mqa_normed2)
                dve.wait_ge(mqa_normed2, i + 2)
                nc.vector.tensor_tensor(T4[:, :, 0:D], T4[:, :, 0:D], over(RW[:, R_ONG:R_ONG + D], 2), ALU.mult).then_inc(mqa_outn, 1)
                dve.wait_ge(mqa_outn, i + 1)
                for u, xt in enumerate(tiles(X, i)):
                    ins = nc.vector.tensor_tensor(xt, xt, T4[:, u, 0:D], ALU.add)
                ins.then_inc(mqa_sum, 1)

            with dve.Fori(0, N2 - 1) as i:
                mqa(i)
            mqa(N2 - 1, True)

            def rope(i, last=False):
                step = Steps(dve, rope_steps, 5 * i + 1)
                for made, into, other in ((rope_qproj, T1, T2), (rope_kproj, T3, T4)):
                    for u in (0, 1):
                        dve.wait_ge(made, 2 * i + u + 1)
                        for k, dst, table in ((0, into, C_COS), (2, other, C_SIN)):
                            ins = nc.vector.tensor_tensor(dst[:, u, :].rearrange("p (j n) -> p j n", n=TILE),
                                                          bank(u, k, 2).rearrange("p (j n) -> p j n", n=TILE),
                                                          over(CT[:, table:table + TILE], 8), ALU.mult)
                        ins.then_inc(rope_parts, 1)
                if not last:
                    rope_norms(i + 1, step)
                for u in (0, 1):
                    dve.wait_ge(rope_pv, 2 * i + u + 1)
                    got = heads4(u, 0, 4)
                    den = sm[:, u, 0:16].rearrange("p (a h) -> p a h", a=4)
                    step(nc.vector.reciprocal(den, got[:, :, :, DH]))
                    nc.vector.tensor_tensor(T1[:, u, :].rearrange("p (a h w) -> p a h w", a=4, w=DH),
                                            got[:, :, :, 0:DH], wide(den, DH), ALU.mult).then_inc(rope_o, 1)
                for u, xt in enumerate(tiles(X, i)):
                    dve.wait_ge(rope_out, 2 * i + u + 1)
                    step(nc.vector.tensor_tensor(xt, bank(u, 2)[:, 0:D], xt, ALU.add))
                assert last or step.n == 5

            with dve.Fori(0, N2 - 1) as i:
                rope(i)
            rope(N2 - 1, True)

            dve.wait_ge(rope_steps, 5 * N2)
            step = Steps(dve, moe_steps, 0)
            for t in range(PAIRS):
                ins = nc.vector.bn_stats(st8[:, t, :], X[:, t, :])
            step(ins)
            for t in range(PAIRS):
                ins = nc.vector.bn_aggr(mv8[:, t, :], st8[:, t, :])
            step(ins)
            nc.vector.tensor_scalar(var8, mv8[:, :, 1], LN_EPS, None, ALU.add).then_inc(ln_variance, 1)
            dve.wait_ge(ln_rstd, LN_F + 1)
            for t in range(PAIRS):
                ins = nc.vector.tensor_scalar(XA[:, t, :], X[:, t, :], mv8[:, t, 0:1], rstd8[:, t:t + 1],
                                              ALU.subtract, ALU.mult)
                if t % 4 == 3:
                    ins.then_inc(moe_normed, 1)
            dve.wait_ge(moe_logits, 1)
            logits = ps[:, 1, 0:PAIRS * E].rearrange("p (t e) -> p t e", e=E)
            top, total, won = TOP[:, 0, :], TOP[:, 1, :], TOP[:, 2, :]
            step(nc.vector.tensor_tensor(LG, logits, over(RW[:, R_RB:R_RB + E], PAIRS), ALU.add))
            step(nc.vector.tensor_reduce(top, LG, AX.X, ALU.max))
            nc.vector.tensor_tensor(LG, LG, wide(top, E), ALU.subtract).then_inc(tail_shifted, 1)
            dve.wait_ge(tail_expd, N2 + 1)
            step(nc.vector.tensor_reduce(total, EX, AX.X, ALU.add))
            step(nc.vector.reciprocal(total, total))
            step(nc.vector.tensor_tensor(GATE, EX, wide(total, E), ALU.mult))
            tie8 = over(CT[:, C_TIE:C_TIE + E], PAIRS)
            pick(step, GATE, top, won, HOT, tie8)
            step(nc.vector.scalar_tensor_tensor(LEFT, HOT, -4.0, GATE, ALU.mult, ALU.add))
            pick(step, LEFT, top, won, HOT2, tie8)
            nc.vector.tensor_tensor(PICK, HOT2, HOT, ALU.add).then_inc(moe_picked, 1)
            dve.wait_ge(moe_count, 1)
            flat = lambda ap: ap.rearrange("p a b -> p (a b)")
            step(nc.vector.tensor_scalar(flat(WGT), ps[:, 2, 0:PAIRS * E], float(CAPACITY), None, ALU.is_le))
            step(nc.vector.tensor_tensor(flat(WGT), flat(WGT), CT[:, C_ONES:C_ONES + PAIRS * E], ALU.mult))
            step(nc.vector.tensor_tensor(flat(WGT), flat(WGT), flat(PICK), ALU.mult))
            step(nc.vector.tensor_tensor(flat(SLOT), ps[:, 2, 0:PAIRS * E], flat(WGT), ALU.mult))
            step(nc.vector.tensor_tensor(flat(WGT), flat(WGT), flat(GATE), ALU.mult))


            def one_hot(u, t):
                return nc.vector.tensor_tensor(ONEHOT[:, u].rearrange("p (e n) -> p e n", n=SLOTS),
                                               over(CT[:, C_PLACE:C_PLACE + SLOTS], E), wide(SLOT[:, t, :], SLOTS), ALU.is_equal)

            for t in range(PAIRS):
                if t >= 2:
                    dve.wait_ge(last_read, t - 1)
                one_hot(t % 2, t).then_inc(last_onehot, 1)

            def weighed(i):
                for u in (0, 1):
                    dve.wait_ge(last_read, PAIRS + 2 * i + u - 1)
                    one_hot(u, 2 * i + u).then_inc(last_onehot, 1)
                    dve.wait_ge(last_onehot, PAIRS + 4 * i + 2 * u + 1)
                    both = ONEHOT[:, u].rearrange("p (e n) -> p e n", n=SLOTS)
                    nc.vector.tensor_tensor(both, both, wide(WGT[:, 2 * i + u, :], SLOTS), ALU.mult).then_inc(last_onehot, 1)

            def add_returned(i):
                for u, xt in enumerate(tiles(X, i)):
                    dve.wait_ge(last_y, E + 2 * i + u + 1)
                    nc.vector.tensor_tensor(xt, bank(u, 3)[:, 0:D], xt, ALU.add).then_inc(last_acc, 1)

            weighed(0)
            dve.wait_ge(load_late_w, 112)
            for e in range(E):
                dve.wait_ge(last_y, e + 1)
                for j, (chunk, row, n, first) in enumerate(pieces(e)):
                    ins = nc.vector.tensor_tensor(OUTS[row:row + n, chunk, :], ps[row:row + n, e % 3, j * D:(j + 1) * D],
                                                  LB2[row:row + n, e, :], ALU.add)
                ins.then_inc(last_acc, 1)
            with dve.Fori(0, N2 - 1) as i:
                weighed(i + 1)
                add_returned(i)
            add_returned(N2 - 1)


def tables():
    import numpy as np

    t = np.zeros((128, C_END), np.float32)
    t[:, C_IDENT:C_IDENT + 128] = np.eye(128)
    p = np.arange(128)
    inv = (np.float32(1.0) / np.float32(10000.0) ** (np.arange(0, DH, 2, dtype=np.float32) / np.float32(DH)))
    angle = (np.arange(HALF, dtype=np.float32)[None, :] * np.repeat(inv, 2)[:, None]).astype(np.float32)
    sign = np.where(np.arange(DH) % 2, 1.0, -1.0)[:, None]
    t[:, C_COS:C_COS + 128] = np.tile(np.cos(angle), (2, 2))
    t[:, C_SIN:C_SIN + 128] = np.tile(np.sin(angle) * sign, (2, 2))
    token, batch = p % HALF, p // HALF
    t[:, C_CAUSAL:C_CAUSAL + HALF] = (token[:, None] <= np.arange(HALF)[None, :]) & (token[:, None] < S)
    order = batch * HALF + token
    t[:, C_TRI:C_TRI + 128] = (order[:, None] <= order[None, :]) & (token[:, None] < S)
    t[:, C_ONES:C_ONES + 128] = (token[:, None] < S)
    t[:, C_TIE:C_TIE + E] = E - np.arange(E)
    row = np.arange(STACK)
    for h in (0, 1):
        t[:STACK, C_BLK + h] = (row // XD % 2) == h
    part = np.array(Q_PART)[row // (2 * XD)]
    t[:STACK, C_MASK1] = -(part >= 1).astype(np.float32)
    t[:STACK, C_MASK2] = -(part >= 2).astype(np.float32)
    t[:, C_MHALF:C_MHALF + PAIRS] = -0.5
    t[:, C_HALF:C_HALF + 18] = 0.5
    t[:, C_PLACE:C_PLACE + SLOTS] = 1 + np.arange(SLOTS)
    return t


def kernel(**inputs):
    import numpy as np
    import concourse.bacc as bacc
    from concourse import mybir as mb
    from concourse.bass_utils import run_bass_kernel_spmd as run

    v = {k: np.asarray(a) for k, a in inputs.items()}

    def halves(z):
        w = np.zeros((B, HALF) + z.shape[2:], z.dtype)
        w[:, :S] = z
        w = w.reshape((PAIRS, TILE) + z.shape[2:])
        return np.ascontiguousarray(np.moveaxis(w, 0, 1))

    def by_row(z):
        return np.broadcast_to(z, (128,) + z.shape)

    def by_parity(w):
        return w.reshape(D, 8, 2, DH).transpose(0, 2, 1, 3).reshape(D, INNER)

    def stacked(w):
        w = w.reshape(w.shape[:-1] + (XG, 1, 2 * XD))
        w = np.repeat(w, len(K_PART), axis=-2)
        return w.reshape(w.shape[:-2] + (STACK,))

    def swapped(w):
        return w.reshape(D, INNER // 2, 2)[:, :, ::-1].reshape(D, INNER)

    def width_first(w):
        return np.swapaxes(w.reshape(w.shape[:-1] + (XG, 2 * XD)), -1, -2).reshape(w.shape)

    rows = np.concatenate([by_row(v[n]) for n in (
        "L0_attn_bo", "L0_xattn_b_v", "L0_xattn_b_o", "L0_ffn_bg", "L1_attn_norm_g", "L1_attn_out_norm_g",
        "L1_xattn_ln_g", "L1_xattn_ln_b", "L1_ffn_router_b")], axis=1)
    bq = np.zeros((128, XG), np.float32)
    bq[:STACK] = stacked(v["L0_xattn_b_q"]).T
    cols = np.concatenate([width_first(v["L0_xattn_b_k"])[:, None], bq,
                           v["L0_ffn_b1"].reshape(-1, 128).T, v["L1_ffn_b1"].reshape(-1, 128).T], axis=1)
    data = {
        "x": halves(v["x"]),
        "ctx_t": v["ctx_1024"].transpose(0, 2, 1),
        "ctx_first": halves(v["ctx_1024"][:, :S]),
        "mask": halves(v["mask_BxS2_bf0"][:, :S]),
        "consts": tables(), "rows": rows, "cols": cols,
        "a_wq": v["L0_attn_Wq"].T, "a_wk": v["L0_attn_Wk"].T, "a_wv": by_parity(v["L0_attn_Wv"].T),
        "a_wo": v["L0_attn_Wo"].T,
        "x_wq": stacked(v["L0_xattn_W_q"].T).reshape(D, XG * STACK),
        "x_wk": width_first(v["L0_xattn_W_k"].T), "x_wv": v["L0_xattn_W_v"].T, "x_wo": v["L0_xattn_W_o"].T,
        "g_w": v["L0_ffn_Wg"], "f_w1": v["L0_ffn_W1"], "f_w2": v["L0_ffn_W2"], "f_b2": v["L0_ffn_b2"],
        "m_wq": v["L1_attn_Wq"], "m_wkv": v["L1_attn_Wkv"], "m_wo": v["L1_attn_Wout"],
        "r_wq": v["L1_xattn_Wq"], "r_wqr": swapped(v["L1_xattn_Wq"]),
        "r_wk": v["L1_xattn_Wk"], "r_wkr": swapped(v["L1_xattn_Wk"]),
        "r_wv": v["L1_xattn_Wv"], "r_wo": v["L1_xattn_Wo"],
        "l_w": v["L1_ffn_router_w"], "l_w1": v["L1_ffn_w1"], "l_w2": v["L1_ffn_w2"], "l_b2": by_row(v["L1_ffn_b2"].reshape(-1)),
    }
    nc = bacc.Bacc("TRN2", target_bir_lowering=False, num_devices=1)
    arrays, args = {}, []
    for name, z in data.items():
        z = np.ascontiguousarray(z)
        arrays[f"in_{name}"] = z
        args.append(nc.dram_tensor(f"in_{name}", z.shape, mb.dt.from_np(z.dtype), kind="ExternalInput").ap())
    args.append(nc.dram_tensor("out", (B, S, D), mb.dt.float32, kind="ExternalOutput").ap())
    decoder_kernel(nc, *args)
    return run(nc, [arrays], core_ids=[0]).results[0]["out"]
```

```python
import math
from contextlib import ExitStack

import concourse.bass as bass
from concourse import mybir

B, S, D = 16, 56, 128
SK = 1500
PAIRS = B // 2
HALF = 64
TILE = 2 * HALF
HEADS, DH = 16, 64
INNER = HEADS * DH
XD = D // HEADS
XG = HEADS // 2
XQ = 2 * S
K_PART = (0, 1, 2, 0, 1, 0)
Q_PART = (0, 0, 0, 1, 1, 2)
K_RUNS = (3, 2, 1)
STACK = len(K_PART) * 2 * XD
SHIFT = STACK
KT, KN = 12, 125
THIRDS, KC = 3, 500
VW = 2 * (XD + 1)
VROW = XG * VW + 32 - VW
H1 = 8
E, F0, F1 = 8, 256, 512
CAPACITY = max(1, math.ceil(B * S / E * 1.25))
SLOTS = -(-CAPACITY // 32) * 32
CHUNKS = E * SLOTS // 128
K0, K1 = F0 // 128, F1 // 128
LN_EPS, SAFE_EPS, NORM_EPS = 1e-5, 1e-10, 1e-12
GROK = 30.0

FIRST = (2, 3, 2, 3, 2, 3, 2, 3, 2, 2, 0, 0)
assert sum(FIRST) == THIRDS * XG

C_IDENT, C_COS, C_SIN, C_CAUSAL, C_TRI, C_ONES = 0, 128, 256, 384, 448, 576
C_TIE, C_BLK, C_MASK1, C_MASK2, C_MHALF, C_HALF, C_PLACE = 704, 712, 714, 715, 716, 724, 742
C_END = C_PLACE + SLOTS
R_BO, R_BV, R_BO2, R_BG, R_NG, R_ONG, R_LG, R_LB, R_RB, R_END = 0, 128, 256, 384, 392, 520, 648, 776, 904, 912
P_BK, P_BQ, P_B1, P_B1L, P_END = 0, 1, 9, 25, 57


class Steps:

    def __init__(self, engine, semaphore, before):
        self.engine, self.semaphore, self.before, self.n = engine, semaphore, before, 0

    def __call__(self, instruction):
        instruction.then_inc(self.semaphore, 1)
        self.n += 1
        self.engine.wait_ge(self.semaphore, self.before + self.n)


def decoder_kernel(nc, x, ctx_t, ctx_first, mask, consts, rows, cols, a_wq, a_wk, a_wv, a_wo,
                   x_wq, x_wk, x_wv, x_wo, g_w, f_w1, f_w2, f_b2, m_wq, m_wkv, m_wo,
                   r_wq, r_wqr, r_wk, r_wkr, r_wv, r_wo, l_w, l_w1, l_w2, l_b2, out):
    f32, bf16 = mybir.dt.float32, mybir.dt.bfloat16
    ALU, ACT, AX = mybir.AluOpType, mybir.ActivationFunctionType, mybir.AxisListType

    ctx = ExitStack()
    with ctx:
        def sb(name, shape, dt=f32):
            return ctx.enter_context(nc.sbuf_tensor(name, shape, dt))

        def signals(stage, names):
            return [ctx.enter_context(nc.semaphore(f"{stage}_{n}")) for n in names.split()]

        X = sb("X", [128, PAIRS, D])
        CT = sb("CT", [128, C_END])
        RW = sb("RW", [128, R_END])
        PC = sb("PC", [128, P_END])
        ident = CT[:, C_IDENT:C_IDENT + 128]
        identb = sb("identb", [128, 128], bf16)
        st = sb("st", [128, 2, 6])
        mv = sb("mv", [128, 2, 2])
        vr = sb("vr", [128, 2])
        rstd = sb("rstd", [128, 2])
        XN = sb("XN", [128, 2, D])
        XNT = sb("XNT", [128, 2, TILE])
        QS = sb("QS", [SHIFT + 1, B, XG, XQ], bf16)
        PO = sb("PO", [128, PAIRS, 2, 2, TILE])
        sm = sb("sm", [128, 2, 64])
        XWK, XWV, XWO = sb("XWK", [128, D]), sb("XWV", [128, D]), sb("XWO", [128, D])
        FW1 = sb("FW1", [128, E, F0])
        FW2 = sb("FW2", [128, E * F0 // 128, D])
        ones = sb("ones", [125, XG * SK // 125], bf16)
        mask8 = sb("mask8", [128, PAIRS], mybir.dt.uint8)

        ARENA = 31400 + 1536
        arena = sb("arena", [128, ARENA])
        place = [0]

        def take(*shape, dt=f32):
            n = math.prod(shape)
            words = n if dt == f32 else (n + 1) // 2
            part = arena[:, place[0]:place[0] + words]
            place[0] += words
            assert place[0] <= ARENA, place[0]
            if dt != f32:
                part = part.bitcast(dt)
            if len(shape) == 1:
                return part
            names = "abcd"[:len(shape)]
            return part.rearrange(f"p ({' '.join(names)}) -> p {' '.join(names)}",
                                  **{k: v for k, v in zip(names[1:], shape[1:])})

        WQ, WK, WV, WO = take(INNER), take(INNER), take(2, 8 * DH), take(8, D)
        WQS = take(XG, STACK)
        work = place[0]
        qT, kT, V = take(2, 8, TILE), take(2, 8, TILE), take(2, 2, 8 * DH)
        P, PT, OT = take(2, HEADS, HALF), take(2, 8, TILE), take(2, 8, TILE)
        XFT = take(2, TILE)
        q_work = place[0]
        XF = take(2, D)
        qf = take(2, XG, TILE)
        q1, q2 = take(2, XG, TILE, dt=bf16), take(2, XG, TILE, dt=bf16)
        attn_end = place[0]
        place[0] = work
        kf, kr, kp = take(THIRDS, KC), take(KC), take(THIRDS, 3, KC, dt=bf16)
        KS = [take(XG, SK, dt=bf16)]
        PX = [take(XG, XQ) for _ in range(2)]
        MX, CM, CB = take(XG, THIRDS), take(XG), take(XG, dt=bf16)
        assert place[0] <= q_work, (place[0], q_work)
        place[0] = q_work
        KS.append(take(XG, SK, dt=bf16))
        CX = [take(SK) for _ in range(2)]
        assert place[0] - 2 * SK >= attn_end
        VX = [take(KT, VROW) for _ in range(2)]
        PF, CN, CNT = take(2, 4, TILE), take(2, D), take(2, TILE)
        place[0] = 0
        MWQ, MWKV, MWO = take(H1 * DH), take(2 * DH), take(4, D)
        GW, LW, FB2 = take(E), take(E), take(D)
        rope_w = place[0]
        RWQ, RWQR = take(INNER), take(INNER)
        assert place[0] <= work
        place[0] = work
        RWK, RWKR, RWV, RWO = take(INNER), take(INNER), take(INNER), take(8, D)
        rope_w_end = place[0]
        LW1, LW2 = take(E, F1), take(E * F1 // 128, D)
        coef, coefT = take(2, E), take(2, TILE)
        GATE, PICK, WGT = (take(PAIRS, E) for _ in range(3))
        XNTA = take(PAIRS, TILE)
        late = place[0]
        HB = take(8, 2 * TILE)
        XA = take(PAIRS, D)
        LG, EX, HOT, LEFT, HOT2 = (take(PAIRS, E) for _ in range(5))
        SLOT, OUTS, PT2 = take(PAIRS, E), take(CHUNKS, D), take(2, CHUNKS, TILE)
        st8, mv8, var8, rstd8, TOP = take(PAIRS, 6), take(PAIRS, 2), take(PAIRS), take(PAIRS), take(3, PAIRS)
        place[0] = rope_w
        ONEHOT, XTS = take(2, E * SLOTS), take(E * SLOTS)
        HG, LB2 = take(2, K1, SLOTS), take(E, D)
        assert place[0] <= rope_w_end
        place[0] = late
        T1, T2, T3, T4 = (take(2, INNER) for _ in range(4))
        VM = take(2, HEADS, DH + 1)
        C56, KEEP, MK = take(PAIRS, D), take(PAIRS, HALF), take(PAIRS)
        KX, KXT = take(2, D), take(2, TILE)

        ps = ctx.enter_context(nc.psum_tensor("ps", [128, 8, 512], f32))
        k_scratch = nc.dram_tensor("k_parts", (2, 3, 128, SK), bf16, kind="Internal").ap()
        ones_scratch = nc.dram_tensor("k_ones", (1, XG, SK), bf16, kind="Internal").ap()

        (load_passed, load_consts, load_tokens, load_attn_w, load_rest_w, load_ones, load_middle_w, load_late_w, load_context) = signals(
            "load", "passed consts tokens attn_w rest_w ones middle_w late_w context")
        (ln_stats, ln_moments, ln_variance, ln_rstd) = signals(
            "ln", "stats moments variance rstd")
        (attn_cleared, attn_normed, attn_xT, attn_xnT, attn_q_proj, attn_k_proj, attn_v_proj, attn_q, attn_k,
         attn_v, attn_scores, attn_top, attn_shifted, attn_expd, attn_steps, attn_probs, attn_probsT, attn_pT,
         attn_pv, attn_o, attn_proj, attn_sum, attn_x1, attn_normed2, attn_xT2, attn_xnT2, attn_stack, attn_qf,
         attn_q1, attn_r1, attn_q2, attn_r2, attn_qstack) = signals(
            "attn", "cleared normed xT xnT q_proj k_proj v_proj q k v scores top shifted expd steps probs probsT pT pv o "
            "proj sum x1 normed2 xT2 xnT2 stack qf q1 r1 q2 r2 qstack")
        (cross_cleared, cross_ctx0, cross_ctx1, cross_k_proj, cross_kf, cross_r1, cross_k2, cross_k3, cross_out0,
         cross_out1, cross_out2, cross_in0, cross_in1, cross_in2, cross_v_proj, cross_v, cross_smax, cross_top,
         cross_best, cross_negated, cross_shift, cross_shifted, cross_scores, cross_probs, cross_pv, cross_o) = signals(
            "cross", "cleared ctx0 ctx1 k_proj kf r1 k2 k3 out0 out1 out2 in0 in1 in2 v_proj v smax top best negated shift "
            "shifted scores probs pv o")
        (tail_copied, tail_turned, tail_steps, tail_ctx, tail_ctxT, tail_ctxS, tail_proj, tail_sum, tail_x2,
         tail_normed, tail_xT, tail_xnT, tail_logits, tail_shifted, tail_expd, tail_coef, tail_coefT, tail_coefS,
         tail_b2, tail_x2b, tail_h, tail_gelu, tail_y, tail_acc) = signals(
            "tail", "copied turned steps ctx ctxT ctxS proj sum x2 normed xT xnT logits shifted expd coef coefT coefS b2 "
            "x2b h gelu y acc")
        (mqa_normed, mqa_scaled, mqa_xT, mqa_xnT, mqa_qkv, mqa_sq, mqa_ss, mqa_root,
         mqa_steps, mqa_qn, mqa_v, mqa_turned, mqa_qT, mqa_kT, mqa_scores, mqa_probs, mqa_pv, mqa_o, mqa_oT, mqa_oS,
         mqa_proj, mqa_normed2, mqa_outn, mqa_sum) = signals(
            "mqa", "normed scaled xT xnT qkv sq ss root steps qn v turned qT kT scores probs pv o oT oS "
            "proj normed2 outn sum")
        (rope_keep, rope_normed, rope_scaled, rope_xT, rope_xnT, rope_qproj, rope_kproj,
         rope_parts, rope_qT, rope_kT, rope_v_proj, rope_v, rope_scores, rope_tanh, rope_expd, rope_masked, rope_pv,
         rope_steps, rope_o, rope_oT, rope_oS, rope_out) = signals(
            "rope", "keep normed scaled xT xnT qproj kproj parts qT kT v_proj v scores tanh expd masked "
            "pv steps o oT oS out")
        (moe_steps, moe_normed, moe_xT, moe_xnT, moe_logits, moe_picked, moe_count) = signals(
            "moe", "steps normed xT xnT logits picked count")
        (last_onehot, last_read, last_copied, last_h, last_gelu, last_y, last_acc, last_out) = signals(
            "last", "onehot read copied h gelu y acc out")

        block = ctx.enter_context(nc.Block())

        def mm(o, lhsT, rhs, start=True, stop=True, **kw):
            return nc.tensor.matmul(o, lhsT, rhs, start=start, stop=stop, **kw)

        def pieces(e):
            at, end = e * SLOTS, (e + 1) * SLOTS
            while at < end:
                row = at % 128
                n = min(end - at, (128 if row == 0 else 64 if row == 64 else 32))
                n = 1 << (n.bit_length() - 1)
                yield at // 128, row, n, at - e * SLOTS
                at += n

        def wide(ap, n):
            k = len(ap.shape)
            return ap.unsqueeze(k).broadcast_to([*ap.shape, n])

        def over(ap, n):
            return ap.unsqueeze(1).broadcast_to([ap.shape[0], n, *ap.shape[1:]])

        def bank(u, k, n=1):
            return ps[:, 4 * u + k:4 * u + k + n, :].rearrange("p a b -> p (a b)")

        def heads4(u, k, n):
            return ps[:, 4 * u + k:4 * u + k + n, 0:4 * (DH + 1)].rearrange("p a (h w) -> p a h w", w=DH + 1)

        def apart(engine):
            engine.sem_inc(load_passed, 1)

        def ln_vector(dve, nth, srcs, dsts, done):
            apart(dve)
            for u in (0, 1):
                ins = nc.vector.bn_stats(st[:, u, :], srcs[u])
            ins.then_inc(ln_stats, 1)
            dve.wait_ge(ln_stats, nth + 1)
            apart(dve)
            for u in (0, 1):
                ins = nc.vector.bn_aggr(mv[:, u, :], st[:, u, :])
            ins.then_inc(ln_moments, 1)
            dve.wait_ge(ln_moments, nth + 1)
            nc.vector.tensor_scalar(vr[:, :], mv[:, :, 1], LN_EPS, None, ALU.add).then_inc(ln_variance, 1)
            dve.wait_ge(ln_rstd, nth + 1)
            for u in (0, 1):
                ins = nc.vector.tensor_scalar(dsts[u], srcs[u], mv[:, u, 0:1], rstd[:, u:u + 1],
                                              ALU.subtract, ALU.mult)
            ins.then_inc(done, 1)

        def ln_pool(pool, nth):
            pool.wait_ge(ln_variance, nth + 1)
            nc.gpsimd.tensor_tensor(rstd[:, :], vr[:, :], CT[:, C_MHALF:C_MHALF + 2], ALU.pow)\
                .then_inc(ln_rstd, 1)

        def q_residual(engine, ops, i, part, made, left):
            for u in (0, 1):
                engine.wait_ge(made, 2 * i + u + 1)
                ops.tensor_tensor(qf[0:STACK, u], qf[0:STACK, u], part[0:STACK, u], ALU.add).then_inc(left, 1)

        def split_k(engine, ops, b, n):
            at = THIRDS * b + n + 1
            engine.wait_ge(cross_kf, at)
            if not (isinstance(at, int) and at == 1):
                engine.wait_ge(cross_k3, at - 1)
            ops.tensor_tensor(kr, kf[:, n, :], kp[:, n, 0, :], ALU.subtract).then_inc(cross_r1, 1)
            ops.tensor_tensor(kp[:, n, 1, :], kf[:, n, :], kp[:, n, 0, :], ALU.subtract).then_inc(cross_k2, 1)
            engine.wait_ge(cross_r1, at)
            engine.wait_ge(cross_k2, at)
            ops.tensor_tensor(kp[:, n, 2, :], kr, kp[:, n, 1, :], ALU.subtract).then_inc(cross_k3, 1)

        N2 = PAIRS // 2
        LN_T = 2 * N2
        LN_M = LN_T + N2
        LN_R = LN_M + 3 * N2
        LN_F = LN_R + 3 * N2
        XS = [XN[:, u, :] for u in (0, 1)]

        @block.sync
        def _(sp):
            sp.dma_start(X[:, 0:2, :], x[:, 0:2, :]).then_inc(load_tokens, 16)
            sp.dma_start(CT[:, :], consts).then_inc(load_consts, 16)
            for dst, src in ((WQ, a_wq), (WK, a_wk), (WV.rearrange("p a b -> p (a b)"), a_wv),
                             (X[:, 2:PAIRS, :], x[:, 2:PAIRS, :])):
                sp.dma_start(dst, src).then_inc(load_attn_w, 16)
            sp.wait_ge(attn_xT, 1)
            for dst, src in ((RW[:, :], rows), (PC[:, :], cols), (mask8[:, :], mask),
                             (WO, a_wo.rearrange("(j p) d -> p j d", p=128)),
                             (WQS.rearrange("p a b -> p (a b)"), x_wq), (XWK[:, :], x_wk), (XWV[:, :], x_wv),
                             (XWO[:, :], x_wo), (FW1[:, :, :], f_w1.rearrange("e p h -> p e h")),
                             (FW2[:, :, :], f_w2.rearrange("e (j p) d -> p (e j) d", p=128))):
                sp.dma_start(dst, src).then_inc(load_rest_w, 16)

            sp.wait_ge(cross_cleared, 1)
            sp.dma_start(ones_scratch.rearrange("o g n -> o (g n)").rearrange("o (p n) -> (o p) n", p=125), ones[:, :])\
                .then_inc(load_ones, 16)
            for u in (0, 1):
                sp.dma_start(CX[u], ctx_t[u, :, :]).then_inc((cross_ctx0, cross_ctx1)[u], 16)
            sp.wait_ge(attn_stack, PAIRS)
            sp.wait_ge(load_ones, 16)
            sp.dma_start(KS[0][SHIFT:SHIFT + 1], ones_scratch).then_inc(load_ones, 16)
            for dst, src in ((MWQ, m_wq), (MWKV, m_wkv), (MWO, m_wo.rearrange("(j p) d -> p j d", p=128)),
                             (GW, g_w), (LW, l_w), (FB2[0:E, :], f_b2), (RWQ, r_wq), (RWQR, r_wqr)):
                sp.dma_start(dst, src).then_inc(load_middle_w, 16)
            outs, ins_ = (cross_out0, cross_out1, cross_out2), (cross_in0, cross_in1, cross_in2)

            def load_ctx(b, u):
                sp.wait_ge(cross_v_proj, THIRDS * (b - 1))
                sp.wait_ge(cross_k_proj, THIRDS * (b - 1))
                apart(sp)
                sp.dma_start(CX[u], ctx_t[b, :, :]).then_inc((cross_ctx0, cross_ctx1)[u], 16)

            def stack_third(b, u, n, first=False):
                lo = n * KC
                sp.wait_ge(cross_k3, THIRDS * b + n + 1)
                apart(sp)
                sp.dma_start(k_scratch[u, :, :, lo:lo + KC].rearrange("c p n -> p c n"), kp[:, n])\
                    .then_inc(outs[n], 16)
                sp.wait_ge(outs[n], 16 * (b + 1))
                apart(sp)
                if not first:
                    sp.wait_ge(cross_scores, KT * (b - 2) + 4 * (n + 1))
                    apart(sp)
                at = 0
                for run in K_RUNS:
                    rows_ = 2 * XD * run
                    sp.dma_start(KS[u][at:at + rows_, :, lo:lo + KC],
                                 k_scratch[u, 0:run, :, lo:lo + KC].rearrange("c (r g) n -> (c r) g n", g=XG))\
                        .then_inc(ins_[n], 16)
                    at += rows_

            for n in range(THIRDS):
                stack_third(0, 0, n, True)
            sp.wait_ge(attn_qstack, PAIRS)
            sp.wait_ge(load_ones, 32)
            sp.dma_start(KS[1][SHIFT:SHIFT + 1], ones_scratch).then_inc(load_ones, 16)
            for n in range(THIRDS):
                stack_third(1, 1, n, True)

            def cross(b, u, more=True):
                for n in range(THIRDS):
                    if n == THIRDS - 1 and more:
                        load_ctx(b + 3, 1 - u)
                    stack_third(b + 2, u, n)

            load_ctx(2, 0)
            with sp.Fori(0, PAIRS - 2) as p:
                cross(2 * p, 0)
                cross(2 * p + 1, 1)
            cross(B - 4, 0)
            cross(B - 3, 1, more=False)

            sp.wait_ge(cross_o, B + 1)
            for dst, src in ((RWK, r_wk), (RWKR, r_wkr), (RWV, r_wv), (RWO, r_wo.rearrange("(j p) d -> p j d", p=128)),
                             (LW1, l_w1.rearrange("e p h -> p e h")),
                             (LW2, l_w2.rearrange("e (j p) d -> p (e j) d", p=128))):
                sp.dma_start(dst, src).then_inc(load_late_w, 16)
            sp.wait_ge(tail_acc, 2 * E * N2 + 1)
            sp.dma_start(C56, ctx_first).then_inc(load_context, 16)
            sp.wait_ge(moe_normed, 1)
            sp.dma_start(LB2.rearrange("p a b -> p (a b)"), l_b2).then_inc(load_late_w, 16)

            with sp.Fori(0, N2) as i:
                sp.wait_ge(last_acc, E + 2 * i + 2)
                apart(sp)
                for b in (0, 1):
                    sp.dma_start(out.rearrange("(t b) s d -> b s t d", b=2)[b, :, bass.ds(2 * i, 2), :],
                                 X[HALF * b:HALF * b + S, bass.ds(2 * i, 2), :]).then_inc(last_out, 16)
            sp.wait_ge(last_out, 16 * 2 * N2)

        @block.tensor
        def _(pe):
            pe.wait_ge(load_consts, 16)
            pe.sem_inc(tail_y, 1)

            def transposed(u, srcs, dst):
                for j, src in enumerate(srcs):
                    ins = nc.tensor.transpose(dst[:, j * TILE:(j + 1) * TILE], src, ident)
                return ins

            def projected(i):
                pe.wait_ge(attn_normed, i + 1)
                for u in (0, 1):
                    transposed(u, [XF[:, u, :]], bank(u, 0)).then_inc(attn_xT, 1)
                pe.wait_ge(load_attn_w, 64)
                for u in (0, 1):
                    pe.wait_ge(attn_xnT, 2 * i + u + 1)
                    for j in range(8):
                        ins = mm(bank(u, 0, 2)[:, j * TILE:(j + 1) * TILE], WQ[:, j * 128:(j + 1) * 128], XFT[:, u, :])
                    ins.then_inc(attn_q_proj, 1)
                for u in (0, 1):
                    pe.wait_ge(attn_q, 2 * i + u + 1)
                    for j in range(8):
                        ins = mm(bank(u, 0, 2)[:, j * TILE:(j + 1) * TILE], WK[:, j * 128:(j + 1) * 128], XFT[:, u, :])
                    ins.then_inc(attn_k_proj, 1)

            def values(i):
                for u in (0, 1):
                    pe.wait_ge(attn_k, 2 * i + u + 1)
                    for b in (0, 1):
                        for o in (0, 1):
                            ins = mm(ps[HALF * o:HALF * (o + 1), 4 * u + b, :],
                                     XFT[:, u, HALF * b:HALF * (b + 1)], WV[:, o, :])
                    ins.then_inc(attn_v_proj, 1)

            def self_attention(i, last=False):
                for u in (0, 1):
                    pe.wait_ge(attn_qf, 2 * i + u + 1)
                    apart(pe)
                    for h in range(HEADS):
                        lo = 64 * (h % 2)
                        for b in (0, 1):
                            ins = mm(bank(u, 2 + h % 2)[HALF * b:HALF * (b + 1), h // 2 * HALF:h // 2 * HALF + S],
                                     qT[lo:lo + DH, u, h // 2, HALF * b:HALF * (b + 1)],
                                     kT[lo:lo + DH, u, h // 2, HALF * b:HALF * b + S])
                    ins.then_inc(attn_scores, 1)
                pe.wait_ge(attn_v, 2 * i + 2)
                apart(pe)
                if not last:
                    projected(i + 1)
                    pe.wait_ge(attn_k, 2 * i + 4)
                    apart(pe)
                for u in (0, 1):
                    pe.wait_ge(attn_probs, 2 * i + u + 1)
                    transposed(u, [P[:, u, 2 * j:2 * j + 2, :].rearrange("p a b -> p (a b)") for j in range(8)],
                               bank(u, 0, 2)).then_inc(attn_probsT, 1)
                for u in (0, 1):
                    pe.wait_ge(attn_pT, 2 * i + u + 1)
                    apart(pe)
                    for h in range(HEADS):
                        lo, j = 64 * (h % 2), h // 2
                        for b in (0, 1):
                            at = j * TILE + HALF * b
                            ins = mm(bank(u, 2, 2)[lo:lo + DH, at:at + HALF],
                                     V[lo:lo + S, u, b, j * DH:(j + 1) * DH],
                                     PT[lo:lo + S, u, j, HALF * b:HALF * (b + 1)])
                    ins.then_inc(attn_pv, 1)
                pe.wait_ge(load_rest_w, 160)
                for u in (0, 1):
                    pe.wait_ge(attn_o, 2 * i + u + 1)
                    for j in range(8):
                        ins = mm(bank(u, 2)[:, 0:D], OT[:, u, j, :], WO[:, j, :], start=j == 0, stop=j == 7)
                    ins.then_inc(attn_proj, 1)
                if not last:
                    values(i + 1)
                pe.wait_ge(attn_normed2, i + 1)
                for u in (0, 1):
                    transposed(u, [XN[:, u, :]], bank(u, 3)).then_inc(attn_xT2, 1)
                for u in (0, 1):
                    pe.wait_ge(attn_xnT2, 2 * i + u + 1)
                    for n in range(XG):
                        ins = mm(bank(u, 2, 2)[0:STACK, n * TILE:(n + 1) * TILE], WQS[:, n, :], XNT[:, u, :])
                    ins.then_inc(attn_stack, 1)

            projected(0)
            values(0)
            with pe.Fori(0, N2 - 1) as i:
                self_attention(i)
            self_attention(N2 - 1, True)

            def turned(i):
                for u in (0, 1):
                    pe.wait_ge(tail_copied, 2 * i + u + 1)
                    transposed(u, [PF[:, u, j, :] for j in range(4)], ps[:, 5 + u, :]).then_inc(tail_turned, 1)

            def heads_turned(i):
                pe.wait_ge(tail_ctx, 2 * i + 2)
                for u in (0, 1):
                    ins = transposed(u, [CN[:, u, :]], ps[:, 5, u * TILE:(u + 1) * TILE])
                ins.then_inc(tail_ctxT, 1)

            def heads_projected(i):
                pe.wait_ge(tail_ctxS, i + 1)
                for u in (0, 1):
                    ins = mm(ps[:, 6, u * D:(u + 1) * D], CNT[:, u, :], XWO[:, :])
                ins.then_inc(tail_proj, 1)

            def tokens_turned(i):
                pe.wait_ge(tail_normed, i + 1)
                for u in (0, 1):
                    ins = transposed(u, [XN[:, u, :]], ps[:, 5, u * TILE:(u + 1) * TILE])
                ins.then_inc(tail_xT, 1)

            def logits(i):
                pe.wait_ge(tail_xnT, i + 1)
                for u in (0, 1):
                    ins = mm(ps[:, 7, 2 * TILE + u * E:2 * TILE + (u + 1) * E], XNT[:, u, :], GW)
                ins.then_inc(tail_logits, 1)

            ins_ = (cross_in0, cross_in1, cross_in2)

            def project_k(turn, u, n):
                pe.wait_ge((cross_ctx0, cross_ctx1)[u], 16 * (turn + 1))
                mm(ps[:, 7, 0:KC], XWK[:, :], CX[u][:, n * KC:(n + 1) * KC]).then_inc(cross_k_proj, 1)

            def project_v(b, u, n):
                for j in range(4):
                    kt = 4 * n + j
                    ins = mm(ps[0:KN, 7, j * D:(j + 1) * D], CX[u][:, kt * KN:(kt + 1) * KN], XWV[:, :])
                ins.then_inc(cross_v_proj, 1)

            def first_scores(b, u, q):
                n, h = q // XG, q % XG
                if h == 0:
                    pe.wait_ge(ins_[n], 16 * len(K_RUNS) * (b + 1))
                if not (isinstance(b, int) and b == 0 and q < 2):
                    pe.wait_ge(cross_top, THIRDS * XG * b + q - 1)
                mm(ps[0:XQ, 5 + q % 2, 0:KC], QS[0:STACK, b, h, :], KS[u][0:STACK, h, n * KC:(n + 1) * KC])\
                    .then_inc(cross_smax, 1)

            def shift_row(b):
                pe.wait_ge(cross_negated, b + 1)
                for h in range(XG):
                    ins = mm(ps[SHIFT:SHIFT + 1, 5 + h // 4, (h % 4) * XQ:(h % 4 + 1) * XQ],
                             CB[0:XQ, h:h + 1], identb[0:XQ, 0:XQ])
                ins.then_inc(cross_shift, 1)

            def scores(b, u, kt):
                if kt == 0:
                    pe.wait_ge(cross_shifted, b + 1)
                for h in range(XG):
                    ins = mm(ps[0:KN, 2 * (kt % 2) + h // 4, (h % 4) * XQ:(h % 4 + 1) * XQ],
                             KS[u][0:SHIFT + 1, h, kt * KN:(kt + 1) * KN], QS[0:SHIFT + 1, b, h, :])
                ins.then_inc(cross_scores, 1)

            def outputs(b, u, kt):
                pe.wait_ge(cross_probs, KT * b + kt + 1)
                if kt in (0, 4):
                    pe.wait_ge(cross_v, THIRDS * b + (2 if kt == 0 else 3))
                if kt == 0:
                    pe.wait_ge(cross_o, b + 1)
                for h in range(XG):
                    ins = mm(ps[32 * (h % 4):32 * (h % 4) + 32, 4, (h // 4) * XQ:(h // 4 + 1) * XQ],
                             VX[u][0:KN, kt, h * VW:h * VW + 32], PX[kt % 2][0:KN, h, :],
                             start=kt == 0 and h < 4, stop=kt == KT - 1, skip_group_check=True)
                ins.then_inc(cross_pv, 1)

            def cross(turn, u, next_too=True, second_too=True):
                b = 2 * turn + u
                q = 0
                for kt in range(KT):
                    if kt > 0:
                        scores(b, u, kt)
                    if next_too and FIRST[kt]:
                        first_scores(b + 1, 1 - u, q)
                        q += 1
                    if next_too and kt % 4 == 1:
                        pe.wait_ge(cross_kf, THIRDS * (b + 2) + (kt // 4 if second_too else 0))
                        project_v(b + 1, 1 - u, kt // 4)
                    if second_too and kt % 4 == 3:
                        pe.wait_ge(cross_v, THIRDS * (b + 1) + kt // 4 + 1)
                        project_k(turn + 1, u, kt // 4)
                    if next_too and FIRST[kt] == 3:
                        first_scores(b + 1, 1 - u, q)
                        q += 1
                    if kt > 0:
                        outputs(b, u, kt - 1)
                    if next_too and FIRST[kt]:
                        first_scores(b + 1, 1 - u, q)
                        q += 1
                    if next_too and kt == KT - 2:
                        shift_row(b + 1)
                    if not next_too:
                        if kt == 1:
                            turned(0)
                        elif kt == 6:
                            heads_turned(0)
                        elif kt == 8:
                            heads_projected(0)
                if next_too:
                    pe.wait_ge(load_ones, 48)
                    scores(b + 1, 1 - u, 0)
                outputs(b, u, KT - 1)

            pe.wait_ge(attn_qf, PAIRS + 2)
            for n in range(THIRDS):
                if n:
                    pe.wait_ge(cross_kf, n)
                project_k(0, 0, n)
            for n in range(THIRDS):
                pe.wait_ge(cross_kf, THIRDS + n)
                if n:
                    pe.wait_ge(cross_v, n)
                project_v(0, 0, n)
                pe.wait_ge(cross_v, n + 1)
                project_k(0, 1, n)
                pe.wait_ge(attn_qstack, PAIRS)
                for q in range(n * XG, (n + 1) * XG):
                    first_scores(0, 0, q)
            shift_row(0)
            pe.wait_ge(load_ones, 32)
            scores(0, 0, 0)
            with pe.Fori(0, PAIRS - 1) as p:
                cross(p, 0)
                cross(p, 1)
            cross(PAIRS - 1, 0, second_too=False)
            cross(PAIRS - 1, 1, next_too=False, second_too=False)


            def experts(i, more=True):
                first = i * E * K0
                for e in range(E + 1):
                    if e < E:
                        if e >= 3:
                            pe.wait_ge(tail_gelu, first + 1 + K0 * (e - 2))
                        for k in range(K0):
                            mm(ps[:, e % 3, k * 2 * TILE:(k + 1) * 2 * TILE],
                               FW1[:, e, k * 128:(k + 1) * 128], XNTA[:, bass.ds(2 * i, 2), :]).then_inc(tail_h, 1)
                    if e == 1 and more:
                        turned(i + 1)
                    if e == 3:
                        pe.wait_ge(tail_coef, i + 1)
                        for u in (0, 1):
                            ins = nc.tensor.transpose(ps[0:E, 7, u * TILE:(u + 1) * TILE], coef[:, u, :], ident)
                        ins.then_inc(tail_coefT, 1)
                    if e == 4:
                        pe.wait_ge(tail_coefS, i + 1)
                        for u in (0, 1):
                            ins = mm(ps[:, 7, u * D:(u + 1) * D], coefT[0:E, u, :], FB2[0:E, :])
                        ins.then_inc(tail_b2, 1)
                    if e == 5 and more:
                        heads_turned(i + 1)
                    if e == 6 and more:
                        heads_projected(i + 1)
                    if e == E and more:
                        tokens_turned(i + 1)
                    if e > 0:
                        y = e - 1
                        pe.wait_ge(tail_gelu, first + 1 + K0 * e)
                        if y == 0:
                            pe.wait_ge(tail_acc, 2 * E * i + 1)
                        elif y >= 4 and y % 2 == 0:
                            pe.wait_ge(tail_acc, 2 * E * i + 1 + 2 * (y - 2))
                        for u in (0, 1):
                            for k in range(K0):
                                ins = mm(ps[:, 3 + y // 2 % 2, (2 * (y % 2) + u) * D:(2 * (y % 2) + u + 1) * D],
                                         HB[:, y % 2 * K0 + k, u * TILE:(u + 1) * TILE],
                                         FW2[:, y * K0 + k, :], start=k == 0, stop=k == K0 - 1)
                            ins.then_inc(tail_y, 1)
                if more:
                    logits(i + 1)

            pe.wait_ge(load_middle_w, 128)
            tokens_turned(0)
            logits(0)
            with pe.Fori(0, N2 - 1) as i:
                experts(i)
            experts(N2 - 1, False)

            def mqa_turned_x(i):
                pe.wait_ge(mqa_scaled, i + 1)
                for u in (0, 1):
                    transposed(u, [KX[:, u, :]], bank(u, 0)).then_inc(mqa_xT, 1)

            def mqa_projected(i):
                for u in (0, 1):
                    pe.wait_ge(mqa_xnT, 2 * i + u + 1)
                    mm(bank(u, 0), XNT[:, u, :], MWQ)
                    mm(bank(u, 1)[:, 0:2 * DH], XNT[:, u, :], MWKV).then_inc(mqa_qkv, 1)

            def mqa(i, last=False):
                for u in (0, 1):
                    pe.wait_ge(mqa_qn, 2 * i + u + 1)
                    transposed(u, [T1[:, u, j * 128:(j + 1) * 128] for j in range(4)], bank(u, 1))
                    transposed(u, [T1[:, u, 512:640]], bank(u, 3)).then_inc(mqa_turned, 1)
                for u in (0, 1):
                    pe.wait_ge(mqa_qT, 2 * i + u + 1)
                    pe.wait_ge(mqa_kT, 2 * i + u + 1)
                    apart(pe)
                    for b in (0, 1):
                        for o in (0, 1):
                            rhs = T2[64 * o:64 * o + DH, u, 0:512].rearrange("p (j n) -> p j n", n=TILE)
                            ins = mm(bank(u, o)[HALF * b:HALF * (b + 1), 0:4 * HALF],
                                     T2[64 * o:64 * o + DH, u, 512 + HALF * b:512 + HALF * (b + 1)],
                                     rhs[:, :, HALF * b:HALF * (b + 1)])
                    ins.then_inc(mqa_scores, 1)
                pe.wait_ge(mqa_normed2, i + 1)
                apart(pe)
                for u in (0, 1):
                    pe.wait_ge(mqa_probs, 2 * i + u + 1)
                    pe.wait_ge(mqa_v, 2 * i + u + 1)
                    apart(pe)
                    for b in (0, 1):
                        for h in range(H1):
                            at = 256 * (h % 2) + HALF * (h // 2)
                            ins = mm(heads4(u, 1, 2)[HALF * b:HALF * (b + 1), h // 4, h % 4, :],
                                     T3[HALF * b:HALF * b + S, u, at:at + HALF],
                                     VM[HALF * b:HALF * b + S, u, 0, :])
                    ins.then_inc(mqa_pv, 1)
                if not last:
                    mqa_turned_x(i + 1)
                for u in (0, 1):
                    pe.wait_ge(mqa_o, 2 * i + u + 1)
                    transposed(u, [T1[:, u, j * 128:(j + 1) * 128] for j in range(4)], bank(u, 3)).then_inc(mqa_oT, 1)
                if not last:
                    mqa_projected(i + 1)
                for u in (0, 1):
                    pe.wait_ge(mqa_oS, 2 * i + u + 1)
                    for j in range(4):
                        ins = mm(bank(u, 2)[:, 0:D], T2[:, u, j * 128:(j + 1) * 128], MWO[:, j, :],
                                 start=j == 0, stop=j == 3)
                    ins.then_inc(mqa_proj, 1)

            pe.wait_ge(tail_acc, 2 * E * N2 + 1)
            mqa_turned_x(0)
            mqa_projected(0)
            with pe.Fori(0, N2 - 1) as i:
                mqa(i)
            mqa(N2 - 1, True)

            def by_heads(u, k, w, tokens):
                for j in range(8):
                    ins = mm(bank(u, k, 2)[:, j * TILE:(j + 1) * TILE], w[:, j * 128:(j + 1) * 128], tokens[:, u, :])
                return ins

            def rope_q(i):
                pe.wait_ge(rope_scaled, i + 1)
                for u in (0, 1):
                    transposed(u, [XN[:, u, :], KX[:, u, :]], bank(u, 0)).then_inc(rope_xT, 1)
                for u in (0, 1):
                    pe.wait_ge(rope_xnT, 2 * i + u + 1)
                    by_heads(u, 0, RWQ, XNT).then_inc(rope_qproj, 1)

            def rope(i, last=False):
                pe.wait_ge(rope_steps, 5 * i + 1)
                apart(pe)
                for u in (0, 1):
                    by_heads(u, 2, RWQR, XNT).then_inc(rope_qproj, 1)
                for u in (0, 1):
                    pe.wait_ge(rope_parts, 6 * i + 2 + u + 1)
                    by_heads(u, 0, RWK, KXT)
                    by_heads(u, 2, RWKR, KXT).then_inc(rope_kproj, 1)
                for u in (0, 1):
                    pe.wait_ge(rope_parts, 6 * i + 4 + u + 1)
                    for k in (0, 1):
                        ins = mm(bank(u, k), KXT[:, u, :], RWV[:, k * 512:(k + 1) * 512])
                    ins.then_inc(rope_v_proj, 1)
                for u in (0, 1):
                    pe.wait_ge(rope_qT, 2 * i + u + 1)
                    pe.wait_ge(rope_kT, 2 * i + u + 1)
                    apart(pe)
                    for h in range(HEADS):
                        lo, at = 64 * (h % 2), (h // 2) * TILE
                        for b in (0, 1):
                            ins = mm(bank(u, 2 + h % 2)[HALF * b:HALF * (b + 1), h // 2 * HALF:(h // 2 + 1) * HALF],
                                     T3[lo:lo + DH, u, at + HALF * b:at + HALF * (b + 1)],
                                     T1[lo:lo + DH, u, at + HALF * b:at + HALF * (b + 1)])
                    ins.then_inc(rope_scores, 1)
                pe.wait_ge(rope_v, 2 * i + 2)
                apart(pe)
                if not last:
                    rope_q(i + 1)
                for u in (0, 1):
                    if not last:
                        pe.wait_ge(rope_parts, 6 * i + 6 + u + 1)
                        apart(pe)
                    pe.wait_ge(rope_masked, 2 * i + u + 1)
                    apart(pe)
                    for b in (0, 1):
                        for h in range(HEADS):
                            ins = mm(heads4(u, 0, 4)[HALF * b:HALF * (b + 1), h // 4, h % 4, :],
                                     T2[HALF * b:HALF * b + S, u, 512 * (h % 2) + HALF * (h // 2):
                                        512 * (h % 2) + HALF * (h // 2 + 1)],
                                     VM[HALF * b:HALF * b + S, u, h, :])
                    ins.then_inc(rope_pv, 1)
                for u in (0, 1):
                    pe.wait_ge(rope_o, 2 * i + u + 1)
                    transposed(u, [T4[:, u, j * 128:(j + 1) * 128] for j in range(8)], bank(u, 0, 2)).then_inc(rope_oT, 1)
                for u in (0, 1):
                    pe.wait_ge(rope_oS, 2 * i + u + 1)
                    for j in range(8):
                        ins = mm(bank(u, 2)[:, 0:D], T3[:, u, j * 128:(j + 1) * 128], RWO[:, j, :],
                                 start=j == 0, stop=j == 7)
                    ins.then_inc(rope_out, 1)

            pe.wait_ge(mqa_normed2, N2 + 1)
            pe.wait_ge(load_late_w, 96)
            rope_q(0)
            with pe.Fori(0, N2 - 1) as i:
                rope(i)
            rope(N2 - 1, True)

            for k in (0, 1):
                pe.wait_ge(moe_normed, k + 1)
                transposed(k, [XA[:, 4 * k + j, :] for j in range(4)], bank(k, 0)).then_inc(moe_xT, 1)
            for k in (0, 1):
                pe.wait_ge(moe_xnT, k + 1)
                for t in range(4 * k, 4 * k + 4):
                    ins = mm(ps[:, 1, t * E:(t + 1) * E], XNTA[:, t, :], LW)
            ins.then_inc(moe_logits, 1)
            pe.wait_ge(moe_picked, 1)
            mm(ps[:, 2, 0:PAIRS * E], CT[:, C_TRI:C_TRI + 128], PICK.rearrange("p a b -> p (a b)"), stop=False)
            for t in range(PAIRS - 1):
                ins = mm(ps[:, 2, (t + 1) * E:PAIRS * E], CT[:, C_ONES:C_ONES + 128],
                         over(PICK[:, t, :], PAIRS - 1 - t), start=False, stop=t == PAIRS - 2)
            ins.then_inc(moe_count, 1)

            for t in range(PAIRS):
                pe.wait_ge(last_onehot, t + 1)
                for at in range(0, E * SLOTS, 512):
                    n = min(512, E * SLOTS - at)
                    ins = mm(ps[:, at // 512, 0:n], XA[:, t, :], ONEHOT[:, t % 2, at:at + n], start=t == 0, stop=t == PAIRS - 1)
                ins.then_inc(last_read, 1)
            pe.wait_ge(last_copied, 3)
            for e in range(E + 1):
                if e < E:
                    if e >= 2:
                        pe.wait_ge(last_gelu, K1 * (e - 1))
                    for k in range(K1):
                        mm(ps[:, 4 + 2 * (e % 2) + k // 2, k % 2 * SLOTS:(k % 2 + 1) * SLOTS],
                           LW1[:, e, k * 128:(k + 1) * 128], XTS[:, e * SLOTS:(e + 1) * SLOTS]).then_inc(last_h, 1)
                if e > 0:
                    y = e - 1
                    pe.wait_ge(last_gelu, K1 * e)
                    if y >= 3:
                        pe.wait_ge(last_acc, y - 2)
                    for j, (chunk, row, n, first) in enumerate(pieces(y)):
                        for k in range(K1):
                            ins = mm(ps[row:row + n, y % 3, j * D:(j + 1) * D], HG[:, y % 2, k, first:first + n],
                                     LW2[:, y * K1 + k, :], start=k == 0, stop=k == K1 - 1)
                    ins.then_inc(last_y, 1)
            pe.wait_ge(last_acc, E)

            def bring_back(i):
                for u in (0, 1):
                    pe.wait_ge(last_onehot, PAIRS + 4 * i + 2 * u + 2)
                    pe.wait_ge(last_copied, 3 + 2 * i + u - 1)
                    transposed(u, [ONEHOT[:, u, c * 128:(c + 1) * 128] for c in range(CHUNKS)], bank(u, 0, 3))\
                        .then_inc(last_read, 1)
                for u in (0, 1):
                    pe.wait_ge(last_copied, 3 + 2 * i + u + 1)
                    pe.wait_ge(last_acc, E + 2 * i + u - 1)
                    for c in range(CHUNKS):
                        ins = mm(bank(u, 3)[:, 0:D], PT2[:, u, c, :], OUTS[:, c, :], start=c == 0, stop=c == CHUNKS - 1)
                    ins.then_inc(last_y, 1)

            with pe.Fori(0, N2) as i:
                bring_back(i)

        @block.scalar
        def _(act):
            def copy(dst, src, **kw):
                return nc.scalar.activation(dst, src, ACT.Copy, **kw)

            def first_parts(i):
                for u in (0, 1):
                    act.wait_ge(attn_qf, 2 * i + u + 3)
                    copy(q1[0:STACK, u], qf[0:STACK, u], scale=CT[0:STACK, C_MASK1:C_MASK1 + 1]).then_inc(attn_q1, 1)

            def second_parts(i):
                for u in (0, 1):
                    act.wait_ge(attn_r1, 2 * i + u + 1)
                    copy(q2[0:STACK, u], qf[0:STACK, u], scale=CT[0:STACK, C_MASK2:C_MASK2 + 1]).then_inc(attn_q2, 1)

            def stacks(i):
                for u in (0, 1):
                    act.wait_ge(attn_r2, 2 * i + u + 1)
                    for b in (0, 1):
                        for h in (0, 1):
                            ins = nc.scalar.activation(QS[0:STACK, 4 * i + 2 * u + b, :, h * S:(h + 1) * S],
                                                       qf[0:STACK, u, :, HALF * b:HALF * b + S], ACT.Copy,
                                                       scale=CT[0:STACK, C_BLK + h:C_BLK + h + 1])
                    ins.then_inc(attn_qstack, 1)

            def take_tokens(i):
                for u in (0, 1):
                    act.wait_ge(attn_xT, 2 * i + u + 1)
                    copy(XFT[:, u, :], bank(u, 0)[:, 0:TILE]).then_inc(attn_xnT, 1)

            def take_q(i, u):
                act.wait_ge(attn_q_proj, 2 * i + u + 1)
                copy(qT[:, u].rearrange("p a b -> p (a b)"), bank(u, 0, 2)).then_inc(attn_q, 1)

            def take_attn_k(i):
                for u in (0, 1):
                    act.wait_ge(attn_k_proj, 2 * i + u + 1)
                    copy(kT[:, u].rearrange("p a b -> p (a b)"), bank(u, 0, 2)).then_inc(attn_k, 1)

            def take_attn_v(i, u):
                act.wait_ge(attn_v_proj, 2 * i + u + 1)
                copy(V[:, u].rearrange("p a b -> p (a b)"), bank(u, 0, 2)).then_inc(attn_v, 1)

            def self_attention(i, first=False, last=False):
                if not first:
                    first_parts(i - 1)
                if not last:
                    take_tokens(i + 1)
                for u in (0, 1):
                    act.wait_ge(attn_shifted, 2 * i + u + 1)
                    nc.scalar.activation(P[:, u, :, 0:S], P[:, u, :, 0:S], ACT.Exp, scale=DH ** -0.5)\
                        .then_inc(attn_expd, 1)
                    if not last:
                        take_q(i + 1, u)
                if not last:
                    take_attn_k(i + 1)
                if not first:
                    second_parts(i - 1)
                for u in (0, 1):
                    act.wait_ge(attn_probsT, 2 * i + u + 1)
                    copy(PT[:, u].rearrange("p a b -> p (a b)"), bank(u, 0, 2)).then_inc(attn_pT, 1)
                if not first:
                    stacks(i - 1)
                for u in (0, 1):
                    act.wait_ge(attn_pv, 2 * i + u + 1)
                    copy(OT[:, u].rearrange("p a b -> p (a b)"), bank(u, 2, 2)).then_inc(attn_o, 1)
                if not last:
                    take_attn_v(i + 1, 0)
                for u in (0, 1):
                    act.wait_ge(attn_xT2, 2 * i + u + 1)
                    copy(XNT[:, u, :], bank(u, 3)[:, 0:TILE]).then_inc(attn_xnT2, 1)
                if not last:
                    take_attn_v(i + 1, 1)
            act.wait_ge(load_consts, 16)
            for counted in (cross_o, tail_gelu):
                act.sem_inc(counted, 1)
            take_tokens(0)
            for u in (0, 1):
                take_q(0, u)
            take_attn_k(0)
            for u in (0, 1):
                take_attn_v(0, u)
            self_attention(0, first=True)
            with act.Fori(1, N2 - 1) as i:
                self_attention(i)
            self_attention(N2 - 1, last=True)

            def take_k(b, u, n):
                act.wait_ge(cross_k_proj, THIRDS * b + n + 1)
                bias = PC[:, P_BK:P_BK + 1]
                if not (isinstance(b, int) and b == 0):
                    act.wait_ge((cross_out0, cross_out1, cross_out2)[n], 16 * b)
                nc.scalar.activation(kp[:, n, 0, :], ps[:, 7, 0:KC], ACT.Identity, bias=bias)
                nc.scalar.activation(kf[:, n, :], ps[:, 7, 0:KC], ACT.Identity, bias=bias).then_inc(cross_kf, 1)

            def take_shift(b):
                act.wait_ge(cross_shift, b + 1)
                copy(QS[SHIFT:SHIFT + 1, b, :, :].rearrange("p (a h) q -> p a (h q)", a=2),
                     ps[SHIFT:SHIFT + 1, 5:7, 0:4 * XQ]).then_inc(cross_shifted, 1)

            def heads_kept(i):
                act.wait_ge(tail_ctxT, i + 1)
                copy(CNT.rearrange("p a b -> p (a b)"), ps[:, 5, 0:2 * TILE]).then_inc(tail_ctxS, 1)

            def exponentials(b, kt):
                act.wait_ge(cross_scores, KT * b + kt + 1)
                nc.scalar.activation(PX[kt % 2][0:KN].rearrange("p (a h) q -> p a (h q)", a=2),
                                     ps[0:KN, 2 * (kt % 2):2 * (kt % 2) + 2, 0:4 * XQ],
                                     ACT.Exp, scale=XD ** -0.5).then_inc(cross_probs, 1)

            def cross(b, u, t_, next_too=True, second_too=True):
                for kt in range(KT):
                    if kt > 0:
                        exponentials(b, kt)
                    if second_too and kt % 4 == 3:
                        take_k(b + 2, u, kt // 4)
                    if next_too and kt == KT - 2:
                        take_shift(b + 1)
                    if not next_too and kt == 6:
                        heads_kept(0)
                if next_too:
                    exponentials(b + 1, 0)
                act.wait_ge(cross_pv, KT * b + KT)
                copy(PO[:, t_, :, :, HALF * u:HALF * u + S],
                     ps[:, 4, 0:2 * XQ].rearrange("p (j h q) -> p j h q", j=2, h=2)).then_inc(cross_o, 1)

            take_k(0, 0, 0)
            first_parts(N2 - 1)
            take_k(0, 0, 1)
            second_parts(N2 - 1)
            take_k(0, 0, 2)
            stacks(N2 - 1)
            for n in range(THIRDS):
                take_k(1, 1, n)
            act.wait_ge(cross_cleared, 4)
            take_shift(0)
            exponentials(0, 0)
            with act.Fori(0, PAIRS - 1) as p:
                cross(2 * p, 0, p)
                cross(2 * p + 1, 1, p)
            cross(B - 2, 0, PAIRS - 1, second_too=False)
            cross(B - 1, 1, PAIRS - 1, next_too=False, second_too=False)

            def tokens_kept(i):
                act.wait_ge(tail_xT, i + 1)
                copy(XNTA[:, bass.ds(2 * i, 2), :].rearrange("p a b -> p (a b)"), ps[:, 5, 0:2 * TILE])
                copy(XNT[:, :, :].rearrange("p a b -> p (a b)"), ps[:, 5, 0:2 * TILE]).then_inc(tail_xnT, 1)
                act.wait_ge(tail_shifted, i + 1)
                nc.scalar.activation(sm[:, :, 8:16], sm[:, :, 0:8], ACT.Exp).then_inc(tail_expd, 1)

            def experts(i, more=True):
                for e in range(E):
                    act.wait_ge(tail_y, 2 * E * i + 1 + 2 * max(e - 1, 0))
                    act.wait_ge(tail_h, i * E * K0 + K0 * (e + 1))
                    apart(act)
                    for k in range(K0):
                        nc.scalar.activation(HB[:, e % 2 * K0 + k, :], ps[:, e % 3, k * 2 * TILE:(k + 1) * 2 * TILE], ACT.Gelu,
                                             bias=PC[:, P_B1 + e * K0 + k:P_B1 + e * K0 + k + 1]).then_inc(tail_gelu, 1)
                    if e == 3:
                        act.wait_ge(tail_coefT, i + 1)
                        copy(coefT[0:E].rearrange("p a b -> p (a b)"), ps[0:E, 7, 0:2 * TILE]).then_inc(tail_coefS, 1)
                    if e == 5 and more:
                        heads_kept(i + 1)
                if more:
                    tokens_kept(i + 1)

            tokens_kept(0)
            with act.Fori(0, N2 - 1) as i:
                experts(i)
            experts(N2 - 1, False)

            def mqa_tokens(i):
                for u in (0, 1):
                    act.wait_ge(mqa_xT, 2 * i + u + 1)
                    copy(XNT[:, u, :], bank(u, 0)[:, 0:TILE]).then_inc(mqa_xnT, 1)

            def mqa_squares(i):
                for u in (0, 1):
                    act.wait_ge(mqa_qkv, 2 * i + u + 1)
                    nc.scalar.activation(T3[:, u, 0:512], bank(u, 0), ACT.Square, scale=16.0)
                    nc.scalar.activation(T3[:, u, 512:576], bank(u, 1)[:, 0:DH], ACT.Square).then_inc(mqa_sq, 1)
                    copy(VM[:, u, 0, 0:DH], bank(u, 1)[:, DH:2 * DH]).then_inc(mqa_v, 1)

            def mqa(i, last=False):
                for u in (0, 1):
                    act.wait_ge(mqa_turned, 2 * i + u + 1)
                    copy(T2[:, u, 0:512], bank(u, 1)).then_inc(mqa_qT, 1)
                for u in (0, 1):
                    act.wait_ge(mqa_scores, 2 * i + u + 1)
                    nc.scalar.activation(T3[:, u, 0:512].rearrange("p (o n) -> p o n", o=2),
                                         bank(u, 0, 2).rearrange("p (o n) -> p o n", o=2)[:, :, 0:4 * HALF], ACT.Exp)\
                        .then_inc(mqa_probs, 1)
                if not last:
                    mqa_tokens(i + 1)
                for u in (0, 1):
                    act.wait_ge(mqa_oT, 2 * i + u + 1)
                    copy(T2[:, u, 0:512], bank(u, 3)).then_inc(mqa_oS, 1)
                if not last:
                    mqa_squares(i + 1)

            mqa_tokens(0)
            mqa_squares(0)
            with act.Fori(0, N2 - 1) as i:
                mqa(i)
            mqa(N2 - 1, True)

            def rope_tokens(i):
                for u in (0, 1):
                    act.wait_ge(rope_xT, 2 * i + u + 1)
                    copy(XNT[:, u, :], bank(u, 0)[:, 0:TILE])
                    copy(KXT[:, u, :], bank(u, 0)[:, TILE:2 * TILE]).then_inc(rope_xnT, 1)

            def rope(i, last=False):
                for u in (0, 1):
                    act.wait_ge(rope_v_proj, 2 * i + u + 1)
                    copy(VM[:, u, :, 0:DH], bank(u, 0, 2).rearrange("p (h w) -> p h w", w=DH)).then_inc(rope_v, 1)
                for u in (0, 1):
                    act.wait_ge(rope_scores, 2 * i + u + 1)
                    nc.scalar.activation(T2[:, u, :], bank(u, 2, 2), ACT.Tanh, scale=DH ** -0.5 / GROK).then_inc(rope_tanh, 1)
                    if u == 0 and not last:
                        rope_tokens(i + 1)
                for u in (0, 1):
                    act.wait_ge(rope_tanh, 2 * i + u + 1)
                    nc.scalar.activation(T2[:, u, :], T2[:, u, :], ACT.Exp, scale=GROK).then_inc(rope_expd, 1)
                for u in (0, 1):
                    act.wait_ge(rope_oT, 2 * i + u + 1)
                    copy(T3[:, u, :], bank(u, 0, 2)).then_inc(rope_oS, 1)

            rope_tokens(0)
            with act.Fori(0, N2 - 1) as i:
                rope(i)
            rope(N2 - 1, True)

            for k in (0, 1):
                act.wait_ge(moe_xT, k + 1)
                copy(XNTA[:, 4 * k:4 * k + 4, :].rearrange("p a b -> p (a b)"), bank(k, 0)).then_inc(moe_xnT, 1)
            act.wait_ge(tail_shifted, N2 + 1)
            nc.scalar.activation(EX, LG, ACT.Exp).then_inc(tail_expd, 1)

            act.wait_ge(last_read, PAIRS)
            for at in range(0, E * SLOTS, 512):
                n = min(512, E * SLOTS - at)
                copy(XTS[:, at:at + n], ps[:, at // 512, 0:n]).then_inc(last_copied, 1)
            for e in range(E):
                if e >= 2:
                    act.wait_ge(last_y, e - 1)
                for k in range(K1):
                    if k % 2 == 0:
                        act.wait_ge(last_h, K1 * e + k + 2)
                    nc.scalar.activation(HG[:, e % 2, k, :], ps[:, 4 + 2 * (e % 2) + k // 2, k % 2 * SLOTS:(k % 2 + 1) * SLOTS],
                                         ACT.Gelu, bias=PC[:, P_B1L + K1 * e + k:P_B1L + K1 * e + k + 1]).then_inc(last_gelu, 1)
            with act.Fori(0, N2) as i:
                for u in (0, 1):
                    act.wait_ge(last_read, PAIRS + 2 * i + u + 1)
                    copy(PT2[:, u].rearrange("p c n -> p (c n)"), bank(u, 0, 3)[:, 0:E * SLOTS]).then_inc(last_copied, 1)

        @block.gpsimd
        def _(pool):
            pool.wait_ge(load_consts, 16)
            for nth in (0, 1):
                ln_pool(pool, nth)
            nc.gpsimd.memset(ones[:, :], 1.0).then_inc(cross_cleared, 1)
            for u in (0, 1):
                nc.gpsimd.memset(VX[u], 1.0).then_inc(cross_cleared, 1)
            nc.gpsimd.memset(PO[:, :, :, :, :], 1.0).then_inc(cross_cleared, 1)

            def self_attention(i, ahead=True, last=False):
                ln_pool(pool, 2 * i + (1 if last else 2))
                if ahead:
                    ln_pool(pool, 2 * i + 3)
                if not last:
                    for part, made, left in ((q1, attn_q1, attn_r1), (q2, attn_q2, attn_r2)):
                        q_residual(pool, nc.gpsimd, i, part, made, left)

            with pool.Fori(0, N2 - 2) as i:
                self_attention(i)
            self_attention(N2 - 2, ahead=False)
            self_attention(N2 - 1, ahead=False, last=True)

            for n in range(THIRDS):
                split_k(pool, nc.gpsimd, 1, n)
            with pool.Fori(2, B) as b:
                for n in range(THIRDS):
                    split_k(pool, nc.gpsimd, b, n)

            def tail(i, first=False):
                for u in (0, 1):
                    if not first:
                        pool.wait_ge(tail_turned, 2 * i + u - 1)
                    nc.gpsimd.tensor_copy(PF[:, u].rearrange("p a b -> p (a b)"),
                                          PO[:, 2 * i + u].rearrange("p a b c -> p (a b c)")).then_inc(tail_copied, 1)
                ln_pool(pool, LN_T + i)

            pool.wait_ge(cross_o, 4 + 1)
            tail(0, True)
            pool.wait_ge(cross_o, B + 1)
            with pool.Fori(1, N2) as i:
                tail(i)

            def roots(i):
                for u in (0, 1):
                    pool.wait_ge(mqa_ss, 2 * i + u + 1)
                    nc.gpsimd.tensor_tensor(sm[:, u, 16:25], sm[:, u, 0:9], CT[:, C_HALF:C_HALF + 9], ALU.pow)\
                        .then_inc(mqa_root, 1)

            def mqa(i, last=False):
                for k in range(3 if last else 2):
                    ln_pool(pool, LN_M + 3 * i + 2 + k)
                if not last:
                    roots(i + 1)
                ln_pool(pool, LN_M + 3 * i + (5 if last else 4))

            for k in (0, 1):
                ln_pool(pool, LN_M + k)
            roots(0)
            with pool.Fori(0, N2 - 1) as i:
                mqa(i)
            mqa(N2 - 1, True)

            def rope(i, last=False):
                for into, other, k, done in ((T1, T2, 2, rope_qT), (T3, T4, 4, rope_kT)):
                    for u in (0, 1):
                        pool.wait_ge(rope_parts, 6 * i + k + u + 1)
                        nc.gpsimd.tensor_tensor(into[:, u, :], into[:, u, :], other[:, u, :], ALU.add).then_inc(done, 1)
                if not last:
                    for k in range(3):
                        ln_pool(pool, LN_R + 3 * i + 3 + k)
                for u in (0, 1):
                    pool.wait_ge(rope_expd, 2 * i + u + 1)
                    nc.gpsimd.tensor_tensor(T2[:, u, :].rearrange("p (h n) -> p h n", n=HALF),
                                            T2[:, u, :].rearrange("p (h n) -> p h n", n=HALF),
                                            over(KEEP[:, 2 * i + u, :], HEADS), ALU.mult).then_inc(rope_masked, 1)

            with pool.Fori(0, N2 - 1) as i:
                rope(i)
            rope(N2 - 1, True)

            pool.wait_ge(ln_variance, LN_F + 1)
            nc.gpsimd.tensor_tensor(rstd8, var8, CT[:, C_MHALF:C_MHALF + PAIRS], ALU.pow).then_inc(ln_rstd, 1)

        @block.vector
        def _(dve):
            dve.wait_ge(load_tokens, 16)
            dve.wait_ge(load_consts, 16)
            dve.sem_inc(tail_acc, 1)
            nc.vector.tensor_copy(identb[:, :], ident).then_inc(attn_cleared, 1)
            nc.vector.memset(P[:, :, :, S:HALF], 0.0).then_inc(attn_cleared, 1)

            def tiles(ap, i):
                return [ap[:, 2 * i + u, :] for u in (0, 1)]

            def add_to_x(i, sig_in, sig_sum, sig_out, k, row):
                for u, xt in enumerate(tiles(X, i)):
                    dve.wait_ge(sig_in, 2 * i + u + 1)
                    nc.vector.tensor_tensor(xt, bank(u, k)[:, 0:D], xt, ALU.add).then_inc(sig_sum, 1)
                for u, xt in enumerate(tiles(X, i)):
                    dve.wait_ge(sig_sum, 2 * i + u + 1)
                    nc.vector.tensor_tensor(xt, xt, RW[:, row:row + D], ALU.add).then_inc(sig_out, 1)

            def self_attention(i, ahead=True, last=False):
                for u in (0, 1):
                    dve.wait_ge(attn_scores, 2 * i + u + 1)
                    sc = bank(u, 2, 2).rearrange("p (o j n) -> p o j n", o=2, n=HALF)[:, :, :, 0:S]
                    best = sm[:, u, 0:HEADS].rearrange("p (o j) -> p o j", o=2)
                    nc.vector.tensor_reduce(best, sc, AX.X, ALU.max).then_inc(attn_top, 1)
                    dve.wait_ge(attn_top, 2 * i + u + 1)
                    nc.vector.tensor_tensor(P[:, u].rearrange("p (j o) n -> p o j n", o=2)[:, :, :, 0:S],
                                            sc, wide(best, S), ALU.subtract).then_inc(attn_shifted, 1)
                for u in (0, 1):
                    step = Steps(dve, attn_steps, 6 * i + 3 * u)
                    dve.wait_ge(attn_expd, 2 * i + u + 1)
                    step(nc.vector.tensor_reduce(sm[:, u, 16:32], P[:, u, :, 0:S], AX.X, ALU.add))
                    step(nc.vector.tensor_scalar(sm[:, u, 32:48], sm[:, u, 16:32], SAFE_EPS, None, ALU.add))
                    step(nc.vector.reciprocal(sm[:, u, 48:64], sm[:, u, 32:48]))
                    nc.vector.tensor_tensor(P[:, u, :, 0:S], P[:, u, :, 0:S], wide(sm[:, u, 48:64], S), ALU.mult)\
                        .then_inc(attn_probs, 1)
                add_to_x(i, attn_proj, attn_sum, attn_x1, 2, R_BO)
                dve.wait_ge(attn_x1, 2 * i + 2)
                ln_vector(dve, 2 * i + (1 if last else 2), tiles(X, i), XS, attn_normed2)
                if ahead:
                    ln_vector(dve, 2 * i + 3, tiles(X, i + 2), XFS, attn_normed)
                for u in (0, 1):
                    dve.wait_ge(attn_stack, 2 * i + u + 1)
                    nc.vector.tensor_tensor(qf[0:STACK, u],
                                            bank(u, 2, 2)[0:STACK, :].rearrange("p (g n) -> p g n", n=TILE),
                                            wide(PC[0:STACK, P_BQ:P_BQ + XG], TILE), ALU.add).then_inc(attn_qf, 1)

            XFS = [XF[:, u, :] for u in (0, 1)]
            dve.sem_inc(attn_qf, 2)
            dve.sem_inc(mqa_normed2, 1)
            ln_vector(dve, 0, tiles(X, 0), XFS, attn_normed)
            dve.wait_ge(attn_xT, 2)
            dve.wait_ge(load_attn_w, 64)
            ln_vector(dve, 1, tiles(X, 1), XFS, attn_normed)
            with dve.Fori(0, N2 - 2) as i:
                self_attention(i)
            self_attention(N2 - 2, ahead=False)
            self_attention(N2 - 1, ahead=False, last=True)

            dve.wait_ge(cross_cleared, 3)

            def take_v(b, u, n):
                dve.wait_ge(cross_v_proj, THIRDS * b + n + 1)
                at = VX[u][0:KN, 4 * n:4 * n + 4, 0:XG * VW].rearrange("p k (h w) -> p k h w", w=XD + 1)
                for j in range(4):
                    ins = nc.vector.tensor_tensor(at[:, j, :, 0:XD],
                                                  ps[0:KN, 7, j * D:(j + 1) * D].rearrange("p (h w) -> p h w", w=XD),
                                                  RW[0:KN, R_BV:R_BV + D].rearrange("p (h w) -> p h w", w=XD), ALU.add)
                ins.then_inc(cross_v, 1)

            def maximum(b, q):
                dve.wait_ge(cross_smax, THIRDS * XG * b + q + 1)
                nc.vector.tensor_reduce(MX[0:XQ, q % XG, q // XG:q // XG + 1], ps[0:XQ, 5 + q % 2, 0:KC], AX.X, ALU.max)\
                    .then_inc(cross_top, 1)

            def shift(b):
                dve.wait_ge(cross_top, THIRDS * XG * (b + 1))
                nc.vector.tensor_reduce(CM[0:XQ, :], MX[0:XQ], AX.X, ALU.max).then_inc(cross_best, 1)
                dve.wait_ge(cross_best, b + 1)
                nc.vector.tensor_scalar(CB[0:XQ, :], CM[0:XQ, :], -1.0, None, ALU.mult).then_inc(cross_negated, 1)

            def cross(b, u):
                q = 0
                for kt in range(KT):
                    for k in range(FIRST[kt]):
                        maximum(b + 1, q)
                        q += 1
                        if k == 0 and kt % 4 == 1:
                            take_v(b + 1, 1 - u, kt // 4)
                    if kt == KT - 3:
                        shift(b + 1)

            split_k(dve, nc.vector, 0, 0)
            q_residual(dve, nc.vector, N2 - 1, q1, attn_q1, attn_r1)
            split_k(dve, nc.vector, 0, 1)
            q_residual(dve, nc.vector, N2 - 1, q2, attn_q2, attn_r2)
            split_k(dve, nc.vector, 0, 2)
            for n in range(THIRDS):
                take_v(0, 0, n)
                for q in range(n * XG, (n + 1) * XG):
                    maximum(0, q)
            shift(0)
            with dve.Fori(0, PAIRS - 1) as p:
                cross(2 * p, 0)
                cross(2 * p + 1, 1)
            cross(B - 2, 0)

            def add_experts(i, e):
                dve.wait_ge(tail_y, 2 * E * i + 1 + 2 * (e + 2))
                for y in (e, e + 1):
                    for u, xt in enumerate(tiles(X, i)):
                        if y > 0:
                            dve.wait_ge(tail_acc, 2 * E * i + 1 + 2 * (y - 1) + u + 1)
                        nc.vector.scalar_tensor_tensor(xt, ps[:, 3 + y // 2 % 2, (2 * (y % 2) + u) * D:(2 * (y % 2) + u + 1) * D],
                                                       coef[:, u, y:y + 1], xt, ALU.mult, ALU.add).then_inc(tail_acc, 1)

            def add_bias(i):
                for u, xt in enumerate(tiles(X, i)):
                    dve.wait_ge(tail_b2, i + 1)
                    nc.vector.tensor_tensor(xt, ps[:, 7, u * D:(u + 1) * D], xt, ALU.add).then_inc(tail_x2b, 1)
                dve.wait_ge(tail_x2b, 2 * i + 2)

            tie = over(CT[:, C_TIE:C_TIE + E], 2)

            def pick(step, g_, top, won, hot, tie):
                step(nc.vector.tensor_reduce(top, g_, AX.X, ALU.max))
                step(nc.vector.tensor_tensor(hot, g_, wide(top, E), ALU.is_equal))
                step(nc.vector.tensor_tensor(hot, hot, tie, ALU.mult))
                step(nc.vector.tensor_reduce(won, hot, AX.X, ALU.max))
                step(nc.vector.tensor_tensor(hot, hot, wide(won, E), ALU.is_equal))

            def gates(i, step, into):
                dve.wait_ge(tail_logits, i + 1)
                step(nc.vector.tensor_tensor(sm[:, :, 0:8], ps[:, 7, 2 * TILE:2 * TILE + 2 * E].rearrange("p (u e) -> p u e", u=2),
                                             over(RW[:, R_BG:R_BG + E], 2), ALU.add))
                step(nc.vector.tensor_reduce(sm[:, :, 16], sm[:, :, 0:8], AX.X, ALU.max))
                nc.vector.tensor_tensor(sm[:, :, 0:8], sm[:, :, 0:8], wide(sm[:, :, 16], E), ALU.subtract)\
                    .then_inc(tail_shifted, 1)
                dve.wait_ge(tail_expd, i + 1)
                step(nc.vector.tensor_reduce(sm[:, :, 17], sm[:, :, 8:16], AX.X, ALU.add))
                step(nc.vector.reciprocal(sm[:, :, 18], sm[:, :, 17]))
                step(nc.vector.tensor_tensor(into, sm[:, :, 8:16], wide(sm[:, :, 18], E), ALU.mult))

            KXS = [KX[:, u, :] for u in (0, 1)]

            def mqa_norms(i, nth):
                ln_vector(dve, nth, tiles(X, i), KXS, mqa_normed)
                dve.wait_ge(mqa_normed, 2 * i + 1)
                ln_vector(dve, nth + 1, KXS, KXS, mqa_normed)
                dve.wait_ge(mqa_normed, 2 * i + 2)
                nc.vector.tensor_tensor(KX, KX, over(RW[:, R_NG:R_NG + D], 2), ALU.mult).then_inc(mqa_scaled, 1)

            def heads(i):
                for u in (0, 1):
                    dve.wait_ge(tail_turned, 2 * i + u + 1)
                    step = Steps(dve, tail_steps, 18 * i + 4 * u)
                    got = ps[:, 5 + u, :].rearrange("p (j h g w) -> p j h g w", j=2, h=2, w=32)
                    for j in (0, 1):
                        for h in (0, 1):
                            step(nc.vector.reciprocal(sm[:, u, 24 + 4 * (2 * j + h):28 + 4 * (2 * j + h)],
                                                      got[:, j, h, :, h * (XD + 1) + XD]))
                    for j in (0, 1):
                        for h in (0, 1):
                            at = sm[:, u, 24 + 4 * (2 * j + h):28 + 4 * (2 * j + h)]
                            ins = nc.vector.tensor_tensor(
                                CN[:, u].rearrange("p (j g h w) -> p j g h w", j=2, h=2, w=XD)[:, j, :, h, :],
                                got[:, j, h, :, h * (XD + 1):h * (XD + 1) + XD], wide(at, XD), ALU.mult)
                    ins.then_inc(tail_ctx, 1)

            def heads_added(i):
                dve.wait_ge(tail_proj, i + 1)
                for u, xt in enumerate(tiles(X, i)):
                    nc.vector.tensor_tensor(xt, ps[:, 6, u * D:(u + 1) * D], xt, ALU.add).then_inc(tail_sum, 1)
                for u, xt in enumerate(tiles(X, i)):
                    dve.wait_ge(tail_sum, 2 * i + u + 1)
                    nc.vector.tensor_tensor(xt, xt, RW[:, R_BO2:R_BO2 + D], ALU.add).then_inc(tail_x2, 1)
                dve.wait_ge(tail_x2, 2 * i + 2)
                ln_vector(dve, LN_T + i, tiles(X, i), XS, tail_normed)

            def route(i):
                step = Steps(dve, tail_steps, 18 * i + 8)
                gates(i, step, sm[:, :, 24:32])
                pick(step, sm[:, :, 24:32], sm[:, :, 19], sm[:, :, 20], sm[:, :, 32:40], tie)
                dve.wait_ge(tail_acc, 2 * E * i + 1)
                nc.vector.tensor_tensor(coef[:, :, :], sm[:, :, 24:32], sm[:, :, 32:40], ALU.mult).then_inc(tail_coef, 1)
                dve.wait_ge(tail_coef, i + 1)
                assert step.n == 10, step.n

            def experts(i, more=True):
                if more:
                    heads(i + 1)
                add_bias(i)
                add_experts(i, 0)
                add_experts(i, 2)
                if more:
                    heads_added(i + 1)
                else:
                    nc.vector.memset(VM, 1.0).then_inc(rope_keep, 1)
                    mqa_norms(0, LN_M)
                add_experts(i, 4)
                add_experts(i, 6)
                if more:
                    route(i + 1)

            heads(0)
            heads_added(0)
            route(0)
            with dve.Fori(0, N2 - 1) as i:
                experts(i)
            experts(N2 - 1, False)

            def rope_norms(i, step):
                nth = LN_R + 3 * i if not isinstance(i, int) or i else LN_R - 1
                ln_vector(dve, nth, tiles(X, i), XS, rope_normed)
                dve.wait_ge(rope_normed, 3 * i + 1)
                ln_vector(dve, nth + 1, XS, XS, rope_normed)
                ln_vector(dve, nth + 2, tiles(C56, i), [KX[:, u, :] for u in (0, 1)], rope_normed)
                dve.wait_ge(rope_normed, 3 * i + 3)
                for y in (XN[:, :, :], KX):
                    ins = nc.vector.tensor_tensor(y, y, over(RW[:, R_LG:R_LG + D], 2), ALU.mult)
                step(ins)
                nc.vector.tensor_tensor(XN[:, :, :], XN[:, :, :], over(RW[:, R_LB:R_LB + D], 2), ALU.add)
                nc.vector.tensor_tensor(KX, KX, over(RW[:, R_LB:R_LB + D], 2), ALU.add).then_inc(rope_scaled, 1)

            def sums_of_squares(i):
                for u in (0, 1):
                    dve.wait_ge(mqa_sq, 2 * i + u + 1)
                    nc.vector.tensor_reduce(sm[:, u, 0:9], T3[:, u, 0:576].rearrange("p (h w) -> p h w", w=DH),
                                            AX.X, ALU.add).then_inc(mqa_ss, 1)

            def lengths_taken(i):
                for u in (0, 1):
                    step = Steps(dve, mqa_steps, 6 * i + 2 * u)
                    dve.wait_ge(mqa_root, 2 * i + u + 1)
                    step(nc.vector.tensor_scalar(sm[:, u, 32:41], sm[:, u, 16:25], NORM_EPS, None, ALU.max))
                    step(nc.vector.reciprocal(sm[:, u, 48:57], sm[:, u, 32:41]))
                    dve.wait_ge(mqa_v, 2 * i + u + 1)
                    nc.vector.scalar_tensor_tensor(T1[:, u, 0:512].rearrange("p (h w) -> p h w", w=DH),
                                                   bank(u, 0).rearrange("p (h w) -> p h w", w=DH), 64.0,
                                                   wide(sm[:, u, 48:56], DH), ALU.mult, ALU.mult)
                    nc.vector.scalar_tensor_tensor(T1[:, u, 512:640].rearrange("p (h w) -> p h w", w=DH),
                                                   over(bank(u, 1)[:, 0:DH], 2), 4.0,
                                                   wide(sm[:, u, 56:57].broadcast_to([128, 2]), DH), ALU.mult, ALU.mult)\
                        .then_inc(mqa_qn, 1)

            def mqa(i, last=False):
                for u in (0, 1):
                    dve.wait_ge(mqa_turned, 2 * i + u + 1)
                    nc.vector.tensor_copy(T2[:, u, 512:640], bank(u, 3)[:, 0:128]).then_inc(mqa_kT, 1)
                if not last:
                    mqa_norms(i + 1, LN_M + 3 * i + 2)
                else:
                    keep = Steps(dve, rope_keep, 1)
                    keep(nc.vector.tensor_copy(MK, mask8[:, :]))
                    keep(nc.vector.tensor_scalar(MK, MK, -1.0, 1.0, ALU.mult, ALU.add))
                    for k in range(PAIRS):
                        ins = nc.vector.tensor_scalar(KEEP[:, k, :], CT[:, C_CAUSAL:C_CAUSAL + HALF], MK[:, k:k + 1], None, ALU.mult)
                    keep(ins)
                    dve.wait_ge(load_context, 16)
                    rope_norms(0, Steps(dve, rope_steps, 0))
                for u in (0, 1):
                    dve.wait_ge(mqa_pv, 2 * i + u + 1)
                    got = heads4(u, 1, 2)
                    den = sm[:, u, 0:8].rearrange("p (a h) -> p a h", a=2)
                    step2 = Steps(dve, mqa_steps, 6 * i + 4 + u)
                    step2(nc.vector.reciprocal(den, got[:, :, :, DH]))
                    nc.vector.tensor_tensor(T1[:, u, 0:512].rearrange("p (a h w) -> p a h w", a=2, w=DH),
                                            got[:, :, :, 0:DH], wide(den, DH), ALU.mult).then_inc(mqa_o, 1)
                if not last:
                    sums_of_squares(i + 1)
                    dve.wait_ge(mqa_oT, 2 * i + 2)
                    apart(dve)
                    lengths_taken(i + 1)
                dve.wait_ge(mqa_proj, 2 * i + 2)
                ln_vector(dve, LN_M + 3 * i + (5 if last else 4), [bank(u, 2)[:, 0:D] for u in (0, 1)],
                          [T4[:, u, 0:D] for u in (0, 1)], mqa_normed2)
                dve.wait_ge(mqa_normed2, i + 2)
                nc.vector.tensor_tensor(T4[:, :, 0:D], T4[:, :, 0:D], over(RW[:, R_ONG:R_ONG + D], 2), ALU.mult).then_inc(mqa_outn, 1)
                dve.wait_ge(mqa_outn, i + 1)
                for u, xt in enumerate(tiles(X, i)):
                    ins = nc.vector.tensor_tensor(xt, xt, T4[:, u, 0:D], ALU.add)
                ins.then_inc(mqa_sum, 1)

            sums_of_squares(0)
            lengths_taken(0)
            with dve.Fori(0, N2 - 1) as i:
                mqa(i)
            mqa(N2 - 1, True)

            def turn(u, into, k, table):
                return nc.vector.tensor_tensor(into[:, u, :].rearrange("p (j n) -> p j n", n=TILE),
                                               bank(u, k, 2).rearrange("p (j n) -> p j n", n=TILE),
                                               over(CT[:, table:table + TILE], 8), ALU.mult)

            def rope_q(i):
                for u in (0, 1):
                    dve.wait_ge(rope_qproj, 4 * i + u + 1)
                    turn(u, T1, 0, C_COS).then_inc(rope_parts, 1)

            def rope(i, last=False):
                step = Steps(dve, rope_steps, 5 * i + 1)
                for u in (0, 1):
                    dve.wait_ge(rope_qproj, 4 * i + 2 + u + 1)
                    turn(u, T2, 2, C_SIN).then_inc(rope_parts, 1)
                for u in (0, 1):
                    dve.wait_ge(rope_kproj, 2 * i + u + 1)
                    turn(u, T3, 0, C_COS)
                    turn(u, T4, 2, C_SIN).then_inc(rope_parts, 1)
                if not last:
                    rope_norms(i + 1, step)
                    rope_q(i + 1)
                for u in (0, 1):
                    dve.wait_ge(rope_pv, 2 * i + u + 1)
                    got = heads4(u, 0, 4)
                    den = sm[:, u, 0:16].rearrange("p (a h) -> p a h", a=4)
                    step(nc.vector.reciprocal(den, got[:, :, :, DH]))
                    nc.vector.tensor_tensor(T4[:, u, :].rearrange("p (a h w) -> p a h w", a=4, w=DH),
                                            got[:, :, :, 0:DH], wide(den, DH), ALU.mult).then_inc(rope_o, 1)
                for u, xt in enumerate(tiles(X, i)):
                    dve.wait_ge(rope_out, 2 * i + u + 1)
                    step(nc.vector.tensor_tensor(xt, bank(u, 2)[:, 0:D], xt, ALU.add))
                assert last or step.n == 5

            rope_q(0)
            with dve.Fori(0, N2 - 1) as i:
                rope(i)
            rope(N2 - 1, True)

            dve.wait_ge(rope_steps, 5 * N2)
            step = Steps(dve, moe_steps, 0)
            for t in range(PAIRS):
                ins = nc.vector.bn_stats(st8[:, t, :], X[:, t, :])
            step(ins)
            for t in range(PAIRS):
                ins = nc.vector.bn_aggr(mv8[:, t, :], st8[:, t, :])
            step(ins)
            nc.vector.tensor_scalar(var8, mv8[:, :, 1], LN_EPS, None, ALU.add).then_inc(ln_variance, 1)
            dve.wait_ge(ln_rstd, LN_F + 1)
            for t in range(PAIRS):
                ins = nc.vector.tensor_scalar(XA[:, t, :], X[:, t, :], mv8[:, t, 0:1], rstd8[:, t:t + 1],
                                              ALU.subtract, ALU.mult)
                if t % 4 == 3:
                    ins.then_inc(moe_normed, 1)
            dve.wait_ge(moe_logits, 1)
            logits = ps[:, 1, 0:PAIRS * E].rearrange("p (t e) -> p t e", e=E)
            top, total, won = TOP[:, 0, :], TOP[:, 1, :], TOP[:, 2, :]
            step(nc.vector.tensor_tensor(LG, logits, over(RW[:, R_RB:R_RB + E], PAIRS), ALU.add))
            step(nc.vector.tensor_reduce(top, LG, AX.X, ALU.max))
            nc.vector.tensor_tensor(LG, LG, wide(top, E), ALU.subtract).then_inc(tail_shifted, 1)
            dve.wait_ge(tail_expd, N2 + 1)
            step(nc.vector.tensor_reduce(total, EX, AX.X, ALU.add))
            step(nc.vector.reciprocal(total, total))
            step(nc.vector.tensor_tensor(GATE, EX, wide(total, E), ALU.mult))
            tie8 = over(CT[:, C_TIE:C_TIE + E], PAIRS)
            pick(step, GATE, top, won, HOT, tie8)
            step(nc.vector.scalar_tensor_tensor(LEFT, HOT, -4.0, GATE, ALU.mult, ALU.add))
            pick(step, LEFT, top, won, HOT2, tie8)
            nc.vector.tensor_tensor(PICK, HOT2, HOT, ALU.add).then_inc(moe_picked, 1)
            dve.wait_ge(moe_count, 1)
            flat = lambda ap: ap.rearrange("p a b -> p (a b)")
            step(nc.vector.tensor_scalar(flat(WGT), ps[:, 2, 0:PAIRS * E], float(CAPACITY), None, ALU.is_le))
            step(nc.vector.tensor_tensor(flat(WGT), flat(WGT), CT[:, C_ONES:C_ONES + PAIRS * E], ALU.mult))
            step(nc.vector.tensor_tensor(flat(WGT), flat(WGT), flat(PICK), ALU.mult))
            step(nc.vector.tensor_tensor(flat(SLOT), ps[:, 2, 0:PAIRS * E], flat(WGT), ALU.mult))
            step(nc.vector.tensor_tensor(flat(WGT), flat(WGT), flat(GATE), ALU.mult))


            def one_hot(u, t):
                return nc.vector.tensor_tensor(ONEHOT[:, u].rearrange("p (e n) -> p e n", n=SLOTS),
                                               over(CT[:, C_PLACE:C_PLACE + SLOTS], E), wide(SLOT[:, t, :], SLOTS), ALU.is_equal)

            for t in range(PAIRS):
                if t >= 2:
                    dve.wait_ge(last_read, t - 1)
                one_hot(t % 2, t).then_inc(last_onehot, 1)

            def weighed(i):
                for u in (0, 1):
                    dve.wait_ge(last_read, PAIRS + 2 * i + u - 1)
                    one_hot(u, 2 * i + u).then_inc(last_onehot, 1)
                    dve.wait_ge(last_onehot, PAIRS + 4 * i + 2 * u + 1)
                    both = ONEHOT[:, u].rearrange("p (e n) -> p e n", n=SLOTS)
                    nc.vector.tensor_tensor(both, both, wide(WGT[:, 2 * i + u, :], SLOTS), ALU.mult).then_inc(last_onehot, 1)

            def add_returned(i):
                for u, xt in enumerate(tiles(X, i)):
                    dve.wait_ge(last_y, E + 2 * i + u + 1)
                    nc.vector.tensor_tensor(xt, bank(u, 3)[:, 0:D], xt, ALU.add).then_inc(last_acc, 1)

            weighed(0)
            dve.wait_ge(load_late_w, 112)
            for e in range(E):
                dve.wait_ge(last_y, e + 1)
                for j, (chunk, row, n, first) in enumerate(pieces(e)):
                    ins = nc.vector.tensor_tensor(OUTS[row:row + n, chunk, :], ps[row:row + n, e % 3, j * D:(j + 1) * D],
                                                  LB2[row:row + n, e, :], ALU.add)
                ins.then_inc(last_acc, 1)
            with dve.Fori(0, N2 - 1) as i:
                weighed(i + 1)
                add_returned(i)
            add_returned(N2 - 1)


def tables():
    import numpy as np

    t = np.zeros((128, C_END), np.float32)
    t[:, C_IDENT:C_IDENT + 128] = np.eye(128)
    p = np.arange(128)
    inv = (np.float32(1.0) / np.float32(10000.0) ** (np.arange(0, DH, 2, dtype=np.float32) / np.float32(DH)))
    angle = (np.arange(HALF, dtype=np.float32)[None, :] * np.repeat(inv, 2)[:, None]).astype(np.float32)
    sign = np.where(np.arange(DH) % 2, 1.0, -1.0)[:, None]
    t[:, C_COS:C_COS + 128] = np.tile(np.cos(angle), (2, 2))
    t[:, C_SIN:C_SIN + 128] = np.tile(np.sin(angle) * sign, (2, 2))
    token, batch = p % HALF, p // HALF
    t[:, C_CAUSAL:C_CAUSAL + HALF] = (token[:, None] <= np.arange(HALF)[None, :]) & (token[:, None] < S)
    order = batch * HALF + token
    t[:, C_TRI:C_TRI + 128] = (order[:, None] <= order[None, :]) & (token[:, None] < S)
    t[:, C_ONES:C_ONES + 128] = (token[:, None] < S)
    t[:, C_TIE:C_TIE + E] = E - np.arange(E)
    row = np.arange(STACK)
    for h in (0, 1):
        t[:STACK, C_BLK + h] = (row // XD % 2) == h
    part = np.array(Q_PART)[row // (2 * XD)]
    t[:STACK, C_MASK1] = -(part >= 1).astype(np.float32)
    t[:STACK, C_MASK2] = -(part >= 2).astype(np.float32)
    t[:, C_MHALF:C_MHALF + PAIRS] = -0.5
    t[:, C_HALF:C_HALF + 18] = 0.5
    t[:, C_PLACE:C_PLACE + SLOTS] = 1 + np.arange(SLOTS)
    return t


def kernel(**inputs):
    import numpy as np
    import concourse.bacc as bacc
    from concourse import mybir as mb
    from concourse.bass_utils import run_bass_kernel_spmd as run

    v = {k: np.asarray(a) for k, a in inputs.items()}

    def halves(z):
        w = np.zeros((B, HALF) + z.shape[2:], z.dtype)
        w[:, :S] = z
        w = w.reshape((PAIRS, TILE) + z.shape[2:])
        return np.ascontiguousarray(np.moveaxis(w, 0, 1))

    def by_row(z):
        return np.broadcast_to(z, (128,) + z.shape)

    def by_parity(w):
        return w.reshape(D, 8, 2, DH).transpose(0, 2, 1, 3).reshape(D, INNER)

    def stacked(w):
        w = w.reshape(w.shape[:-1] + (XG, 1, 2 * XD))
        w = np.repeat(w, len(K_PART), axis=-2)
        return w.reshape(w.shape[:-2] + (STACK,))

    def swapped(w):
        return w.reshape(D, INNER // 2, 2)[:, :, ::-1].reshape(D, INNER)

    def width_first(w):
        return np.swapaxes(w.reshape(w.shape[:-1] + (XG, 2 * XD)), -1, -2).reshape(w.shape)

    rows = np.concatenate([by_row(v[n]) for n in (
        "L0_attn_bo", "L0_xattn_b_v", "L0_xattn_b_o", "L0_ffn_bg", "L1_attn_norm_g", "L1_attn_out_norm_g",
        "L1_xattn_ln_g", "L1_xattn_ln_b", "L1_ffn_router_b")], axis=1)
    bq = np.zeros((128, XG), np.float32)
    bq[:STACK] = stacked(v["L0_xattn_b_q"]).T
    cols = np.concatenate([width_first(v["L0_xattn_b_k"])[:, None], bq,
                           v["L0_ffn_b1"].reshape(-1, 128).T, v["L1_ffn_b1"].reshape(-1, 128).T], axis=1)
    data = {
        "x": halves(v["x"]),
        "ctx_t": v["ctx_1024"].transpose(0, 2, 1),
        "ctx_first": halves(v["ctx_1024"][:, :S]),
        "mask": halves(v["mask_BxS2_bf0"][:, :S]),
        "consts": tables(), "rows": rows, "cols": cols,
        "a_wq": v["L0_attn_Wq"].T, "a_wk": v["L0_attn_Wk"].T, "a_wv": by_parity(v["L0_attn_Wv"].T),
        "a_wo": v["L0_attn_Wo"].T,
        "x_wq": stacked(v["L0_xattn_W_q"].T).reshape(D, XG * STACK),
        "x_wk": width_first(v["L0_xattn_W_k"].T), "x_wv": v["L0_xattn_W_v"].T, "x_wo": v["L0_xattn_W_o"].T,
        "g_w": v["L0_ffn_Wg"], "f_w1": v["L0_ffn_W1"], "f_w2": v["L0_ffn_W2"], "f_b2": v["L0_ffn_b2"],
        "m_wq": v["L1_attn_Wq"], "m_wkv": v["L1_attn_Wkv"], "m_wo": v["L1_attn_Wout"],
        "r_wq": v["L1_xattn_Wq"], "r_wqr": swapped(v["L1_xattn_Wq"]),
        "r_wk": v["L1_xattn_Wk"], "r_wkr": swapped(v["L1_xattn_Wk"]),
        "r_wv": v["L1_xattn_Wv"], "r_wo": v["L1_xattn_Wo"],
        "l_w": v["L1_ffn_router_w"], "l_w1": v["L1_ffn_w1"], "l_w2": v["L1_ffn_w2"], "l_b2": by_row(v["L1_ffn_b2"].reshape(-1)),
    }
    nc = bacc.Bacc("TRN2", target_bir_lowering=False, num_devices=1)
    arrays, args = {}, []
    for name, z in data.items():
        z = np.ascontiguousarray(z)
        arrays[f"in_{name}"] = z
        args.append(nc.dram_tensor(f"in_{name}", z.shape, mb.dt.from_np(z.dtype), kind="ExternalInput").ap())
    args.append(nc.dram_tensor("out", (B, S, D), mb.dt.float32, kind="ExternalOutput").ap())
    decoder_kernel(nc, *args)
    return run(nc, [arrays], core_ids=[0]).results[0]["out"]
```
